# Optimizing a Trainium2 kernel written in Bass

```python
import numpy as np
import jax
import jax.numpy as jnp

def _softmax(x, axis=-1):
    return jax.nn.softmax(x, axis=axis)

def _gelu(x):
    return jax.nn.gelu(x, approximate=True)

def _silu(x):
    return jax.nn.silu(x)

def _sigmoid(x):
    return jax.nn.sigmoid(x)

def _layernorm(x, axis=-1, eps=1e-05):
    m = jnp.mean(x, axis=axis, keepdims=True)
    v = jnp.var(x, axis=axis, keepdims=True)
    return (x - m) / jnp.sqrt(v + eps)

def _scatter_add(tgt, idx, src, axis=0):
    return tgt.at[idx].add(src)

def _segment_sum(src, seg, n):
    return jax.ops.segment_sum(src, seg, n)
kernel_name = 'mk_gps_d1_gnn_r8_35c801'

def setup_inputs(seed: int=0):
    np.random.seed(seed)
    _w = jnp.asarray

    def _rec_inputs():
        import jax
        import jax.numpy as jnp
        _gk = jax.random.key(seed)
        x = -0.0006008 + 1.001 * jax.random.normal(jax.random.fold_in(_gk, 1), (6250, 256), jnp.float32)
        src = jax.random.randint(jax.random.fold_in(_gk, 2), (200000,), 0, 6250, jnp.int32)
        dst = jnp.minimum((6250 * jax.random.uniform(jax.random.fold_in(_gk, 3), (200000,)) ** 2.0).astype(jnp.int32), 49999)
        _o = jnp.argsort(dst, stable=True)
        src = src[_o]
        dst = dst[_o]
        edge_type_20 = jax.random.randint(jax.random.fold_in(_gk, 12), (200000,), 0, 20, jnp.int32)
        edge_weight1 = jax.random.uniform(jax.random.fold_in(_gk, 13), (200000, 1), jnp.float32, 0.0, 0.999998)
        return (x, src, dst, edge_type_20, edge_weight1)
    x, src, dst, edge_type_20, edge_weight1 = _rec_inputs()

    def _L0_gnn_setup():
        import jax, jax.numpy as jnp
        import numpy as np
        N_NODES = 1250
        N_EDGES = 40000
        NUM_RELS = 20
        IN_FEAT = 256
        OUT_FEAT = 256
        key = jax.random.key(seed)
        k1, k2, k3, k4, k5, k6 = jax.random.split(key, 6)
        h = jax.random.normal(k1, (N_NODES, IN_FEAT), dtype=jnp.float32)
        gain = float(np.sqrt(2.0))
        limit = gain * float(np.sqrt(6.0 / (IN_FEAT + OUT_FEAT)))
        weight = jax.random.uniform(k2, (NUM_RELS, IN_FEAT, OUT_FEAT), dtype=jnp.float32, minval=-limit, maxval=limit)
        norm = jax.random.uniform(k3, (N_EDGES, 1), dtype=jnp.float32)
        edge_src = jax.random.randint(k4, (N_EDGES,), 0, N_NODES, dtype=jnp.int32)
        edge_dst = jax.random.randint(k5, (N_EDGES,), 0, N_NODES, dtype=jnp.int32)
        rel_type = jax.random.randint(k6, (N_EDGES,), 0, NUM_RELS, dtype=jnp.int32)
        return {'h': h, 'weight': weight, 'norm': norm, 'edge_src': edge_src, 'edge_dst': edge_dst, 'rel_type': rel_type}
    _L0_gnn_all = _L0_gnn_setup()
    _L0_gnn_in = {k: v for k, v in _L0_gnn_all.items() if k in ('weight',)}
    del _L0_gnn_all

    def _L0_mix_setup():
        import jax, jax.numpy as jnp
        import numpy as np
        A, Bc, Cc = (0.5, 1.0, 1.0)
        H = 8
        EPS = 1e-12

        def _normalize(t):
            n = jnp.linalg.norm(t, axis=-1, keepdims=True)
            return t / jnp.maximum(n, EPS)
        key = jax.random.key(seed)
        ks = jax.random.split(key, 5)
        B, N, C = (8, 256, 256)
        D = C // H
        x = jax.random.normal(ks[0], (B, N, C), dtype=jnp.float32)
        Wqkv = jax.random.normal(ks[1], (3 * H * D, C), dtype=jnp.float32) * 0.02
        bqkv = jnp.zeros((3 * H * D,), dtype=jnp.float32)
        Wproj = jax.random.normal(ks[2], (C, H * D), dtype=jnp.float32) * 0.02
        bproj = jnp.zeros((C,), dtype=jnp.float32)
        temperature = jnp.ones((1, H, 1, 1), dtype=jnp.float32)
        return {'x': x, 'Wqkv': Wqkv, 'bqkv': bqkv, 'Wproj': Wproj, 'bproj': bproj, 'temperature': temperature}
    _L0_mix_all = _L0_mix_setup()
    _L0_mix_in = {k: v for k, v in _L0_mix_all.items() if k in ('Wqkv', 'bqkv', 'Wproj', 'bproj', 'temperature')}
    del _L0_mix_all

    def _L0_ffn_setup():
        import jax, jax.numpy as jnp
        import numpy as np
        C = 256
        HID = 1024
        E = 8
        TEMP = 1.0
        key = jax.random.key(seed)
        ks = jax.random.split(key, 7)
        x = jax.random.normal(ks[0], (8, 2048, C), dtype=jnp.float32)
        W1 = jax.random.normal(ks[1], (C, HID), dtype=jnp.float32) * 0.02
        b1 = jnp.zeros((HID,), dtype=jnp.float32)
        Wg = jax.random.normal(ks[2], (HID, E), dtype=jnp.float32) * 0.02
        bg = jnp.zeros((E,), dtype=jnp.float32)
        Wd = jax.random.normal(ks[3], (E, HID, C), dtype=jnp.float32) * 0.02
        bd = jnp.zeros((E, C), dtype=jnp.float32)
        return {'x': x, 'W1': W1, 'b1': b1, 'Wg': Wg, 'bg': bg, 'Wd': Wd, 'bd': bd}
    _L0_ffn_all = _L0_ffn_setup()
    _L0_ffn_in = {k: v for k, v in _L0_ffn_all.items() if k in ('W1', 'b1', 'Wg', 'bg', 'Wd', 'bd')}
    del _L0_ffn_all
    return {'x': x, 'src': src, 'dst': dst, 'edge_type_20': edge_type_20, 'edge_weight1': edge_weight1, 'L0_gnn_weight': _L0_gnn_in['weight'], 'L0_mix_Wqkv': _L0_mix_in['Wqkv'], 'L0_mix_bqkv': _L0_mix_in['bqkv'], 'L0_mix_Wproj': _L0_mix_in['Wproj'], 'L0_mix_bproj': _L0_mix_in['bproj'], 'L0_mix_temperature': _L0_mix_in['temperature'], 'L0_ffn_W1': _L0_ffn_in['W1'], 'L0_ffn_b1': _L0_ffn_in['b1'], 'L0_ffn_Wg': _L0_ffn_in['Wg'], 'L0_ffn_bg': _L0_ffn_in['bg'], 'L0_ffn_Wd': _L0_ffn_in['Wd'], 'L0_ffn_bd': _L0_ffn_in['bd']}

def reference(x, src, dst, edge_type_20, edge_weight1, L0_gnn_weight, L0_mix_Wqkv, L0_mix_bqkv, L0_mix_Wproj, L0_mix_bproj, L0_mix_temperature, L0_ffn_W1, L0_ffn_b1, L0_ffn_Wg, L0_ffn_bg, L0_ffn_Wd, L0_ffn_bd):
    import jax
    import jax.numpy as jnp

    def _L0_gnn_ref(h, weight, norm, edge_src, edge_dst, rel_type):
        import jax, jax.numpy as jnp
        import numpy as np
        N_NODES = 1250
        N_EDGES = 40000
        NUM_RELS = 20
        IN_FEAT = 256
        OUT_FEAT = 256
        h_all = jnp.einsum('ni,rio->nro', h, weight)
        msg = h_all[edge_src, rel_type] * norm
        agg = jax.ops.segment_sum(msg, edge_dst, num_segments=h.shape[0])
        return jax.nn.relu(agg)

    def _L0_mix_ref(x, Wqkv, bqkv, Wproj, bproj, temperature):
        import jax, jax.numpy as jnp
        import numpy as np
        A, Bc, Cc = (0.5, 1.0, 1.0)
        H = 8
        EPS = 1e-12

        def _normalize(t):
            n = jnp.linalg.norm(t, axis=-1, keepdims=True)
            return t / jnp.maximum(n, EPS)
        B, N, C = x.shape
        D = C // H
        scale = float(D) ** 0.25
        qkv = (x @ Wqkv.T + bqkv).reshape(B, N, 3, H, D)
        qkv = jnp.transpose(qkv, (2, 0, 3, 1, 4))
        q, k, v = (qkv[0], qkv[1], qkv[2])
        q = q * scale
        v1 = jnp.concatenate([jnp.ones((B, H, N, 1), dtype=v.dtype), v], axis=-1)
        qn = _normalize(q) * (scale * temperature)
        kn = _normalize(k) * scale
        vN = v1 / N
        kv_mod = jnp.einsum('bhni,bhnj,bhne->bhije', kn, kn, vN)
        kv = jnp.einsum('bhnd,bhne->bhde', kn, vN)
        vsum = jnp.sum(vN, axis=-2)[:, :, None, :]
        y = A * jnp.einsum('bhni,bhnj,bhije->bhne', qn, qn, kv_mod) + scale ** 2 * Bc * jnp.einsum('bhnd,bhde->bhne', qn, kv) + scale ** 4 * Cc * vsum
        y_norm, y = (y[..., :1], y[..., 1:])
        y = y / y_norm
        out = jnp.transpose(y, (0, 2, 1, 3)).reshape(B, N, H * D)
        return out @ Wproj.T + bproj

    def _L0_ffn_ref(x, W1, b1, Wg, bg, Wd, bd):
        import jax, jax.numpy as jnp
        import numpy as np
        C = 256
        HID = 1024
        E = 8
        TEMP = 1.0
        orig_shape = x.shape
        xf = x.reshape(-1, orig_shape[-1])
        H = jax.nn.gelu(xf @ W1 + b1, approximate=False)
        probs = jax.nn.softmax((H @ Wg + bg) / TEMP, axis=-1)
        assign = jnp.argmax(probs, axis=-1)
        out = jnp.zeros_like(xf)
        for e in range(Wd.shape[0]):
            y = H @ Wd[e] + bd[e]
            sel = (assign == e)[:, None]
            out = out + jnp.where(sel, probs[:, e:e + 1] * y, 0.0)
        return out.reshape(orig_shape)
    xn = _layernorm(x, axis=-1)
    x = x + _L0_gnn_ref(xn, L0_gnn_weight, edge_weight1, src, dst, edge_type_20) + _L0_mix_ref(xn[None], L0_mix_Wqkv, L0_mix_bqkv, L0_mix_Wproj, L0_mix_bproj, L0_mix_temperature)[0]
    x = x + _L0_ffn_ref(_layernorm(x, axis=-1)[None], L0_ffn_W1, L0_ffn_b1, L0_ffn_Wg, L0_ffn_bg, L0_ffn_Wd, L0_ffn_bd)[0]
    return x

_drawn_inputs = setup_inputs


def setup_inputs(seed=0):
    import zlib

    import numpy as np

    out = dict(_drawn_inputs(seed))
    spreads = {'L0_mix_bqkv': (0.0, 0.8),
     'L0_mix_bproj': (0.0, 0.1),
     'L0_mix_temperature': (1.0, 0.6),
     'L0_ffn_b1': (0.0, 0.8),
     'L0_ffn_bg': (0.0, 0.8),
     'L0_ffn_bd': (0.0, 0.8)}
    factors = {'L0_mix_Wqkv': 8.0,
     'L0_mix_Wproj': 6.48,
     'L0_ffn_W1': 8.0,
     'L0_ffn_Wg': 8.0,
     'L0_ffn_Wd': 8.0}
    for name, (base, spread) in spreads.items():
        noise = np.random.default_rng([zlib.crc32(name.encode()), seed]).standard_normal(out[name].shape)
        drawn = base * np.exp(spread * noise) if base else spread * noise
        out[name] = jnp.asarray(drawn.astype(out[name].dtype))
    for name, factor in factors.items():
        out[name] = (out[name] * factor).astype(out[name].dtype)
    return out
```

```python
from contextlib import ExitStack

import numpy as np

import concourse.bass as bass
from concourse import mybir

ALU = mybir.AluOpType
ACT = mybir.ActivationFunctionType
F32 = mybir.dt.float32
I32 = mybir.dt.int32
AX_X = mybir.AxisListType.X

P = 128
N, C = 6250, 256
KC = C // P
TILES = (N + P - 1) // P
NPAD = TILES * P
LAST = N - (TILES - 1) * P
LN_EPS = 1e-5

E, RELS = 200000, 20
GE = 4
GROUP = GE * P
WIN = 64
GPT = 4
GROUPS = 2 * GPT * TILES
CHUNKS = (GROUPS + P - 1) // P
COLS = GROUPS * GE
FULL_G, REST_E = E // GROUP, E % GROUP
WINDOWS = (N + WIN - 1) // WIN
AGG = N + WIN
assert GROUPS * GROUP >= E and FULL_G // P == CHUNKS - 1

HEADS, D = 8, 32
DV = D + 1
SHIFTS = D // 2
PAIRS = HEADS * SHIFTS * D
PT = PAIRS // P
TPH = PT // HEADS
HG = P // D
NG = HEADS // HG
FT = PT + 2 * NG
DW = D + SHIFTS
SC = float(D) ** 0.25
ROOT_EPS = 1e-12

HID, EXP = 1024, 8
HC = HID // P


def after(eng, sem, value):
    if isinstance(value, int) and value <= 0:
        return
    eng.wait_ge(sem, value)


class Chain:

    def __init__(self, eng, sem, per=0):
        self.eng, self.sem, self.per, self.n, self.base = eng, sem, per, 0, 0

    def start(self, done):
        self.base, self.n = done * self.per, 0

    def end(self):
        assert self.n == self.per, (self.n, self.per)

    def mark(self, ins):
        self.n += 1
        ins.then_inc(self.sem, 1)
        return self.n

    def wait(self, n=None):
        self.eng.wait_ge(self.sem, self.base + (self.n if n is None else n))

    def __call__(self, ins):
        self.mark(ins)
        self.wait()


def loop(eng, body, first=1, last=TILES):
    body(first)
    with eng.Fori(first + 1, last) as i:
        body(i)
    body(last)


class Scope:

    def __init__(self, nc):
        self.nc, self.ctx = nc, ExitStack()

    def __enter__(self):
        self.ctx.__enter__()
        return self

    def __exit__(self, *a):
        return self.ctx.__exit__(*a)

    def sb(self, name, shape, dt=F32):
        return self.ctx.enter_context(self.nc.sbuf_tensor(name, shape, dt))

    def ps(self, name, shape):
        return self.ctx.enter_context(self.nc.psum_tensor(name, shape, F32))

    def sem(self, name):
        return self.ctx.enter_context(self.nc.semaphore(name))

    def sems(self, name, n):
        return [self.sem(f"{name}{i}") for i in range(n)]

    def block(self):
        return self.ctx.enter_context(self.nc.Block())


def edges(nc, keep, src, dst, rel, norm):
    with Scope(nc) as s:
        raw = {k: s.sb(f"e_{k}", [P, CHUNKS, GROUP], I32) for k in ("src", "rel", "dst")}
        top = s.sb("e_top", [P, GROUP], I32)
        nrm = s.sb("e_nrm", [P, CHUNKS, GROUP])
        idx = s.sb("e_idx", [P, CHUNKS, GROUP])
        dstf = s.sb("e_dstf", [P, CHUNKS, GROUP])
        topf = s.sb("e_topf", [P, GROUP])
        low = s.sb("e_low", [P, CHUNKS])
        high = s.sb("e_high", [P, CHUNKS])
        span = s.sb("e_span", [P, CHUNKS])
        wide = s.sb("e_wide", [P, 1])
        turned = s.ps("e_turned", [P, 2, GE, P])
        rows = s.ps("e_rows", [1, CHUNKS, P])
        count = s.ps("e_count", [1, 1])
        padded, loaded, ident_ready = s.sem("padded"), s.sem("loaded"), s.sem("ident_ready")
        ready, rows_ready, turned_sem, emptied = s.sem("ready"), s.sem("rows_ready"), s.sem("turned"), s.sem("emptied")
        steps = s.sem("dve_steps")
        block = s.block()
        named = {"src": src, "rel": rel, "dst": dst}

        def load(eng, out, a):
            eng.dma_start(out[:, 0:CHUNKS - 1, :],
                          a[0:(CHUNKS - 1) * P * GROUP].rearrange("(c g e) -> g c e", g=P, e=GROUP)).then_inc(loaded, 16)
            tail(eng, out[:, CHUNKS - 1, :], a)

        def tail(eng, out, a):
            g0, g1 = (CHUNKS - 1) * P, FULL_G
            eng.dma_start(out[0:g1 - g0, :], a[g0 * GROUP:g1 * GROUP].rearrange("(g e) -> g e", e=GROUP)).then_inc(loaded, 16)
            eng.dma_start(out[g1 - g0:g1 - g0 + 1, 0:REST_E], a[g1 * GROUP:E].rearrange("(g e) -> g e", g=1)).then_inc(loaded, 16)

        @block.sync
        def _(sp):
            sp.wait_ge(padded, 5)
            for k in ("dst", "src", "rel"):
                load(sp, raw[k], named[k])
            tail(sp, top, dst)
            load(sp, nrm, norm)

        @block.gpsimd
        def _(pool):
            for k in ("src", "rel"):
                nc.gpsimd.memset(raw[k][:, CHUNKS - 1, :], 0).then_inc(padded, 1)
            nc.gpsimd.memset(raw["dst"][:, CHUNKS - 1, :], N - 1).then_inc(padded, 1)
            nc.gpsimd.memset(top[:], 0).then_inc(padded, 1)
            nc.gpsimd.memset(nrm[:, CHUNKS - 1, :], 0.0).then_inc(padded, 1)
            nc.gpsimd.memset(keep.ident[:], 0.0).then_inc(ident_ready, 1)
            pool.wait_ge(ident_ready, 1)
            nc.gpsimd.affine_select(out=keep.ident[:], in_=keep.ident[:], compare_op=ALU.not_equal, fill=1.0,
                                    base=0, pattern=[[-1, P]], channel_multiplier=1).then_inc(ident_ready, 1)
            nc.gpsimd.iota(keep.offsets[:], [[1, WIN]], base=0, channel_multiplier=0,
                           allow_small_or_imprecise_dtypes=True).then_inc(ident_ready, 1)
            nc.gpsimd.memset(keep.ones[:], 1.0).then_inc(ident_ready, 1)
            nc.gpsimd.memset(keep.eps[:], LN_EPS).then_inc(ident_ready, 1)

        @block.vector
        def _(v):
            step = Chain(v, steps)
            v.wait_ge(loaded, 16 * 14)
            step.mark(nc.vector.tensor_copy(dstf[:], raw["dst"][:]))
            step.mark(nc.vector.tensor_copy(topf[:], top[:]))
            step.mark(nc.vector.tensor_scalar(idx[:], raw["src"][:], float(RELS), None, ALU.mult))
            step.wait()
            step.mark(nc.vector.tensor_tensor(idx[:], idx[:], raw["rel"][:], ALU.add))
            step.mark(nc.vector.tensor_reduce(low[:], dstf[:], AX_X, ALU.min))
            step.mark(nc.vector.tensor_reduce(high[:, 0:CHUNKS - 1], dstf[:, 0:CHUNKS - 1, :], AX_X, ALU.max))
            step.mark(nc.vector.tensor_reduce(high[:, CHUNKS - 1:CHUNKS], topf[:], AX_X, ALU.max))
            step.wait()
            step.mark(nc.vector.tensor_tensor(span[:], high[:], low[:], ALU.subtract))
            for c in range(CHUNKS):
                step.mark(nc.vector.tensor_scalar(dstf[:, c, :], dstf[:, c, :], low[:, c:c + 1], None, ALU.subtract))
            step.wait()
            step(nc.vector.tensor_scalar(span[:], span[:], float(WIN), None, ALU.is_ge))
            nc.vector.tensor_reduce(wide[:], span[:], AX_X, ALU.add).then_inc(ready, 1)
            v.wait_ge(rows_ready, 1)
            nc.vector.tensor_copy(keep.base[:], rows[:].rearrange("o c g -> o (c g)")[:, 0:GROUPS]).then_inc(emptied, 1)
            nc.vector.tensor_copy(keep.far[:], count[:]).then_inc(emptied, 1)
            n = 0
            for out in (keep.winT, keep.idxT, keep.nrmT):
                for c in range(CHUNKS):
                    g = min(P, GROUPS - c * P)
                    v.wait_ge(turned_sem, n + 1)
                    nc.vector.tensor_copy(out[:, c * P * GE:(c * P + g) * GE].rearrange("p (g j) -> p j g", j=GE),
                                          turned[:, n % 2, :, 0:g]).then_inc(emptied, 1)
                    n += 1

        @block.tensor
        def _(pe):
            pe.wait_ge(ready, 1)
            pe.wait_ge(ident_ready, 5)
            for c in range(CHUNKS):
                nc.tensor.matmul(rows[:, c, :], low[:, c:c + 1], keep.ident[:], start=True, stop=True)
            nc.tensor.matmul(count[:], wide[:], keep.ones[:, 0:1], start=True, stop=True).then_inc(rows_ready, 1)
            n = 0
            for a in (dstf, idx, nrm):
                for c in range(CHUNKS):
                    after(pe, emptied, n + 1 if n >= 2 else 0)
                    for j in range(GE):
                        last = nc.tensor.transpose(turned[:, n % 2, j, :], a[:, c, j * P:(j + 1) * P], keep.ident[:])
                    last.then_inc(turned_sem, 1)
                    n += 1


LB = 7
assert TILES % LB == 0


def norm_x(nc, keep, x):
    with Scope(nc) as s:
        xs = s.sb("l_x", [P, LB, C])
        sq = s.sb("l_sq", [P, LB, C])
        total, var, sd, inv, root = (s.sb(f"l_{n}", [P, LB]) for n in ("total", "var", "sd", "inv", "root"))
        turned = s.ps("l_turned", [P, LB, KC, P])
        padded, loaded = s.sem("padded"), s.sem("loaded")
        var_ready, sd_ready, xn_ready = s.sem("var_ready"), s.sem("sd_ready"), s.sem("xn_ready")
        turned_sem, emptied, steps = s.sem("turned"), s.sem("emptied"), s.sem("dve_steps")
        root_ready = s.sem("root_ready")
        block = s.block()
        steps_per = 8

        @block.sync
        def _(sp):
            def body(i):
                after(sp, turned_sem, i - 1)
                if isinstance(i, int) and i == TILES // LB:
                    first = (i - 1) * LB * P
                    sp.dma_start(xs[:, 0:LB - 1, :], x[first:first + (LB - 1) * P, :]
                                 .rearrange("(t p) c -> p t c", p=P)).then_inc(loaded, 16)
                    sp.dma_start(xs[0:LAST, LB - 1, :], x[first + (LB - 1) * P:N, :]).then_inc(loaded, 16)
                else:
                    sp.dma_start(xs[:], x[bass.ds((i - 1) * (LB * P), LB * P), :]
                                 .rearrange("(t p) c -> p t c", p=P)).then_inc(loaded, 16)
            sp.wait_ge(padded, 1)
            loop(sp, body, last=TILES // LB)

        @block.scalar
        def _(act):
            def body(i):
                act.wait_ge(var_ready, i)
                nc.scalar.activation(sd[:], var[:], ACT.Sqrt).then_inc(sd_ready, 1)
            loop(act, body, last=TILES // LB)

        @block.vector
        def _(v):
            step = Chain(v, steps, steps_per)

            def wide(a):
                return a[:].rearrange("p (t o) -> p t o", o=1).broadcast_to([P, LB, C])

            def body(i):
                step.start(i - 1)
                v.wait_ge(loaded, i * 16 if not (isinstance(i, int) and i == TILES // LB) else (i + 1) * 16)
                step(nc.vector.tensor_reduce(total[:], xs[:], AX_X, ALU.add))
                step(nc.vector.tensor_scalar(total[:], total[:], 1.0 / C, None, ALU.mult))
                step(nc.vector.tensor_tensor(xs[:], xs[:], wide(total), ALU.subtract))
                step(nc.vector.tensor_tensor(sq[:], xs[:], xs[:], ALU.mult))
                step(nc.vector.tensor_reduce(var[:], sq[:], AX_X, ALU.add))
                nc.vector.tensor_scalar(var[:], var[:], 1.0 / C, LN_EPS, ALU.mult, ALU.add).then_inc(var_ready, 1)
                v.wait_ge(sd_ready, i)
                step(nc.vector.reciprocal(inv[:], sd[:]))
                v.wait_ge(var_ready, i)
                step(nc.vector.tensor_tensor(inv[:], inv[:], var[:], ALU.mult))
                nc.vector.tensor_tensor(root[:], inv[:], sd[:], ALU.add).then_inc(root_ready, 1)
                v.wait_ge(root_ready, i)
                step(nc.vector.reciprocal(root[:], root[:]))
                nc.vector.scalar_tensor_tensor(out=xs[:], in0=xs[:], scalar=2.0, in1=wide(root), op0=ALU.mult,
                                               op1=ALU.mult).then_inc(xn_ready, 1)
                step.end()
                v.wait_ge(turned_sem, i)
                for k in range(KC):
                    nc.vector.tensor_scalar(keep.xnT[:, k, bass.ds((i - 1) * (LB * P), LB * P)]
                                            .rearrange("p (t n) -> p t n", n=P),
                                            turned[:, :, k, :], 1.0, None, ALU.mult).then_inc(emptied, 1)
            nc.vector.memset(xs[:], 0.0).then_inc(padded, 1)
            loop(v, body, last=TILES // LB)

        @block.tensor
        def _(pe):
            def body(i):
                pe.wait_ge(xn_ready, i)
                after(pe, emptied, KC * (i - 1))
                for t in range(LB):
                    for k in range(KC):
                        last = nc.tensor.transpose(turned[:, t, k, :], xs[:, t, k * P:(k + 1) * P], keep.ident[:])
                last.then_inc(turned_sem, 1)
            loop(pe, body, last=TILES // LB)


CH = 10
RPC = RELS // CH
BANKS = 5


def relations(nc, keep, weight, table):
    with Scope(nc) as s:
        w = s.sb("r_w", [P, KC, RELS, C])
        xT = s.sb("r_xT", [P, 2, KC, P])
        rows = keep.aggT[:].rearrange("p k n -> p (k n)")[:, 0:2 * RELS * C].rearrange("p (b c) -> p b c", b=2)
        acc = s.ps("r_acc", [P, BANKS, 512])
        w_loaded, stored = s.sem("w_loaded"), s.sems("stored", 2)
        x_ready = s.sem("x_ready")
        summed, emptied = s.sems("summed", CH), s.sems("emptied", CH)
        block = s.block()
        out = table.rearrange("(n r) c -> n (r c)", r=RELS)

        def pairs(eng, body):
            body(1, 0, 1)
            body(2, 1, 1)
            with eng.Fori(1, TILES // 2) as i:
                for k in range(2):
                    body(2 * i + (k + 1), k, i + 1)
            body(TILES, 0, TILES // 2 + 1)

        def evacuate(eng, copy, mine):
            def body(n, k, i):
                for c in mine:
                    eng.wait_ge(summed[c], n)
                    if c == mine[0]:
                        after(eng, stored[k], (i - 1) * 16)
                    copy(rows[:, k, c * 512:(c + 1) * 512], acc[:, c % BANKS, :]).then_inc(emptied[c], 1)
            return body

        @block.sync
        def _(sp):
            for k in range(KC):
                sp.dma_start(w[:, k], weight[:, k * P:(k + 1) * P, :].rearrange("r p o -> p r o")).then_inc(w_loaded, 16)

            def body(n, k, i):
                for c in range(CH):
                    sp.wait_ge(emptied[c], n)
                first = (n - 1) * P
                dst = out[first:first + P, :] if isinstance(n, int) else out[bass.ds(first, P), :]
                sp.dma_start(dst, rows[:, k, :]).then_inc(stored[k], 16)
            pairs(sp, body)
            sp.wait_ge(stored[0], (TILES // 2 + 1) * 16)
            sp.wait_ge(stored[1], (TILES // 2) * 16)

        @block.scalar
        def _(act):
            pairs(act, evacuate(act, nc.scalar.copy, list(range(0, CH, 2))))

        @block.vector
        def _(v):
            empty = evacuate(v, nc.vector.tensor_copy, list(range(1, CH, 2)))

            def fix(n, k):
                after(v, summed[CH - 1], n - 2)
                nc.vector.tensor_scalar(xT[:, k], keep.xnT[:, :, bass.ds((n - 1) * P, P)], 1.0, None,
                                        ALU.mult).then_inc(x_ready, 1)

            def body(n, k, i):
                if not (isinstance(n, int) and n == TILES):
                    fix(n + 1, 1 - k)
                empty(n, k, i)
            fix(1, 0)
            pairs(v, body)

        @block.tensor
        def _(pe):
            pe.wait_ge(w_loaded, 16 * KC)

            def body(n, k, i):
                for c in range(CH):
                    if c == 0:
                        pe.wait_ge(x_ready, n)
                    after(pe, emptied[(c + BANKS) % CH], n - 1 if c < BANKS else n)
                    for kc in range(KC):
                        last = nc.tensor.matmul(acc[:, c % BANKS, :], xT[:, k, kc, :],
                                                w[:, kc, c * RPC:(c + 1) * RPC, :].rearrange("p r o -> p (r o)"),
                                                start=(kc == 0), stop=(kc == KC - 1))
                    last.then_inc(summed[c], 1)
            pairs(pe, body)


class Gather:

    def __init__(self, nc, s, keep, table, first, tag, counted=0):
        self.nc, self.keep, self.table, self.first = nc, keep, table, first
        self.counted = counted
        k = f"g_{tag}"
        self.rows = s.sb(f"{k}_rows", [P, GPT, GE, C])
        self.where = s.sb(f"{k}_where", [P, GPT, GE], I32)
        self.hot = s.sb(f"{k}_hot", [P, GPT, GE, WIN])
        self.win = s.sb(f"{k}_win", [P, GPT * GE])
        self.nrm = s.sb(f"{k}_nrm", [P, GPT * GE])
        self.sum = s.ps(f"{k}_sum", [P, 2, 512])
        self.where_ready, self.pool_go = s.sem("where_ready"), s.sem("pool_go")
        self.cols_ready = s.sem("cols_ready")
        self.gathered = s.sems("gathered", GPT)
        self.hot_ready = s.sems("hot_ready", GPT)
        self.summed = s.sems("summed", GPT)
        self.added = s.sem("added")

    def cols(self, at, j=0, n=GPT * GE):
        return bass.ds((at - 1) * (GPT * GE) + (self.first + j) * GE, n)

    def pool_fetch(self, pool, i, at=None):
        at = i if at is None else at
        for j in range(GPT):
            after(pool, self.summed[j], i - 1)
            pool.sem_inc(self.pool_go, 1)
            self.nc.gpsimd.tensor_copy(self.where[:, j, :], self.keep.idxT[:, self.cols(at, j, GE)])\
                .then_inc(self.where_ready, 1)
            pool.wait_ge(self.where_ready, GPT * (i - 1) + (j + 1))
            pool.sem_inc(self.pool_go, 1)
            for t in range(GE):
                self.nc.gpsimd.indirect_dma_start(
                    self.rows[:, j, t, :], None, self.table,
                    bass.IndirectOffsetOnAxis(ap=self.where[:, j, t:t + 1], axis=0)).then_inc(self.gathered[j], 16)

    def vector_hot(self, v, i, at=None):
        at = i if at is None else at
        for a, b in ((self.win, self.keep.winT), (self.nrm, self.keep.nrmT)):
            self.nc.vector.tensor_scalar(a[:], b[:, self.cols(at)], 1.0, None, ALU.mult).then_inc(self.cols_ready, 1)
        v.wait_ge(self.cols_ready, 2 * i)
        for j in range(GPT):
            after(v, self.summed[j], i - 1)
            for t in range(GE):
                c = j * GE + t
                last = self.nc.vector.tensor_scalar(self.hot[:, j, t, :], self.keep.offsets[:], self.win[:, c:c + 1],
                                                    self.nrm[:, c:c + 1], ALU.is_equal, ALU.mult)
            last.then_inc(self.hot_ready[j], 1)

    def tensor_sum(self, pe, i, j):
        pe.wait_ge(self.hot_ready[j], i)
        pe.wait_ge(self.gathered[j], (i - self.counted) * (16 * GE))
        after(pe, self.added, GPT * (i - 1) + (j - 1))
        for t in range(GE):
            for k in range(KC):
                last = self.nc.tensor.matmul(self.sum[:, j % 2, k * WIN:(k + 1) * WIN],
                                             self.rows[:, j, t, k * P:(k + 1) * P], self.hot[:, j, t, :],
                                             start=(t == 0 and k == 0), stop=(t == GE - 1), skip_group_check=True)
        last.then_inc(self.summed[j], 1)

    def vector_add(self, v, i, j, at=None):
        at = i if at is None else at
        v.wait_ge(self.summed[j], i)
        after(v, self.added, GPT * (i - 1) + j)
        node = v.value_load(self.keep.base[0:1, bass.ds((at - 1) * GPT + (self.first + j), 1)], min_val=0, max_val=N)
        self.nc.vector.tensor_tensor(self.keep.aggT[:, :, bass.ds(node, WIN)], self.keep.aggT[:, :, bass.ds(node, WIN)],
                                     self.sum[:, j % 2, 0:KC * WIN].rearrange("p (k w) -> p k w", w=WIN),
                                     ALU.add).then_inc(self.added, 1)


def heads(a, n):
    return a.rearrange("p (h d) -> p h d", d=n)


def features(nc, out, z, ready):
    a = z[:]
    part, off = a.ap[0], a.offset
    shifted = bass.AP(a.tensor, off, [part, (DW, HEADS), (1, SHIFTS), (1, D)])
    plain = bass.AP(a.tensor, off, [part, (DW, HEADS), (0, SHIFTS), (1, D)])
    nc.vector.tensor_tensor(out[:, 0:PAIRS].rearrange("p (h s d) -> p h s d", s=SHIFTS, d=D), plain, shifted,
                            ALU.mult).then_inc(ready, 1)
    nc.vector.tensor_tensor(heads(out[:, PAIRS:PAIRS + HEADS * D], D), z[:, :, 0:D], z[:, :, SHIFTS:DW],
                            ALU.mult).then_inc(ready, 1)
    nc.vector.tensor_copy(heads(out[:, PAIRS + HEADS * D:PAIRS + 2 * HEADS * D], D), z[:, :, 0:D]).then_inc(ready, 1)


def moments(nc, keep, table):
    with Scope(nc) as s:
        g = Gather(nc, s, keep, table, 0, "keys")
        xT = s.sb("m_xT", [P, KC, P])
        kv = s.sb("m_kv", [P, 2 * C])
        sq = s.sb("m_sq", [P, C])
        ss, sd, inv = (s.sb(f"m_{n}", [P, HEADS]) for n in ("ss", "sd", "inv"))
        kd = s.sb("m_kd", [P, HEADS, DW])
        kk = s.sb("m_kk", [P, FT * P])
        v1 = s.sb("m_v1", [P, HEADS, DV])
        proj = s.ps("m_proj", [P, 512])
        acc = s.ps("m_acc", [P, 4, 512])
        x_ready, projected, kv_ready = s.sem("x_ready"), s.sem("projected"), s.sem("kv_ready")
        ss_ready, sd_ready, feats_ready, multiplied = s.sem("ss_ready"), s.sem("sd_ready"), s.sem("feats_ready"), s.sem("multiplied")
        zeroed, steps = s.sem("zeroed"), s.sem("dve_steps")
        block = s.block()
        per_bank = 512 // DV

        def acc_pair(t):
            return acc[:, t // per_bank, (t % per_bank) * DV:(t % per_bank + 1) * DV]
        rest = PT - 2 * per_bank
        wide = HG * DV
        acc_half = [acc[:, 3, q * wide:(q + 1) * wide] for q in range(NG)]
        acc_lin = [acc[:, 3, 2 * wide:3 * wide], acc[:, 2, rest * DV:rest * DV + wide]]
        acc_one = acc[0:1, 2, rest * DV + wide:rest * DV + wide + HEADS * DV]
        assert rest * DV + wide + HEADS * DV <= 512

        @block.gpsimd
        def _(pool):
            loop(pool, lambda i: g.pool_fetch(pool, i))

        @block.scalar
        def _(act):
            def body(i):
                act.wait_ge(ss_ready, i)
                nc.scalar.activation(sd[:], ss[:], ACT.Sqrt).then_inc(sd_ready, 1)
            loop(act, body)

        @block.vector
        def _(v):
            step = Chain(v, steps, 9)
            nc.vector.memset(v1[:], 1.0).then_inc(zeroed, 1)
            nc.vector.memset(keep.aggT[:], 0.0).then_inc(zeroed, 1)
            v.wait_ge(zeroed, 2)

            def body(i):
                step.start(i - 1)
                after(v, projected, i - 1)
                nc.vector.tensor_scalar(xT[:], keep.xnT[:, :, bass.ds((i - 1) * P, P)], 1.0, None,
                                        ALU.mult).then_inc(x_ready, 1)
                g.vector_hot(v, i)
                v.wait_ge(projected, i)
                after(v, multiplied, i - 1)
                nc.vector.tensor_tensor(kv[:], proj[:], keep.bias_qkv[:, C:3 * C], ALU.add).then_inc(kv_ready, 1)
                v.wait_ge(kv_ready, i)
                step(nc.vector.tensor_tensor(sq[:], kv[:, 0:C], kv[:, 0:C], ALU.mult))
                step(nc.vector.tensor_reduce(ss[:], heads(sq[:], D), AX_X, ALU.add))
                nc.vector.tensor_scalar(ss[:], ss[:], ROOT_EPS * ROOT_EPS, None, ALU.max).then_inc(ss_ready, 1)
                step(nc.vector.tensor_copy(v1[:, :, 1:DV], heads(kv[:, C:2 * C], D)))
                v.wait_ge(sd_ready, i)
                step(nc.vector.reciprocal(inv[:], sd[:]))
                step(nc.vector.tensor_tensor(inv[:], inv[:], ss[:], ALU.mult))
                step(nc.vector.tensor_tensor(inv[:], inv[:], sd[:], ALU.add))
                step(nc.vector.reciprocal(inv[:], inv[:]))
                scaled = inv[:].rearrange("p (h o) -> p h o", o=1)
                for a, n in ((0, D), (D, SHIFTS)):
                    step.mark(nc.vector.scalar_tensor_tensor(out=kd[:, :, a:a + n], in0=heads(kv[:, 0:C], D)[:, :, 0:n],
                                                             scalar=2.0 * SC, in1=scaled.broadcast_to([P, HEADS, n]),
                                                             op0=ALU.mult, op1=ALU.mult))
                step.wait()
                g.vector_add(v, i, 0)
                features(nc, kk, kd, feats_ready)
                step.end()
                for j in range(1, GPT):
                    g.vector_add(v, i, j)
            loop(v, body)
            v.wait_ge(multiplied, TILES)
            for t in range(PT):
                nc.vector.tensor_scalar(keep.mom[:, t, :], acc_pair(t), keep.factor[:, min(t % TPH, 1):min(t % TPH, 1) + 1],
                                        None, ALU.mult)
            for q in range(NG):
                for n, (a, f) in enumerate(((acc_half[q], 0.5 / N), (acc_lin[q], SC ** 2 / N))):
                    nc.vector.scalar_tensor_tensor(out=keep.momw[:, n * NG + q], in0=a, scalar=f,
                                                   in1=keep.own[:].rearrange("p h e -> p (h e)"),
                                                   op0=ALU.mult, op1=ALU.mult)
            nc.vector.tensor_scalar(keep.mom1[:], acc_one, SC ** 4 / N, None, ALU.mult)

        @block.tensor
        def _(pe):
            def body(i):
                first = isinstance(i, int) and i == 1
                last_tile = isinstance(i, int) and i == TILES
                m = LAST if last_tile else P
                pe.wait_ge(x_ready, i)
                after(pe, kv_ready, i - 1)
                for k in range(KC):
                    last = nc.tensor.matmul(proj[:], xT[:, k, :], keep.wT[:, k, C:3 * C], start=(k == 0), stop=(k == KC - 1))
                last.then_inc(projected, 1)
                g.tensor_sum(pe, i, 0)
                pe.wait_ge(feats_ready, 3 * i)

                def add(out, lhs, rhs, opens):
                    return nc.tensor.matmul(out, lhs, rhs, start=(first and opens), stop=last_tile,
                                            skip_group_check=True)
                for t in range(PT):
                    add(acc_pair(t), kk[0:m, t * P:(t + 1) * P], v1[0:m, t // TPH, :], t % per_bank == 0)
                for q in range(NG):
                    h = slice(q * HG, (q + 1) * HG)
                    rhs = v1[0:m, h, :].rearrange("p h e -> p (h e)")
                    add(acc_half[q], kk[0:m, PAIRS + q * P:PAIRS + (q + 1) * P], rhs, q == 0)
                    add(acc_lin[q], kk[0:m, (PT + NG + q) * P:(PT + NG + q + 1) * P], rhs, False)
                add(acc_one, keep.ones[0:m, 0:1], v1[0:m].rearrange("p h e -> p (h e)"), False).then_inc(multiplied, 1)
                for j in range(1, GPT):
                    g.tensor_sum(pe, i, j)
            loop(pe, body)


FB = 4
assert FT % FB == 0


def readout(nc, keep, table, x, x1):
    with Scope(nc) as s:
        g = Gather(nc, s, keep, table, GPT * TILES, "queries")
        xT = s.sb("q_xT", [P, KC, P])
        xs = s.sb("q_x", [P, C])
        q = s.sb("q_q", [P, C])
        sq = s.sb("q_sq", [P, C])
        ss, sd, inv, ry = (s.sb(f"q_{n}", [P, HEADS]) for n in ("ss", "sd", "inv", "ry"))
        qd = s.sb("q_qd", [P, HEADS, DW])
        qq = s.sb("q_qq", [P, FT * P])
        fT = s.sb("q_fT", [P, FT, P])
        o = s.sb("q_o", [P, C])
        oT = s.sb("q_oT", [P, KC, P])
        res = s.sb("q_res", [P, C])
        proj = s.ps("q_proj", [P, 512])
        turned = s.ps("q_turned", [P, 2, FB, P])
        y = s.ps("q_y", [P, 512])
        oTp = s.ps("q_oTp", [P, 512])
        out = s.ps("q_out", [P, 512])
        x_ready, projected, q_ready, ss_ready, sd_ready = (s.sem(n) for n in (
            "x_ready", "projected", "q_ready", "ss_ready", "sd_ready"))
        feats_ready, turned_sem, copied, y_ready, o_ready, o_turned, oT_ready, out_ready, res_ready = (s.sem(n) for n in (
            "feats_ready", "turned", "copied", "y_ready", "o_ready", "o_turned", "oT_ready", "out_ready", "res_ready"))
        x_loaded, stored, steps, biased = s.sem("x_loaded"), s.sem("stored"), s.sem("dve_steps"), s.sem("biased")
        block = s.block()
        nb = FT // FB

        @block.sync
        def _(sp):
            def body(i):
                after(sp, res_ready, i - 1)
                if isinstance(i, int) and i == TILES:
                    sp.dma_start(xs[0:LAST, :], x[(TILES - 1) * P:N, :]).then_inc(x_loaded, 16)
                    sp.wait_ge(res_ready, i)
                    sp.dma_start(x1[(TILES - 1) * P:NPAD, :], res[:]).then_inc(stored, 16)
                else:
                    sp.dma_start(xs[:], x[bass.ds((i - 1) * P, P), :]).then_inc(x_loaded, 16)
                    sp.wait_ge(res_ready, i)
                    sp.dma_start(x1[bass.ds((i - 1) * P, P), :], res[:]).then_inc(stored, 16)
            loop(sp, body)
            sp.wait_ge(stored, TILES * 16)

        @block.gpsimd
        def _(pool):
            loop(pool, lambda i: g.pool_fetch(pool, i))

        @block.scalar
        def _(act):
            def body(i):
                act.wait_ge(ss_ready, i)
                nc.scalar.activation(sd[:], ss[:], ACT.Sqrt).then_inc(sd_ready, 1)
                for b in range(nb):
                    act.wait_ge(turned_sem, nb * (i - 1) + (b + 1))
                    if b == 0:
                        after(act, y_ready, i - 1)
                    nc.scalar.copy(fT[:, b * FB:(b + 1) * FB, :], turned[:, b % 2]).then_inc(copied, 1)
                act.wait_ge(o_turned, i)
                nc.scalar.copy(oT[:].rearrange("p k n -> p (k n)"), oTp[:, 0:C]).then_inc(oT_ready, 1)
            loop(act, body)

        @block.vector
        def _(v):
            step = Chain(v, steps, 10)

            def body(i):
                step.start(i - 1)
                after(v, projected, i - 1)
                nc.vector.tensor_scalar(xT[:], keep.xnT[:, :, bass.ds((i - 1) * P, P)], 1.0, None,
                                        ALU.mult).then_inc(x_ready, 1)
                g.vector_hot(v, i)
                v.wait_ge(projected, i)
                after(v, turned_sem, nb * (i - 1))
                nc.vector.tensor_tensor(q[:], proj[:, 0:C], keep.bias_qkv[:, 0:C], ALU.add).then_inc(q_ready, 1)
                v.wait_ge(q_ready, i)
                step(nc.vector.tensor_tensor(sq[:], q[:], q[:], ALU.mult))
                step(nc.vector.tensor_reduce(ss[:], heads(sq[:], D), AX_X, ALU.add))
                nc.vector.tensor_scalar(ss[:], ss[:], SC * SC, ROOT_EPS * ROOT_EPS, ALU.mult, ALU.max).then_inc(ss_ready, 1)
                v.wait_ge(sd_ready, i)
                step(nc.vector.reciprocal(inv[:], sd[:]))
                step(nc.vector.tensor_tensor(inv[:], inv[:], ss[:], ALU.mult))
                step(nc.vector.tensor_tensor(inv[:], inv[:], sd[:], ALU.add))
                step(nc.vector.reciprocal(inv[:], inv[:]))
                step(nc.vector.tensor_tensor(inv[:], inv[:], keep.temp[:], ALU.mult))
                scaled = inv[:].rearrange("p (h o) -> p h o", o=1)
                for a, n in ((0, D), (D, SHIFTS)):
                    step.mark(nc.vector.tensor_tensor(qd[:, :, a:a + n], heads(q[:], D)[:, :, 0:n],
                                                      scaled.broadcast_to([P, HEADS, n]), ALU.mult))
                step.wait()
                g.vector_add(v, i, 0)
                features(nc, qq, qd, feats_ready)
                g.vector_add(v, i, 1)
                v.wait_ge(y_ready, i)
                yh = y[:, 0:HEADS * DV].rearrange("p (h e) -> p h e", e=DV)
                step(nc.vector.reciprocal(ry[:].rearrange("p (h o) -> p h o", o=1), yh[:, :, 0:1]))
                nc.vector.tensor_tensor(heads(o[:], D), yh[:, :, 1:DV],
                                        ry[:].rearrange("p (h o) -> p h o", o=1).broadcast_to([P, HEADS, D]),
                                        ALU.mult).then_inc(o_ready, 1)
                g.vector_add(v, i, 2)
                v.wait_ge(out_ready, i)
                after(v, stored, (i - 1) * 16)
                v.wait_ge(x_loaded, i * 16)
                nc.vector.tensor_tensor(xs[:], xs[:], keep.bias_p[:], ALU.add).then_inc(biased, 1)
                v.wait_ge(biased, i)
                nc.vector.tensor_tensor(res[:], out[:, 0:C], xs[:], ALU.add).then_inc(res_ready, 1)
                g.vector_add(v, i, 3)
                step.end()
            loop(v, body)

        @block.tensor
        def _(pe):
            def body(i):
                pe.wait_ge(x_ready, i)
                after(pe, q_ready, i - 1)
                for k in range(KC):
                    last = nc.tensor.matmul(proj[:, 0:C], xT[:, k, :], keep.wT[:, k, 0:C], start=(k == 0), stop=(k == KC - 1))
                last.then_inc(projected, 1)
                g.tensor_sum(pe, i, 0)
                pe.wait_ge(feats_ready, 3 * i)
                for b in range(nb):
                    after(pe, copied, nb * (i - 1) + (b - 1))
                    for n in range(FB):
                        t = b * FB + n
                        last = nc.tensor.transpose(turned[:, b % 2, n, :], qq[:, t * P:(t + 1) * P], keep.ident[:])
                    last.then_inc(turned_sem, 1)
                g.tensor_sum(pe, i, 1)
                pe.wait_ge(copied, nb * i)
                after(pe, o_ready, i - 1)
                nc.tensor.matmul(y[:, 0:HEADS * DV], keep.ones[0:1, :], keep.mom1[:], start=True, stop=False,
                                 skip_group_check=True)
                for t in range(PT):
                    h = t // TPH
                    nc.tensor.matmul(y[:, h * DV:(h + 1) * DV], fT[:, t, :], keep.mom[:, t, :], start=False, stop=False,
                                     skip_group_check=True)
                for n in range(2 * NG):
                    w = HG * DV
                    last = nc.tensor.matmul(y[:, (n % NG) * w:(n % NG + 1) * w], fT[:, PT + n, :], keep.momw[:, n],
                                            start=False, stop=(n >= NG), skip_group_check=True)
                last.then_inc(y_ready, 1)
                g.tensor_sum(pe, i, 2)
                pe.wait_ge(o_ready, i)
                for k in range(KC):
                    last = nc.tensor.transpose(oTp[:, k * P:(k + 1) * P], o[:, k * P:(k + 1) * P], keep.ident[:])
                last.then_inc(o_turned, 1)
                pe.wait_ge(oT_ready, i)
                after(pe, res_ready, i - 1)
                for k in range(KC):
                    last = nc.tensor.matmul(out[:, 0:C], oT[:, k, :], keep.wpT[:, k, :], start=(k == 0), stop=(k == KC - 1))
                last.then_inc(out_ready, 1)
                g.tensor_sum(pe, i, 3)
            loop(pe, body)


def weights(nc, keep, wqkv, bqkv, wproj, bproj, temperature):
    with Scope(nc) as s:
        rows = 3 * C // P
        w = s.sb("w_qkv", [P, rows, C])
        wp = s.sb("w_proj", [P, KC, C])
        turned = s.ps("w_turned", [P, KC, 2, 512])
        loaded, turned_sem, factors = s.sem("loaded"), s.sem("turned"), s.sem("factors")
        block = s.block()

        @block.sync
        def _(sp):
            sp.dma_start(w[:], wqkv.rearrange("(r p) c -> p r c", p=P)).then_inc(loaded, 16)
            sp.dma_start(wp[:], wproj.rearrange("(r p) c -> p r c", p=P)).then_inc(loaded, 16)
            sp.dma_start(keep.bias_qkv[:], bqkv.partition_broadcast(P)).then_inc(loaded, 16)
            sp.dma_start(keep.bias_p[:], bproj.partition_broadcast(P)).then_inc(loaded, 16)
            sp.dma_start(keep.temp[:], temperature.rearrange("a h b c -> (a h b c)").partition_broadcast(P)).then_inc(loaded, 16)

        @block.tensor
        def _(pe):
            pe.wait_ge(loaded, 5 * 16)
            for k in range(KC):
                for r in range(rows):
                    nc.tensor.transpose(turned[:, k, r * P // 512, r * P % 512:r * P % 512 + P],
                                        w[:, r, k * P:(k + 1) * P], keep.ident[:])
                for r in range(KC):
                    last = nc.tensor.transpose(turned[:, k, 1, 256 + r * P:256 + (r + 1) * P],
                                               wp[:, r, k * P:(k + 1) * P], keep.ident[:])
            last.then_inc(turned_sem, 1)

        @block.vector
        def _(v):
            v.wait_ge(loaded, 5 * 16)
            nc.vector.tensor_scalar(keep.temp[:], keep.temp[:], 2.0 * SC * SC, None, ALU.mult)
            nc.vector.memset(keep.factor[:], 1.0 / N).then_inc(factors, 1)
            nc.vector.memset(keep.own[:], 0.0).then_inc(factors, 1)
            v.wait_ge(factors, 2)
            nc.vector.memset(keep.factor[0:D, 0:1], 0.5 / N)
            for h in range(HG):
                nc.vector.memset(keep.own[h * D:(h + 1) * D, h, :], 1.0)
            v.wait_ge(turned_sem, 1)
            for k in range(KC):
                t = turned[:, k].rearrange("p b n -> p (b n)")
                nc.vector.tensor_copy(keep.wT[:, k, :], t[:, 0:3 * C])
                nc.vector.tensor_copy(keep.wpT[:, k, :], t[:, 3 * C:4 * C])


def far_edges(nc, keep, table):
    with Scope(nc) as s:
        g = Gather(nc, s, keep, table, 0, "far", counted=1)
        shifted, shift_seen = s.sem("shifted"), s.sem("shift_seen")
        block = s.block()
        steps = GROUPS // GPT

        def rounds(eng, body, before=None):
            far = eng.value_load(keep.far[0:1, 0:1], min_val=0, max_val=GROUPS)
            with eng.If(far > 0):
                with eng.Fori(1, WINDOWS) as k:
                    if before:
                        before(k)
                    with eng.Fori(0, steps) as n:
                        body((k - 1) * steps + n + 2, n + 1)

        @block.gpsimd
        def _(pool):
            pool.sem_inc(g.where_ready, GPT)
            rounds(pool, lambda i, at: g.pool_fetch(pool, i, at))

        @block.vector
        def _(v):
            for sem, n in [(g.cols_ready, 2), (g.added, GPT)] + [(x, 1) for x in g.hot_ready]:
                v.sem_inc(sem, n)

            def shift(k):
                v.wait_ge(g.added, (k - 1) * (steps * GPT) + GPT)
                nc.vector.tensor_scalar(keep.winT[:], keep.winT[:], -float(WIN), None, ALU.add).then_inc(shifted, 1)
                nc.vector.tensor_scalar(keep.base[:], keep.base[:], float(WIN), float(N), ALU.add,
                                        ALU.min).then_inc(shifted, 1)
                v.wait_ge(shifted, 2 * k)
                v.sem_inc(shift_seen, 1)

            def body(i, at):
                g.vector_hot(v, i, at)
                for j in range(GPT):
                    g.vector_add(v, i, j, at)
            rounds(v, body, shift)

        @block.tensor
        def _(pe):
            for sem in g.summed:
                pe.sem_inc(sem, 1)

            def body(i, at):
                for j in range(GPT):
                    g.tensor_sum(pe, i, j)
            rounds(pe, body)


def experts(nc, keep, x1, W1, b1, Wg, bg, Wd, bd, out):
    with Scope(nc) as s:
        w1 = s.sb("f_w1", [P, KC, HID])
        wd = s.sb("f_wd", [P, HC, EXP, C])
        wg = s.sb("f_wg", [P, HC, EXP])
        b1r = s.sb("f_b1r", [HC, P])
        b1T = s.sb("f_b1", [P, HC])
        bgb = s.sb("f_bg", [P, EXP])
        bds = s.sb("f_bd", [EXP, C])
        first = s.sb("f_first", [P, EXP])
        agg = s.sb("f_agg", [P, KC, P])
        x1s = s.sb("f_x1", [P, C])
        x2 = s.sb("f_x2", [P, C])
        xc = s.sb("f_xc", [P, C])
        sq = s.sb("f_sq", [P, C])
        xT = s.sb("f_xT", [P, KC, P])
        h = s.sb("f_h", [P, HC, P])
        acc = s.sb("f_acc", [P, C])
        mean, var, sd, inv, mx, tot, best = (s.sb(f"f_{n}", [P, 1]) for n in ("mean", "var", "sd", "inv", "mx", "tot", "best"))
        lg, ex, score, coef = (s.sb(f"f_{n}", [P, EXP]) for n in ("lg", "ex", "score", "coef"))
        coefT = s.sb("f_coefT", [EXP, P])
        turned = s.ps("f_turned", [P, 512])
        hp = s.ps("f_hp", [P, 2, 4, P])
        small = s.ps("f_small", [P, 512])
        yp = s.ps("f_yp", [P, EXP // 2, 2, C])
        loaded, b1_turned, consts = s.sem("loaded"), s.sem("b1_turned"), s.sem("consts")
        names = ("x1_loaded", "stored", "agg_ready", "agg_turned", "x2_ready", "var_ready", "sd_ready", "xn_ready", "xn_turned",
                 "xT_ready", "logits", "shifted", "exps", "coef_ready", "coef_turned", "coefT_ready", "bias_ready",
                 "acc_ready", "best_ready", "with_bias")
        m = {n: s.sem(n) for n in names}
        h_summed, h_ready, y_ready, y_used = s.sems("h_summed", 2), s.sems("h_ready", 2), s.sem("y_ready"), s.sem("y_used")
        steps = s.sem("dve_steps")
        block = s.block()

        @block.sync
        def _(sp):
            for dst, src in ((w1[:], W1.rearrange("(k p) h -> p k h", p=P)),
                             (wg[:], Wg.rearrange("(c p) e -> p c e", p=P)),
                             (b1r[:], b1.rearrange("(c p) -> c p", p=P)), (bgb[:], bg.partition_broadcast(P)), (bds[:], bd)):
                sp.dma_start(dst, src).then_inc(loaded, 16)
            for c in range(HC):
                sp.dma_start(wd[:, c], Wd[:, c * P:(c + 1) * P, :].rearrange("e p o -> p e o")).then_inc(loaded, 16)

            def body(i):
                after(sp, m["x2_ready"], i - 1)
                last = isinstance(i, int) and i == TILES
                rows = slice((TILES - 1) * P, NPAD) if last else bass.ds((i - 1) * P, P)
                sp.dma_start(x1s[:], x1[rows, :]).then_inc(m["x1_loaded"], 16)
                sp.wait_ge(m["acc_ready"], EXP * i)
                if last:
                    sp.dma_start(out[(TILES - 1) * P:N, :], acc[0:LAST, :]).then_inc(m["stored"], 16)
                else:
                    sp.dma_start(out[rows, :], acc[:]).then_inc(m["stored"], 16)
            loop(sp, body)
            sp.wait_ge(m["stored"], TILES * 16)

        @block.scalar
        def _(act):
            def body(i):
                act.wait_ge(m["var_ready"], i)
                nc.scalar.activation(sd[:], var[:], ACT.Sqrt).then_inc(m["sd_ready"], 1)
                for b in range(2):
                    act.wait_ge(h_summed[b], i)
                    if b == 0:
                        after(act, y_ready, i - 1)
                    for c in range(4):
                        n = b * 4 + c
                        last = nc.scalar.activation(h[:, n, :], hp[:, b, c, :], ACT.Gelu, bias=b1T[:, n:n + 1])
                    last.then_inc(h_ready[b], 1)
                act.wait_ge(m["shifted"], i)
                nc.scalar.activation(ex[:], lg[:], ACT.Exp, accum_out=tot[:]).then_inc(m["exps"], 1)
            act.wait_ge(b1_turned, 1)
            nc.scalar.copy(b1T[:], small[:, 0:HC]).then_inc(consts, 1)
            act.wait_ge(consts, EXP + 1)
            loop(act, body)

        @block.vector
        def _(v):
            step = Chain(v, steps, 15)
            for e in range(EXP):
                nc.vector.memset(first[:, e:e + 1], float(EXP - e)).then_inc(consts, 1)
            v.wait_ge(consts, EXP + 1)
            v.wait_ge(loaded, 16 * (5 + HC))

            def body(i):
                step.start(i - 1)
                after(v, m["agg_turned"], i - 1)
                nc.vector.tensor_scalar(agg[:], keep.aggT[:, :, bass.ds((i - 1) * P, P)], 0.0, None,
                                        ALU.max).then_inc(m["agg_ready"], 1)
                v.wait_ge(m["agg_turned"], i)
                v.wait_ge(m["x1_loaded"], 16 * i)
                nc.vector.tensor_tensor(x2[:], x1s[:], turned[:, 0:C], ALU.add).then_inc(m["x2_ready"], 1)
                v.wait_ge(m["x2_ready"], i)
                step(nc.vector.tensor_reduce(mean[:], x2[:], AX_X, ALU.add))
                step(nc.vector.tensor_scalar(mean[:], mean[:], 1.0 / C, None, ALU.mult))
                step(nc.vector.tensor_scalar(xc[:], x2[:], mean[:], None, ALU.subtract))
                step(nc.vector.tensor_tensor(sq[:], xc[:], xc[:], ALU.mult))
                step(nc.vector.tensor_reduce(var[:], sq[:], AX_X, ALU.add))
                nc.vector.tensor_scalar(var[:], var[:], 1.0 / C, LN_EPS, ALU.mult, ALU.add).then_inc(m["var_ready"], 1)
                v.wait_ge(m["sd_ready"], i)
                step(nc.vector.reciprocal(inv[:], sd[:]))
                step(nc.vector.tensor_tensor(inv[:], inv[:], var[:], ALU.mult))
                step(nc.vector.tensor_tensor(inv[:], inv[:], sd[:], ALU.add))
                step(nc.vector.reciprocal(inv[:], inv[:]))
                nc.vector.tensor_scalar(xc[:], xc[:], inv[:], 2.0, ALU.mult, ALU.mult).then_inc(m["xn_ready"], 1)
                v.wait_ge(m["xn_turned"], i)
                nc.vector.tensor_copy(xT[:].rearrange("p k n -> p (k n)"), turned[:, 0:C]).then_inc(m["xT_ready"], 1)
                v.wait_ge(m["logits"], i)
                step(nc.vector.tensor_tensor(lg[:], small[:, 0:EXP], bgb[:], ALU.add))
                step(nc.vector.tensor_reduce(mx[:], lg[:], AX_X, ALU.max))
                nc.vector.tensor_scalar(lg[:], lg[:], mx[:], None, ALU.subtract).then_inc(m["shifted"], 1)
                v.wait_ge(m["exps"], i)
                step(nc.vector.reciprocal(tot[:], tot[:]))
                step(nc.vector.tensor_scalar(ex[:], ex[:], tot[:], None, ALU.mult))
                step(nc.vector.tensor_reduce(mx[:], ex[:], AX_X, ALU.max))
                step(nc.vector.scalar_tensor_tensor(out=score[:], in0=ex[:], scalar=mx[:], in1=first[:],
                                                    op0=ALU.is_ge, op1=ALU.mult))
                nc.vector.tensor_reduce(best[:], score[:], AX_X, ALU.max).then_inc(m["best_ready"], 1)
                v.wait_ge(m["best_ready"], i)
                nc.vector.scalar_tensor_tensor(out=coef[:], in0=score[:], scalar=best[:], in1=ex[:],
                                               op0=ALU.is_equal, op1=ALU.mult).then_inc(m["coef_ready"], 1)
                v.wait_ge(m["coef_turned"], i)
                nc.vector.tensor_copy(coefT[:], turned[0:EXP, 0:P]).then_inc(m["coefT_ready"], 1)
                v.wait_ge(m["bias_ready"], i)
                after(v, m["stored"], 16 * (i - 1))
                v.wait_ge(m["coef_ready"], i)
                for e in range(EXP):
                    if e == 0:
                        nc.vector.tensor_tensor(sq[:], x2[:], small[:, 0:C], ALU.add).then_inc(m["with_bias"], 1)
                        v.wait_ge(m["with_bias"], i)
                    else:
                        v.wait_ge(m["acc_ready"], EXP * (i - 1) + e)
                    if e % 2 == 0:
                        v.wait_ge(y_ready, (EXP // 2) * (i - 1) + (e // 2 + 1))
                    nc.vector.scalar_tensor_tensor(out=acc[:], in0=yp[:, e // 2, e % 2, :], scalar=coef[:, e:e + 1],
                                                   in1=sq[:] if e == 0 else acc[:], op0=ALU.mult,
                                                   op1=ALU.add).then_inc(m["acc_ready"], 1)
                step.end()
            loop(v, body)

        @block.tensor
        def _(pe):
            pe.wait_ge(loaded, 16 * (5 + HC))
            nc.tensor.transpose(small[:, 0:HC], b1r[:], keep.ident[0:HC, 0:HC]).then_inc(b1_turned, 1)
            pe.wait_ge(consts, EXP + 1)

            def body(i):
                pe.wait_ge(m["agg_ready"], i)
                after(pe, m["coefT_ready"], i - 1)
                for k in range(KC):
                    last = nc.tensor.transpose(turned[:, k * P:(k + 1) * P], agg[:, k, :], keep.ident[:])
                last.then_inc(m["agg_turned"], 1)
                pe.wait_ge(m["xn_ready"], i)
                for k in range(KC):
                    last = nc.tensor.transpose(turned[:, k * P:(k + 1) * P], xc[:, k * P:(k + 1) * P], keep.ident[:])
                last.then_inc(m["xn_turned"], 1)
                pe.wait_ge(m["xT_ready"], i)
                for b in range(2):
                    after(pe, h_ready[b], i - 1)
                    for c in range(4):
                        n = b * 4 + c
                        for k in range(KC):
                            last = nc.tensor.matmul(hp[:, b, c, :], w1[:, k, n * P:(n + 1) * P], xT[:, k, :],
                                                    start=(k == 0), stop=(k == KC - 1))
                    last.then_inc(h_summed[b], 1)
                for b in range(2):
                    pe.wait_ge(h_ready[b], i)
                after(pe, m["acc_ready"], EXP * (i - 1))
                for c in range(HC):
                    last = nc.tensor.matmul(small[:, 0:EXP], h[:, c, :], wg[:, c, :], start=(c == 0), stop=(c == HC - 1))
                last.then_inc(m["logits"], 1)
                for b in range(EXP // 2):
                    after(pe, m["acc_ready"], EXP * (i - 1))
                    for c in range(HC):
                        last = nc.tensor.matmul(yp[:, b].rearrange("p e c -> p (e c)"), h[:, c, :],
                                                wd[:, c, 2 * b:2 * b + 2, :].rearrange("p e c -> p (e c)"),
                                                start=(c == 0), stop=(c == HC - 1))
                    last.then_inc(y_ready, 1)
                    if b == 0:
                        pe.wait_ge(m["coef_ready"], i)
                        nc.tensor.transpose(turned[0:EXP, 0:P], coef[:], keep.ident[:]).then_inc(m["coef_turned"], 1)
                        pe.wait_ge(m["coefT_ready"], i)
                        nc.tensor.matmul(small[:, 0:C], coefT[:], bds[:], start=True, stop=True).then_inc(m["bias_ready"], 1)
            loop(pe, body)


class Keep:
    pass


def build(nc, x, src, dst, edge_type_20, edge_weight1, L0_gnn_weight, L0_mix_Wqkv, L0_mix_bqkv, L0_mix_Wproj,
          L0_mix_bproj, L0_mix_temperature, L0_ffn_W1, L0_ffn_b1, L0_ffn_Wg, L0_ffn_bg, L0_ffn_Wd, L0_ffn_bd, out):
    table = nc.dram_tensor("table", (NPAD * RELS, C), F32, kind="Internal").ap()
    x1 = nc.dram_tensor("x1", (NPAD, C), F32, kind="Internal").ap()
    keep = Keep()
    with Scope(nc) as s:
        keep.ident = s.sb("k_ident", [P, P])
        keep.offsets = s.sb("k_offsets", [P, WIN])
        keep.ones = s.sb("k_ones", [P, P])
        keep.eps = s.sb("k_eps", [P, 1])
        keep.idxT = s.sb("k_idxT", [P, COLS], I32)
        keep.winT = s.sb("k_winT", [P, COLS])
        keep.nrmT = s.sb("k_nrmT", [P, COLS])
        keep.base = s.sb("k_base", [1, GROUPS], I32)
        keep.far = s.sb("k_far", [1, 1], I32)
        keep.wT = s.sb("k_wT", [P, KC, 3 * C])
        keep.wpT = s.sb("k_wpT", [P, KC, C])
        keep.bias_qkv = s.sb("k_bias_qkv", [P, 3 * C])
        keep.bias_p = s.sb("k_bias_p", [P, C])
        keep.temp = s.sb("k_temp", [P, HEADS])
        keep.factor = s.sb("k_factor", [P, 2])
        keep.own = s.sb("k_own", [P, HG, DV])
        keep.mom = s.sb("k_mom", [P, PT, DV])
        keep.momw = s.sb("k_momw", [P, 2 * NG, HG * DV])
        keep.mom1 = s.sb("k_mom1", [1, HEADS * DV])
        edges(nc, keep, src, dst, edge_type_20, edge_weight1.rearrange("e o -> (e o)"))
        weights(nc, keep, L0_mix_Wqkv, L0_mix_bqkv, L0_mix_Wproj, L0_mix_bproj, L0_mix_temperature)
        keep.aggT = s.sb("k_aggT", [P, KC, AGG])
        with Scope(nc) as t:
            keep.xnT = t.sb("k_xnT", [P, KC, NPAD])
            norm_x(nc, keep, x)
            relations(nc, keep, L0_gnn_weight, table)
            moments(nc, keep, table)
            readout(nc, keep, table, x, x1)
            far_edges(nc, keep, table)
        experts(nc, keep, x1, L0_ffn_W1, L0_ffn_b1, L0_ffn_Wg, L0_ffn_bg, L0_ffn_Wd, L0_ffn_bd, out)


_INS = ['x', 'src', 'dst', 'edge_type_20', 'edge_weight1', 'L0_gnn_weight', 'L0_mix_Wqkv', 'L0_mix_bqkv',
        'L0_mix_Wproj', 'L0_mix_bproj', 'L0_mix_temperature', 'L0_ffn_W1', 'L0_ffn_b1', 'L0_ffn_Wg', 'L0_ffn_bg',
        'L0_ffn_Wd', 'L0_ffn_bd']
_OUTS = [((N, C), 'float32')]


def kernel(**inputs):
    import numpy as _np
    import concourse.bacc as _bacc
    from concourse import mybir as _mybir
    from concourse.bass_utils import run_bass_kernel_spmd as _run

    nc = _bacc.Bacc("TRN2", target_bir_lowering=False, num_devices=1)
    arrays, args = {}, []
    for name in _INS:
        a = _np.ascontiguousarray(inputs[name])
        arrays[f"in_{name}_dram"] = a
        args.append(nc.dram_tensor(f"in_{name}_dram", a.shape, _mybir.dt.from_np(a.dtype), kind="ExternalInput").ap())
    for i, (shape, dtype) in enumerate(_OUTS):
        dt = _mybir.dt.from_np(_np.dtype(dtype))
        args.append(nc.dram_tensor(f"out_{i}_dram", shape, dt, kind="ExternalOutput").ap())
    build(nc, *args)
    r = _run(nc, [arrays], core_ids=[0])
    got = tuple(r.results[0][f"out_{i}_dram"] for i in range(len(_OUTS)))
    return got[0]
```

```python
from contextlib import ExitStack

import numpy as np

import concourse.bass as bass
from concourse import mybir

ALU = mybir.AluOpType
ACT = mybir.ActivationFunctionType
F32 = mybir.dt.float32
F32R = mybir.dt.float32r
I32 = mybir.dt.int32
AX_X = mybir.AxisListType.X

P = 128
N, C = 6250, 256
KC = C // P
TILES = (N + P - 1) // P
NPAD = TILES * P
LAST = N - (TILES - 1) * P
LN_EPS = 1e-5

E, RELS = 200000, 20
GE = 4
GROUP = GE * P
WIN = 64
GPT = 4
GROUPS = 2 * GPT * TILES
CHUNKS = (GROUPS + P - 1) // P
COLS = GROUPS * GE
FULL_G, REST_E = E // GROUP, E % GROUP
WINDOWS = (N + WIN - 1) // WIN
AGG = N + WIN
assert GROUPS * GROUP >= E and FULL_G // P == CHUNKS - 1

HEADS, D = 8, 32
DV = D + 1
SHIFTS = D // 2
PAIRS = HEADS * SHIFTS * D
PT = PAIRS // P
TPH = PT // HEADS
FT = PT + 2 * HEADS * D // P
DW = D + SHIFTS
SC = float(D) ** 0.25
ROOT_EPS = 1e-12

HID, EXP = 1024, 8
HC = HID // P


def after(eng, sem, value):
    if isinstance(value, int) and value <= 0:
        return
    eng.wait_ge(sem, value)


class Chain:

    def __init__(self, eng, sem, per=0):
        self.eng, self.sem, self.per, self.n, self.base = eng, sem, per, 0, 0

    def start(self, done):
        self.base, self.n = done * self.per, 0

    def end(self):
        assert self.n == self.per, (self.n, self.per)

    def mark(self, ins):
        self.n += 1
        ins.then_inc(self.sem, 1)
        return self.n

    def wait(self, n=None):
        self.eng.wait_ge(self.sem, self.base + (self.n if n is None else n))

    def __call__(self, ins):
        self.mark(ins)
        self.wait()


def loop(eng, body, first=1, last=TILES):
    body(first)
    with eng.Fori(first + 1, last) as i:
        body(i)
    body(last)


def is_last(i):
    return isinstance(i, int) and i == TILES


class Scope:

    def __init__(self, nc):
        self.nc, self.ctx = nc, ExitStack()

    def __enter__(self):
        self.ctx.__enter__()
        return self

    def __exit__(self, *a):
        return self.ctx.__exit__(*a)

    def sb(self, name, shape, dt=F32):
        return self.ctx.enter_context(self.nc.sbuf_tensor(name, shape, dt))

    def ps(self, name, shape):
        return self.ctx.enter_context(self.nc.psum_tensor(name, shape, F32))

    def sem(self, name):
        return self.ctx.enter_context(self.nc.semaphore(name))

    def sems(self, name, n):
        return [self.sem(f"{name}{i}") for i in range(n)]

    def block(self):
        return self.ctx.enter_context(self.nc.Block())


def edges(nc, keep, src, dst, rel, norm, weight):
    with Scope(nc) as s:
        def room(n):
            size = CHUNKS * GROUP
            return keep.xnT[:].rearrange("p k n -> p (k n)")[:, n * size:(n + 1) * size]\
                .rearrange("p (c e) -> p c e", e=GROUP)
        raw = {k: room(n).bitcast(I32) for n, k in enumerate(("src", "rel", "dst"))}
        top = s.sb("e_top", [P, GROUP], I32)
        nrm, idx, dstf = room(3), room(4), room(5)
        topf = s.sb("e_topf", [P, GROUP])
        low = s.sb("e_low", [P, CHUNKS])
        high = s.sb("e_high", [P, CHUNKS])
        span = s.sb("e_span", [P, CHUNKS])
        wide = s.sb("e_wide", [P, 1])
        turned = s.ps("e_turned", [P, 2, GE, P])
        rows = s.ps("e_rows", [1, CHUNKS, P])
        count = s.ps("e_count", [1, 1])
        padded, loaded, ident_ready = s.sem("padded"), s.sem("loaded"), s.sem("ident_ready")
        ready, rows_ready, turned_sem, emptied = s.sem("ready"), s.sem("rows_ready"), s.sem("turned"), s.sem("emptied")
        steps = s.sem("dve_steps")
        block = s.block()
        named = {"src": src, "rel": rel, "dst": dst}

        def load(eng, out, a):
            eng.dma_start(out[:, 0:CHUNKS - 1, :],
                          a[0:(CHUNKS - 1) * P * GROUP].rearrange("(c g e) -> g c e", g=P, e=GROUP)).then_inc(loaded, 16)
            tail(eng, out[:, CHUNKS - 1, :], a)

        def tail(eng, out, a):
            g0, g1 = (CHUNKS - 1) * P, FULL_G
            eng.dma_start(out[0:g1 - g0, :], a[g0 * GROUP:g1 * GROUP].rearrange("(g e) -> g e", e=GROUP)).then_inc(loaded, 16)
            eng.dma_start(out[g1 - g0:g1 - g0 + 1, 0:REST_E], a[g1 * GROUP:E].rearrange("(g e) -> g e", g=1)).then_inc(loaded, 16)

        @block.sync
        def _(sp):
            sp.wait_ge(padded, 5)
            for k in ("dst", "src", "rel"):
                load(sp, raw[k], named[k])
            tail(sp, top, dst)
            load(sp, nrm, norm)
            for k in range(KC):
                sp.dma_start(keep.weight[:, k],
                             weight[:, k * P:(k + 1) * P, :].rearrange("r p o -> p r o")).then_inc(keep.w_loaded, 16)

        @block.gpsimd
        def _(pool):
            for k in ("src", "rel"):
                nc.gpsimd.memset(raw[k][:, CHUNKS - 1, :], 0).then_inc(padded, 1)
            nc.gpsimd.memset(raw["dst"][:, CHUNKS - 1, :], N - 1).then_inc(padded, 1)
            nc.gpsimd.memset(top[:], 0).then_inc(padded, 1)
            nc.gpsimd.memset(nrm[:, CHUNKS - 1, :], 0.0).then_inc(padded, 1)
            nc.gpsimd.memset(keep.ident[:], 0.0).then_inc(ident_ready, 1)
            pool.wait_ge(ident_ready, 1)
            nc.gpsimd.affine_select(out=keep.ident[:], in_=keep.ident[:], compare_op=ALU.not_equal, fill=1.0,
                                    base=0, pattern=[[-1, P]], channel_multiplier=1).then_inc(ident_ready, 1)
            nc.gpsimd.iota(keep.offsets[:], [[1, WIN]], base=0, channel_multiplier=0,
                           allow_small_or_imprecise_dtypes=True).then_inc(ident_ready, 1)
            nc.gpsimd.memset(keep.ones[:], 1.0).then_inc(ident_ready, 1)

        @block.vector
        def _(v):
            step = Chain(v, steps)
            v.wait_ge(loaded, 16 * 14)
            step.mark(nc.vector.tensor_copy(dstf[:], raw["dst"][:]))
            step.mark(nc.vector.tensor_copy(topf[:], top[:]))
            step.mark(nc.vector.tensor_scalar(idx[:], raw["src"][:], float(RELS), None, ALU.mult))
            step.wait()
            step.mark(nc.vector.tensor_tensor(idx[:], idx[:], raw["rel"][:], ALU.add))
            step.mark(nc.vector.tensor_reduce(low[:], dstf[:], AX_X, ALU.min))
            step.mark(nc.vector.tensor_reduce(high[:, 0:CHUNKS - 1], dstf[:, 0:CHUNKS - 1, :], AX_X, ALU.max))
            step.mark(nc.vector.tensor_reduce(high[:, CHUNKS - 1:CHUNKS], topf[:], AX_X, ALU.max))
            step.wait()
            step.mark(nc.vector.tensor_tensor(span[:], high[:], low[:], ALU.subtract))
            for c in range(CHUNKS):
                step.mark(nc.vector.tensor_scalar(dstf[:, c, :], dstf[:, c, :], low[:, c:c + 1], None, ALU.subtract))
            step.wait()
            step(nc.vector.tensor_scalar(span[:], span[:], float(WIN), None, ALU.is_ge))
            nc.vector.tensor_reduce(wide[:], span[:], AX_X, ALU.add).then_inc(ready, 1)
            v.wait_ge(rows_ready, 1)
            nc.vector.tensor_copy(keep.base[:], rows[:].rearrange("o c g -> o (c g)")[:, 0:GROUPS]).then_inc(emptied, 1)
            nc.vector.tensor_copy(keep.far[:], count[:]).then_inc(emptied, 1)
            n = 0
            for out in (keep.winT, keep.idxT, keep.nrmT):
                for c in range(CHUNKS):
                    g = min(P, GROUPS - c * P)
                    v.wait_ge(turned_sem, n + 1)
                    nc.vector.tensor_copy(out[:, c * P * GE:(c * P + g) * GE].rearrange("p (g j) -> p j g", j=GE),
                                          turned[:, n % 2, :, 0:g]).then_inc(emptied, 1)
                    n += 1

        @block.tensor
        def _(pe):
            pe.wait_ge(ready, 1)
            pe.wait_ge(ident_ready, 4)
            for c in range(CHUNKS):
                nc.tensor.matmul(rows[:, c, :], low[:, c:c + 1], keep.ident[:], start=True, stop=True)
            nc.tensor.matmul(count[:], wide[:], keep.ones[:, 0:1], start=True, stop=True).then_inc(rows_ready, 1)
            n = 0
            for a in (dstf, idx, nrm):
                for c in range(CHUNKS):
                    after(pe, emptied, n + 1 if n >= 2 else 0)
                    for j in range(GE):
                        last = nc.tensor.transpose(turned[:, n % 2, j, :], a[:, c, j * P:(j + 1) * P], keep.ident[:])
                    last.then_inc(turned_sem, 1)
                    n += 1


LB = 7
assert TILES % LB == 0


CH = 10
RPC = RELS // CH
BANKS = 5


def relations(nc, keep, x, table):
    with Scope(nc) as s:
        xs = s.sb("r_x", [P, 2, C])
        sq = s.sb("r_sq", [P, C])
        total, var, sd, inv = (s.sb(f"r_{n}", [P, 1]) for n in ("total", "var", "sd", "inv"))
        xT = s.sb("r_xT", [P, 2, 2, KC, P], F32R)
        w_high, w_low = (s.sb(f"r_w_{n}", [P, KC, RELS, C], F32R) for n in ("high", "low"))
        rows = keep.aggT[:].rearrange("p k n -> p (k n)")[:, 0:2 * RELS * C].rearrange("p (b c) -> p b c", b=2)
        acc = s.ps("r_acc", [P, BANKS, 512])
        turned = s.ps("r_turned", [P, 512])
        loaded, stored, emptied = s.sems("x_loaded", 2), s.sems("stored", 2), s.sems("emptied", 2)
        (high_ready, w_ready, xc_ready, squared, var_ready, sd_ready, xn_ready, turned_sem, xT_high, xT_low,
         summed, steps) = (s.sem(n) for n in (
             "w_high_ready", "w_ready", "xc_ready", "squared", "var_ready", "sd_ready", "xn_ready", "turned",
             "xT_high", "xT_low", "summed", "dve_steps"))
        block = s.block()
        out = table.rearrange("(n r) c -> n (r c)", r=RELS)
        half = CH // 2
        step = Chain(nc.vector, steps, 7)

        def pairs(eng, body):
            body(1, 0, 1)
            body(2, 1, 1)
            with eng.Fori(1, TILES // 2) as i:
                for k in range(2):
                    body(2 * i + (k + 1), k, i + 1)
            body(TILES, 0, TILES // 2 + 1)

        def piece(a, c):
            return a[:, :, c * RPC:(c + 1) * RPC, :]

        def empty(eng, copy, n, k, i, c):
            eng.wait_ge(summed, CH * (n - 1) + (c + 1))
            if c < 2:
                after(eng, stored[k], (i - 1) * 16)
            copy(rows[:, k, c * 512:(c + 1) * 512], acc[:, c % BANKS, :]).then_inc(emptied[c % 2], 1)

        @block.gpsimd
        def _(pool):
            def body(n, k, i):
                after(pool, turned_sem, n - 2)
                if is_last(n):
                    pool.dma_start(xs[0:LAST, k, :], x[(n - 1) * P:N, :]).then_inc(loaded[k], 16)
                else:
                    pool.dma_start(xs[:, k, :], x[bass.ds((n - 1) * P, P), :]).then_inc(loaded[k], 16)
            pairs(pool, body)

        @block.sync
        def _(sp):
            def body(n, k, i):
                sp.wait_ge(emptied[0], half * n)
                sp.wait_ge(emptied[1], half * n)
                sp.dma_start(out[bass.ds((n - 1) * P, P), :], rows[:, k, :]).then_inc(stored[k], 16)
            pairs(sp, body)
            sp.wait_ge(stored[0], (TILES // 2 + 1) * 16)
            sp.wait_ge(stored[1], (TILES // 2) * 16)

        @block.scalar
        def _(act):
            def square(n, k):
                act.wait_ge(xc_ready, n)
                nc.scalar.activation(sq[:], xs[:, k, :], ACT.Square).then_inc(squared, 1)

            def root(n):
                act.wait_ge(var_ready, n)
                nc.scalar.activation(sd[:], var[:], ACT.Sqrt).then_inc(sd_ready, 1)

            def split(n, k):
                act.wait_ge(turned_sem, n)
                after(act, summed, CH * (n - 2))
                nc.scalar.copy(xT[:, k, 0].rearrange("p c n -> p (c n)"), turned[:, 0:C]).then_inc(xT_high, 1)

            act.wait_ge(keep.w_loaded, 16 * KC)
            square(1, 0)
            root(1)
            for c in range(CH):
                nc.scalar.copy(piece(w_high, c), piece(keep.weight, c)).then_inc(high_ready, 1)
            split(1, 0)

            def body(n, k, i):
                for c in range(0, CH, 2):
                    empty(act, nc.scalar.copy, n, k, i, c)
                    if is_last(n):
                        continue
                    if c == 2:
                        square(n + 1, 1 - k)
                    if c == 4:
                        root(n + 1)
                    if c == 6:
                        split(n + 1, 1 - k)
            pairs(act, body)

        @block.vector
        def _(v):
            def centre(n, k, i):
                v.wait_ge(loaded[k], 16 * i)
                step.start(n - 1)
                step(nc.vector.tensor_reduce(total[:], xs[:, k, :], AX_X, ALU.add))
                step(nc.vector.tensor_scalar(total[:], total[:], 1.0 / C, None, ALU.mult))
                nc.vector.tensor_scalar(xs[:, k, :], xs[:, k, :], total[:], None, ALU.subtract).then_inc(xc_ready, 1)

            def normalise(n, k):
                v.wait_ge(squared, n)
                step(nc.vector.tensor_reduce(var[:], sq[:], AX_X, ALU.add))
                nc.vector.tensor_scalar(var[:], var[:], 1.0 / C, LN_EPS, ALU.mult, ALU.add).then_inc(var_ready, 1)
                v.wait_ge(sd_ready, n)
                root_inverse(nc, step, inv, sd, var)
                step.end()
                nc.vector.tensor_scalar(xs[:, k, :], xs[:, k, :], inv[:], 2.0, ALU.mult, ALU.mult).then_inc(xn_ready, 1)

            def split(n, k):
                v.wait_ge(xT_high, n)
                nc.vector.tensor_scalar(keep.xnT[:, :, bass.ds((n - 1) * P, P)],
                                        turned[:, 0:C].rearrange("p (k n) -> p k n", k=KC), 1.0, None,
                                        ALU.mult)
                nc.vector.tensor_tensor(xT[:, k, 1], turned[:, 0:C].rearrange("p (k n) -> p k n", k=KC),
                                        xT[:, k, 0].bitcast(F32), ALU.subtract).then_inc(xT_low, 1)

            centre(1, 0, 1)
            normalise(1, 0)
            v.wait_ge(keep.w_loaded, 16 * KC)
            for c in range(CH):
                v.wait_ge(high_ready, c + 1)
                nc.vector.tensor_tensor(piece(w_low, c), piece(keep.weight, c), piece(w_high, c).bitcast(F32),
                                        ALU.subtract).then_inc(w_ready, 1)
            split(1, 0)

            def body(n, k, i):
                for c in range(1, CH, 2):
                    empty(v, nc.vector.tensor_copy, n, k, i, c)
                    if is_last(n):
                        continue
                    if c == 1:
                        centre(n + 1, 1 - k, i + k)
                    if c == 3:
                        normalise(n + 1, 1 - k)
                    if c == 7:
                        split(n + 1, 1 - k)
            pairs(v, body)

        @block.tensor
        def _(pe):
            def turn(n, k):
                pe.wait_ge(xn_ready, n)
                after(pe, xT_low, n - 1)
                for c in range(KC):
                    last = nc.tensor.transpose(turned[:, c * P:(c + 1) * P], xs[:, k, c * P:(c + 1) * P], keep.ident[:])
                last.then_inc(turned_sem, 1)

            def body(n, k, i):
                pe.wait_ge(xT_high, n)
                pe.wait_ge(xT_low, n)
                for c in range(CH):
                    if isinstance(n, int) and n == 1:
                        pe.wait_ge(w_ready, c + 1)
                    old = (c - BANKS) % CH
                    after(pe, emptied[old % 2], half * (n - 2 if c < BANKS else n - 1) + (old // 2 + 1))
                    products = [(a, w, kc) for a, w in ((0, w_high), (0, w_low), (1, w_high))
                                for kc in range(KC)]
                    for m, (a, w, kc) in enumerate(products):
                        last = nc.tensor.matmul(acc[:, c % BANKS, :], xT[:, k, a, kc, :],
                                                w[:, kc, c * RPC:(c + 1) * RPC, :].rearrange("p r o -> p (r o)"),
                                                start=(m == 0), stop=(m == len(products) - 1))
                    last.then_inc(summed, 1)
                    if c == 6 and not is_last(n):
                        turn(n + 1, 1 - k)
            turn(1, 0)
            pairs(pe, body)


class Gather:

    def __init__(self, nc, s, keep, table, first, tag, counted=0):
        self.nc, self.keep, self.table, self.first = nc, keep, table, first
        self.counted = counted
        k = f"g_{tag}"
        self.rows = s.sb(f"{k}_rows", [P, GPT, GE, C])
        self.where = s.sb(f"{k}_where", [P, GPT, GE], I32)
        self.hot = s.sb(f"{k}_hot", [P, GPT, GE, WIN])
        self.node_regs = [nc.vector.alloc_register(f"{k}_node{j}") for j in range(GPT)]
        self.sum = s.ps(f"{k}_sum", [P, 2, 512])
        self.where_ready, self.pool_go = s.sem("where_ready"), s.sem("pool_go")
        self.equal_ready = s.sem("equal_ready")
        self.gathered = s.sems("gathered", GPT)
        self.hot_ready = s.sem("hot_ready")
        self.summed = s.sem("summed")
        self.added = s.sem("added")

    def cols(self, at, j=0, n=GPT * GE):
        return bass.ds((at - 1) * (GPT * GE) + (self.first + j) * GE, n)

    def pool_fetch(self, pool, i, at=None):
        at = i if at is None else at
        for j in range(GPT):
            after(pool, self.summed, GPT * (i - 2) + (j + 1))
            pool.sem_inc(self.pool_go, 1)
            self.nc.gpsimd.tensor_copy(self.where[:, j, :], self.keep.idxT[:, self.cols(at, j, GE)])\
                .then_inc(self.where_ready, 1)
            pool.wait_ge(self.where_ready, GPT * (i - 1) + (j + 1))
            pool.sem_inc(self.pool_go, 1)
            for t in range(GE):
                self.nc.gpsimd.indirect_dma_start(
                    self.rows[:, j, t, :], None, self.table,
                    bass.IndirectOffsetOnAxis(ap=self.where[:, j, t:t + 1], axis=0)).then_inc(self.gathered[j], 16)

    def vector_hot(self, v, i, at=None):
        at = i if at is None else at
        shape = [P, GPT * GE, WIN]
        hot = self.hot[:].rearrange("p g t w -> p (g t) w")

        def cols(a):
            return a[:, self.cols(at)].rearrange("p (c o) -> p c o", o=1).broadcast_to(shape)
        after(v, self.summed, GPT * (i - 1))
        self.nc.vector.tensor_tensor(hot, self.keep.offsets[:].rearrange("p (o w) -> p o w", o=1).broadcast_to(shape),
                                     cols(self.keep.winT), ALU.is_equal).then_inc(self.equal_ready, 1)
        v.wait_ge(self.equal_ready, i)
        self.nc.vector.tensor_tensor(hot, hot, cols(self.keep.nrmT), ALU.mult).then_inc(self.hot_ready, 1)
        v.load(self.node_regs, self.keep.base[0:1, bass.ds((at - 1) * GPT + self.first, GPT)])

    def tensor_sum(self, pe, i, j):
        pe.wait_ge(self.hot_ready, i)
        pe.wait_ge(self.gathered[j], (i - self.counted) * (16 * GE))
        after(pe, self.added, GPT * (i - 1) + (j - 1))
        for t in range(GE):
            for k in range(KC):
                last = self.nc.tensor.matmul(self.sum[:, j % 2, k * WIN:(k + 1) * WIN],
                                             self.rows[:, j, t, k * P:(k + 1) * P], self.hot[:, j, t, :],
                                             start=(t == 0 and k == 0), stop=(t == GE - 1), skip_group_check=True)
        last.then_inc(self.summed, 1)

    def vector_add(self, v, i, j):
        v.wait_ge(self.summed, GPT * (i - 1) + (j + 1))
        after(v, self.added, GPT * (i - 1) + j)
        node = v.snap(self.node_regs[j], min_val=0, max_val=N)
        self.nc.vector.tensor_tensor(self.keep.aggT[:, :, bass.ds(node, WIN)], self.keep.aggT[:, :, bass.ds(node, WIN)],
                                     self.sum[:, j % 2, 0:KC * WIN].rearrange("p (k w) -> p k w", w=WIN),
                                     ALU.add).then_inc(self.added, 1)


def heads(a, n):
    return a.rearrange("p (h d) -> p h d", d=n)


HP = HEADS // 2
DV2 = 2 * DV
RES = 2 * D


def pair_features(nc, out, z, hp, ready):
    a = z[:, 2 * hp:2 * hp + 2, :]
    part = a.ap[0]
    shifted = bass.AP(a.tensor, a.offset, [part, (DW, 2), (1, SHIFTS), (1, D)])
    plain = bass.AP(a.tensor, a.offset, [part, (DW, 2), (0, SHIFTS), (1, D)])
    n = 2 * SHIFTS * D
    nc.vector.tensor_tensor(out[:, hp * n:(hp + 1) * n].rearrange("p (h s d) -> p h s d", s=SHIFTS, d=D),
                            plain, shifted, ALU.mult).then_inc(ready, 1)


def rest_features(nc, out, z, ready):
    nc.vector.tensor_tensor(out[:, :, 0:D], z[:, :, 0:D], z[:, :, SHIFTS:DW], ALU.mult).then_inc(ready, 1)
    nc.vector.tensor_copy(out[:, :, D:RES], z[:, :, 0:D]).then_inc(ready, 1)


def root_inverse(nc, step, inv, sd, ss):
    step(nc.vector.reciprocal(inv[:], sd[:]))
    step(nc.vector.tensor_tensor(inv[:], inv[:], ss[:], ALU.mult))
    step(nc.vector.tensor_tensor(inv[:], inv[:], sd[:], ALU.add))
    step(nc.vector.reciprocal(inv[:], inv[:]))


def moments(nc, keep, table):
    with Scope(nc) as s:
        g = Gather(nc, s, keep, table, 0, "keys")
        xT = s.sb("m_xT", [P, KC, P])
        kv = s.sb("m_kv", [P, 2 * C])
        sq = s.sb("m_sq", [P, C])
        ss, sd, inv = (s.sb(f"m_{n}", [P, HEADS]) for n in ("ss", "sd", "inv"))
        kd = s.sb("m_kd", [P, HEADS, DW])
        kk = s.sb("m_kk", [P, PAIRS])
        kr = s.sb("m_kr", [P, HEADS, RES + 1])
        v1 = s.sb("m_v1", [P, HEADS, DV])
        proj = s.ps("m_proj", [P, 512])
        acc = s.ps("m_acc", [P, HP + 1, 512])
        x_ready, projected, kv_ready, squared = s.sem("x_ready"), s.sem("projected"), s.sem("kv_ready"), s.sem("squared")
        ss_ready, sd_ready, feats_ready, v_ready, multiplied = (s.sem(n) for n in (
            "ss_ready", "sd_ready", "feats_ready", "v_ready", "multiplied"))
        pairsT = s.sb("m_pairsT", [P, HP, 512])
        restT = s.sb("m_restT", [P, HP, 2 * RES])
        oneT = s.sb("m_oneT", [P, HP])
        zeroed, steps, kd_ready, emptied, turned = (s.sem(n) for n in ("zeroed", "dve_steps", "kd_ready", "emptied", "turned"))
        block = s.block()

        @block.gpsimd
        def _(pool):
            nc.gpsimd.memset(v1[:], 1.0).then_inc(zeroed, 1)
            nc.gpsimd.memset(kr[:], 1.0).then_inc(zeroed, 1)
            for a in (pairsT, restT, oneT, keep.mom, keep.momw):
                nc.gpsimd.memset(a[:], 0.0).then_inc(zeroed, 1)
            loop(pool, lambda i: g.pool_fetch(pool, i))

        @block.scalar
        def _(act):
            def tile(t):
                act.wait_ge(kv_ready, t)
                nc.scalar.activation(sq[:], kv[:, 0:C], ACT.Square).then_inc(squared, 1)
                act.wait_ge(ss_ready, t)
                nc.scalar.activation(sd[:], ss[:], ACT.Sqrt).then_inc(sd_ready, 1)
                for hp in range(HP):
                    after(act, multiplied, HP * (t - 2) + (hp + 1) if not isinstance(t, int) or t > 1 else 0)
                    nc.scalar.copy(v1[:, 2 * hp:2 * hp + 2, 1:DV],
                                   heads(kv[:, C + 2 * hp * D:C + (2 * hp + 2) * D], D)).then_inc(v_ready, 1)
            act.wait_ge(zeroed, 8)
            loop(act, tile)

        @block.vector
        def _(v):
            step = Chain(v, steps, 5)

            def fix(t):
                after(v, projected, t - 1)
                nc.vector.tensor_scalar(xT[:], keep.xnT[:, :, bass.ds((t - 1) * P, P)], 1.0, None,
                                        ALU.mult).then_inc(x_ready, 1)

            def norm(t):
                step.start(t - 1)
                v.wait_ge(projected, t)
                after(v, v_ready, HP * (t - 1))
                nc.vector.tensor_tensor(kv[:], proj[:], keep.bias_qkv[:, C:3 * C], ALU.add).then_inc(kv_ready, 1)
                v.wait_ge(squared, t)
                step(nc.vector.tensor_reduce(ss[:], heads(sq[:], D), AX_X, ALU.add))
                nc.vector.tensor_scalar(ss[:], ss[:], ROOT_EPS * ROOT_EPS, None, ALU.max).then_inc(ss_ready, 1)
                v.wait_ge(sd_ready, t)
                root_inverse(nc, step, inv, sd, ss)
                scaled = inv[:].rearrange("p (h o) -> p h o", o=1)
                for a, n in ((0, D), (D, SHIFTS)):
                    last = nc.vector.scalar_tensor_tensor(out=kd[:, :, a:a + n], in0=heads(kv[:, 0:C], D)[:, :, 0:n],
                                                          scalar=2.0 * SC, in1=scaled.broadcast_to([P, HEADS, n]),
                                                          op0=ALU.mult, op1=ALU.mult)
                    last.then_inc(kd_ready, 1)
                step.end()

            def part(hp):
                pair_features(nc, kk, kd, hp, feats_ready)
                h = slice(2 * hp, 2 * hp + 2)
                rest_features(nc, kr[:, h, :], kd[:, h, :], feats_ready)

            nc.vector.memset(keep.aggT[:], 0.0).then_inc(zeroed, 1)
            v.wait_ge(zeroed, 8)
            fix(1)
            norm(1)
            v.wait_ge(kd_ready, 2)
            for hp in range(HP):
                part(hp)

            def body(i):
                if not is_last(i):
                    fix(i + 1)
                g.vector_hot(v, i)
                if not is_last(i):
                    norm(i + 1)
                    v.wait_ge(kd_ready, 2 * (i + 1))
                for hp in range(HP):
                    if not is_last(i):
                        v.wait_ge(multiplied, HP * (i - 1) + (hp + 1))
                        part(hp)
                    g.vector_add(v, i, hp)
            loop(v, body)

            v.wait_ge(multiplied, HP * TILES)
            for h2 in range(2):
                rows = slice(64 * h2, 64 * h2 + DV)
                rest = acc[rows, HP, 0:HP * (RES + 1)].rearrange("p (a f) -> p a f", f=RES + 1)
                nc.vector.tensor_copy(pairsT[rows], acc[rows, 0:HP, :]).then_inc(emptied, 1)
                nc.vector.tensor_copy(restT[rows, :, h2 * RES:(h2 + 1) * RES], rest[:, :, 0:RES]).then_inc(emptied, 1)
                nc.vector.tensor_copy(oneT[rows, :], rest[:, :, RES]).then_inc(emptied, 1)
            v.wait_ge(turned, 1)
            for h2 in range(2):
                src = slice(64 * h2, 64 * h2 + DV)
                dst = slice(DV * h2, DV * h2 + DV)
                for hp in range(HP):
                    for t in range(TPH):
                        nc.vector.tensor_scalar(keep.mom[:, (2 * hp + h2) * TPH + t, dst],
                                                acc[:, hp, t * P:(t + 1) * P][:, src],
                                                keep.factor[:, min(t, 1):min(t, 1) + 1], None, ALU.mult)
                nc.vector.tensor_scalar(keep.momw[:, :, dst], acc[:, HP, :].rearrange("p (a c) -> p a c", c=P)[:, :, src],
                                        keep.factor[:, 2:3], None, ALU.mult)
            nc.vector.tensor_scalar(keep.mom1[:].rearrange("o (h e) -> o h e", e=DV),
                                    proj[0:1, :].rearrange("o (h c) -> o h c", c=64)[:, :, 0:DV], SC ** 4 / N, None, ALU.mult)

        @block.tensor
        def _(pe):
            def project(t):
                pe.wait_ge(x_ready, t)
                after(pe, kv_ready, t - 1)
                for k in range(KC):
                    last = nc.tensor.matmul(proj[:], xT[:, k, :], keep.wT[:, k, C:3 * C], start=(k == 0), stop=(k == KC - 1))
                last.then_inc(projected, 1)

            def multiply(i, hp):
                first = isinstance(i, int) and i == 1
                m = LAST if is_last(i) else P
                pe.wait_ge(feats_ready, 3 * HP * (i - 1) + 3 * (hp + 1))
                pe.wait_ge(v_ready, HP * (i - 1) + (hp + 1))
                for h in (2 * hp, 2 * hp + 1):
                    p0 = 64 * (h % 2)
                    n = SHIFTS * D
                    last = nc.tensor.matmul(acc[p0:p0 + DV, hp, :], v1[0:m, h, :], kk[0:m, h * n:(h + 1) * n],
                                            start=first, stop=is_last(i), skip_group_check=True)
                    last = nc.tensor.matmul(acc[p0:p0 + DV, HP, hp * (RES + 1):(hp + 1) * (RES + 1)],
                                            v1[0:m, h, :], kr[0:m, h, :], start=(first and hp == 0),
                                            stop=is_last(i), skip_group_check=True)
                last.then_inc(multiplied, 1)

            pe.wait_ge(zeroed, 8)
            project(1)

            def body(i):
                for hp in range(HP):
                    multiply(i, hp)
                    if hp == 0 and not is_last(i):
                        project(i + 1)
                    g.tensor_sum(pe, i, hp)
            loop(pe, body)
            pe.wait_ge(emptied, 6)
            for hp in range(HP):
                for t in range(TPH):
                    nc.tensor.transpose(acc[:, hp, t * P:(t + 1) * P], pairsT[:, hp, t * P:(t + 1) * P], keep.ident[:])
                nc.tensor.transpose(acc[:, HP, hp * P:(hp + 1) * P], restT[:, hp, :], keep.ident[:])
                last = nc.tensor.transpose(proj[0:1, hp * P:(hp + 1) * P], oneT[:, hp:hp + 1], keep.ident[:])
            last.then_inc(turned, 1)


FB = 4
FCH = FT // FB
RING = 3
assert FT % FB == 0 and TPH == FB


def readout(nc, keep, table, x, x1):
    with Scope(nc) as s:
        g = Gather(nc, s, keep, table, GPT * TILES, "queries")
        xT = s.sb("q_xT", [P, KC, P])
        xs = s.sb("q_x", [P, C])
        q = s.sb("q_q", [P, C])
        sq = s.sb("q_sq", [P, C])
        ss, sd, inv, ry = (s.sb(f"q_{n}", [P, HEADS]) for n in ("ss", "sd", "inv", "ry"))
        qd = s.sb("q_qd", [P, HEADS, DW])
        qq = s.sb("q_qq", [P, PAIRS])
        qr = s.sb("q_qr", [P, HEADS, RES])
        fT = s.sb("q_fT", [P, RING, FB, P])
        o = s.sb("q_o", [P, C])
        oT = s.sb("q_oT", [P, KC, P])
        res = s.sb("q_res", [P, C])
        proj = s.ps("q_proj", [P, 512])
        turned = s.ps("q_turned", [P, 2, FB, P])
        y = s.ps("q_y", [P, 512])
        oTp = s.ps("q_oTp", [P, 512])
        out = s.ps("q_out", [P, 512])
        (x_ready, projected, q_ready, squared, ss_ready, sd_ready, qd_ready, feats_ready, rest_ready, turned_sem, copied,
         multiplied, ry_ready, o_ready, o_turned, oT_ready, out_ready, biased, res_ready, x_loaded, stored, steps) = (
            s.sem(n) for n in (
                "x_ready", "projected", "q_ready", "squared", "ss_ready", "sd_ready", "qd_ready", "feats_ready",
                "rest_ready", "turned", "copied", "multiplied", "ry_ready", "o_ready", "o_turned", "oT_ready",
                "out_ready", "biased", "res_ready", "x_loaded", "stored", "dve_steps"))
        block = s.block()

        def is_first(i):
            return isinstance(i, int) and i == 1

        @block.sync
        def _(sp):
            def body(i):
                after(sp, res_ready, i - 1)
                if is_last(i):
                    sp.dma_start(xs[0:LAST, :], x[(TILES - 1) * P:N, :]).then_inc(x_loaded, 16)
                    sp.wait_ge(res_ready, i)
                    sp.dma_start(x1[(TILES - 1) * P:NPAD, :], res[:]).then_inc(stored, 16)
                else:
                    sp.dma_start(xs[:], x[bass.ds((i - 1) * P, P), :]).then_inc(x_loaded, 16)
                    sp.wait_ge(res_ready, i)
                    sp.dma_start(x1[bass.ds((i - 1) * P, P), :], res[:]).then_inc(stored, 16)
            loop(sp, body)
            sp.wait_ge(stored, TILES * 16)

        @block.gpsimd
        def _(pool):
            loop(pool, lambda i: g.pool_fetch(pool, i))

        @block.scalar
        def _(act):
            def square(t):
                act.wait_ge(q_ready, t)
                nc.scalar.activation(sq[:], q[:], ACT.Square).then_inc(squared, 1)

            def root(t):
                act.wait_ge(ss_ready, t)
                nc.scalar.activation(sd[:], ss[:], ACT.Sqrt).then_inc(sd_ready, 1)

            def copy_output(i):
                act.wait_ge(o_turned, i)
                nc.scalar.copy(oT[:].rearrange("p k n -> p (k n)"), oTp[:, 0:C]).then_inc(oT_ready, 1)

            def copy(i, b):
                act.wait_ge(turned_sem, FCH * (i - 1) + (b + 1))
                after(act, multiplied, FCH * (i - 1) + (b + 1 - RING))
                nc.scalar.copy(fT[:, b % RING], turned[:, b % 2]).then_inc(copied, 1)

            def body(i):
                for b in range(FCH):
                    copy(i, b)
                    if b == 2 and not is_last(i):
                        square(i + 1)
                        root(i + 1)
                    if b == 3 and not is_first(i):
                        copy_output(i - 1)
            square(1)
            root(1)
            loop(act, body)
            copy_output(TILES)

        @block.vector
        def _(v):
            step = Chain(v, steps, 6)

            def fix(t):
                after(v, projected, t - 1)
                nc.vector.tensor_scalar(xT[:], keep.xnT[:, :, bass.ds((t - 1) * P, P)], 1.0, None,
                                        ALU.mult).then_inc(x_ready, 1)

            def norm(t):
                step.start(t - 1)
                v.wait_ge(projected, t)
                nc.vector.tensor_tensor(q[:], proj[:, 0:C], keep.bias_qkv[:, 0:C], ALU.add).then_inc(q_ready, 1)
                v.wait_ge(squared, t)
                step(nc.vector.tensor_reduce(ss[:], heads(sq[:], D), AX_X, ALU.add))
                nc.vector.tensor_scalar(ss[:], ss[:], SC * SC, ROOT_EPS * ROOT_EPS, ALU.mult, ALU.max).then_inc(ss_ready, 1)
                v.wait_ge(sd_ready, t)
                root_inverse(nc, step, inv, sd, ss)
                step(nc.vector.tensor_tensor(inv[:], inv[:], keep.temp[:], ALU.mult))
                scaled = inv[:].rearrange("p (h o) -> p h o", o=1)
                for a, n in ((0, D), (D, SHIFTS)):
                    nc.vector.tensor_tensor(qd[:, :, a:a + n], heads(q[:], D)[:, :, 0:n],
                                            scaled.broadcast_to([P, HEADS, n]), ALU.mult).then_inc(qd_ready, 1)
                step.end()

            def output(i):
                v.wait_ge(multiplied, FCH * i)
                yh = y[:, 0:HEADS * DV].rearrange("p (h e) -> p h e", e=DV)
                nc.vector.reciprocal(ry[:].rearrange("p (h o) -> p h o", o=1), yh[:, :, 0:1]).then_inc(ry_ready, 1)
                v.wait_ge(ry_ready, i)
                after(v, o_turned, i - 1)
                nc.vector.tensor_tensor(heads(o[:], D), yh[:, :, 1:DV],
                                        ry[:].rearrange("p (h o) -> p h o", o=1).broadcast_to([P, HEADS, D]),
                                        ALU.mult).then_inc(o_ready, 1)

            def add_up(i):
                v.wait_ge(x_loaded, i * 16)
                nc.vector.tensor_tensor(xs[:], xs[:], keep.bias_p[:], ALU.add).then_inc(biased, 1)
                v.wait_ge(biased, i)
                v.wait_ge(out_ready, i)
                after(v, stored, (i - 1) * 16)
                nc.vector.tensor_tensor(res[:], out[:, 0:C], xs[:], ALU.add).then_inc(res_ready, 1)

            fix(1)
            norm(1)
            v.wait_ge(qd_ready, 2)
            for hp in range(HP):
                pair_features(nc, qq, qd, hp, feats_ready)
            rest_features(nc, qr, qd, rest_ready)

            def body(i):
                if not is_last(i):
                    fix(i + 1)
                if not is_first(i):
                    output(i - 1)
                g.vector_hot(v, i)
                if not is_last(i):
                    norm(i + 1)
                    v.wait_ge(qd_ready, 2 * (i + 1))
                for hp in range(HP):
                    if not is_last(i):
                        v.wait_ge(turned_sem, FCH * (i - 1) + (2 * hp + 2))
                        pair_features(nc, qq, qd, hp, feats_ready)
                        if hp == HP - 1:
                            v.wait_ge(turned_sem, FCH * i)
                            rest_features(nc, qr, qd, rest_ready)
                    g.vector_add(v, i, hp)
                    if hp == 2 and not is_first(i):
                        add_up(i - 1)
            loop(v, body)
            output(TILES)
            add_up(TILES)

        @block.tensor
        def _(pe):
            def project(t):
                pe.wait_ge(x_ready, t)
                after(pe, q_ready, t - 1)
                for k in range(KC):
                    last = nc.tensor.matmul(proj[:, 0:C], xT[:, k, :], keep.wT[:, k, 0:C], start=(k == 0), stop=(k == KC - 1))
                last.then_inc(projected, 1)

            def turn(i, b):
                if b % 2 == 0 and b < FCH - 1:
                    pe.wait_ge(feats_ready, HP * (i - 1) + (b // 2 + 1))
                if b == FCH - 1:
                    pe.wait_ge(rest_ready, 2 * i)
                after(pe, copied, FCH * (i - 1) + max(b - 1, 0))
                for n in range(FB):
                    if b < FCH - 1:
                        a = qq[:, (b * FB + n) * P:(b * FB + n + 1) * P]
                    else:
                        a = qr[:, 2 * n:2 * n + 2, :].rearrange("p h f -> p (h f)")
                    last = nc.tensor.transpose(turned[:, b % 2, n, :], a, keep.ident[:])
                last.then_inc(turned_sem, 1)

            def multiply(i, b):
                pe.wait_ge(copied, FCH * (i - 1) + (b + 1))
                if b == 0:
                    after(pe, o_ready, i - 1)
                    nc.tensor.matmul(y[:, 0:HEADS * DV], keep.ones[0:1, :], keep.mom1[:], start=True, stop=False,
                                     skip_group_check=True)
                for n in range(FB):
                    hp = b // 2 if b < FCH - 1 else n
                    m = keep.mom[:, b * FB + n, :] if b < FCH - 1 else keep.momw[:, n, :]
                    last = nc.tensor.matmul(y[:, hp * DV2:(hp + 1) * DV2], fT[:, b % RING, n, :], m, start=False,
                                            stop=(b == FCH - 1), skip_group_check=True)
                last.then_inc(multiplied, 1)

            def turn_output(i):
                pe.wait_ge(o_ready, i)
                after(pe, oT_ready, i - 1)
                for k in range(KC):
                    last = nc.tensor.transpose(oTp[:, k * P:(k + 1) * P], o[:, k * P:(k + 1) * P], keep.ident[:])
                last.then_inc(o_turned, 1)

            def project_output(i):
                pe.wait_ge(oT_ready, i)
                after(pe, res_ready, i - 1)
                for k in range(KC):
                    last = nc.tensor.matmul(out[:, 0:C], oT[:, k, :], keep.wpT[:, k, :], start=(k == 0), stop=(k == KC - 1))
                last.then_inc(out_ready, 1)

            def body(i):
                turn(i, 0)
                turn(i, 1)
                if not is_last(i):
                    project(i + 1)
                turn(i, 2)
                multiply(i, 0)
                g.tensor_sum(pe, i, 0)
                turn(i, 3)
                if not is_first(i):
                    turn_output(i - 1)
                multiply(i, 1)
                turn(i, 4)
                multiply(i, 2)
                g.tensor_sum(pe, i, 1)
                turn(i, 5)
                multiply(i, 3)
                turn(i, 6)
                multiply(i, 4)
                if not is_first(i):
                    project_output(i - 1)
                g.tensor_sum(pe, i, 2)
                turn(i, 7)
                multiply(i, 5)
                turn(i, 8)
                multiply(i, 6)
                g.tensor_sum(pe, i, 3)
                multiply(i, 7)
                multiply(i, 8)
            project(1)
            loop(pe, body)
            turn_output(TILES)
            project_output(TILES)


def weights(nc, keep, wqkv, bqkv, wproj, bproj, temperature):
    with Scope(nc) as s:
        rows = 3 * C // P
        w = s.sb("w_qkv", [P, rows, C])
        wp = s.sb("w_proj", [P, KC, C])
        turned = s.ps("w_turned", [P, KC, 2, 512])
        loaded, turned_sem, factors = s.sem("loaded"), s.sem("turned"), s.sem("factors")
        block = s.block()

        @block.sync
        def _(sp):
            sp.dma_start(w[:], wqkv.rearrange("(r p) c -> p r c", p=P)).then_inc(loaded, 16)
            sp.dma_start(wp[:], wproj.rearrange("(r p) c -> p r c", p=P)).then_inc(loaded, 16)
            sp.dma_start(keep.bias_qkv[:], bqkv.partition_broadcast(P)).then_inc(loaded, 16)
            sp.dma_start(keep.bias_p[:], bproj.partition_broadcast(P)).then_inc(loaded, 16)
            sp.dma_start(keep.temp[:], temperature.rearrange("a h b c -> (a h b c)").partition_broadcast(P)).then_inc(loaded, 16)

        @block.tensor
        def _(pe):
            pe.wait_ge(loaded, 5 * 16)
            for k in range(KC):
                for r in range(rows):
                    nc.tensor.transpose(turned[:, k, r * P // 512, r * P % 512:r * P % 512 + P],
                                        w[:, r, k * P:(k + 1) * P], keep.ident[:])
                for r in range(KC):
                    last = nc.tensor.transpose(turned[:, k, 1, 256 + r * P:256 + (r + 1) * P],
                                               wp[:, r, k * P:(k + 1) * P], keep.ident[:])
            last.then_inc(turned_sem, 1)

        @block.vector
        def _(v):
            v.wait_ge(loaded, 5 * 16)
            nc.vector.tensor_scalar(keep.temp[:], keep.temp[:], 2.0 * SC * SC, None, ALU.mult)
            nc.vector.memset(keep.factor[:], 1.0 / N).then_inc(factors, 1)
            v.wait_ge(factors, 1)
            nc.vector.memset(keep.factor[0:D, 0:1], 0.5 / N)
            for h in range(2):
                nc.vector.memset(keep.factor[h * RES:h * RES + D, 2:3], 0.5 / N)
                nc.vector.memset(keep.factor[h * RES + D:(h + 1) * RES, 2:3], SC ** 2 / N)
            v.wait_ge(turned_sem, 1)
            for k in range(KC):
                t = turned[:, k].rearrange("p b n -> p (b n)")
                nc.vector.tensor_copy(keep.wT[:, k, :], t[:, 0:3 * C])
                nc.vector.tensor_copy(keep.wpT[:, k, :], t[:, 3 * C:4 * C])


def far_edges(nc, keep, table):
    with Scope(nc) as s:
        g = Gather(nc, s, keep, table, 0, "far", counted=1)
        shifted, shift_seen = s.sem("shifted"), s.sem("shift_seen")
        block = s.block()
        steps = GROUPS // GPT

        def rounds(eng, body, before=None):
            far = eng.value_load(keep.far[0:1, 0:1], min_val=0, max_val=GROUPS)
            with eng.If(far > 0):
                with eng.Fori(1, WINDOWS) as k:
                    if before:
                        before(k)
                    with eng.Fori(0, steps) as n:
                        body((k - 1) * steps + n + 2, n + 1)

        @block.gpsimd
        def _(pool):
            pool.sem_inc(g.where_ready, GPT)
            rounds(pool, lambda i, at: g.pool_fetch(pool, i, at))

        @block.vector
        def _(v):
            for sem, n in ((g.equal_ready, 1), (g.hot_ready, 1), (g.added, GPT)):
                v.sem_inc(sem, n)

            def shift(k):
                v.wait_ge(g.added, (k - 1) * (steps * GPT) + GPT)
                nc.vector.tensor_scalar(keep.winT[:], keep.winT[:], -float(WIN), None, ALU.add).then_inc(shifted, 1)
                nc.vector.tensor_scalar(keep.base[:], keep.base[:], float(WIN), float(N), ALU.add,
                                        ALU.min).then_inc(shifted, 1)
                v.wait_ge(shifted, 2 * k)
                v.sem_inc(shift_seen, 1)

            def body(i, at):
                g.vector_hot(v, i, at)
                for j in range(GPT):
                    g.vector_add(v, i, j)
            rounds(v, body, shift)

        @block.tensor
        def _(pe):
            pe.sem_inc(g.summed, GPT)

            def body(i, at):
                for j in range(GPT):
                    g.tensor_sum(pe, i, j)
            rounds(pe, body)


def second_norm(nc, keep, x1, rows):
    with Scope(nc) as s:
        agg = s.sb("n_agg", [P, KC, LB * P])
        x1s = s.sb("n_x1", [P, LB, C])
        both = s.sb("n_both", [P, LB, 2, C])
        xc = s.sb("n_xc", [P, LB, C])
        total, var, sd, inv = (s.sb(f"n_{n}", [P, LB]) for n in ("total", "var", "sd", "inv"))
        aggp = s.ps("n_aggp", [P, LB, KC, P])
        xnp = s.ps("n_xnp", [P, LB, KC, P])
        (agg_ready, agg_turned, x1_loaded, x2_ready, xc_ready, squared, var_ready, sd_ready, xn_ready, xn_turned, emptied,
         stored, steps) = (s.sem(n) for n in (
             "agg_ready", "agg_turned", "x1_loaded", "x2_ready", "xc_ready", "squared", "var_ready", "sd_ready",
             "xn_ready", "xn_turned", "emptied", "stored", "dve_steps"))
        block = s.block()
        batches = TILES // LB
        rows_flat = rows.rearrange("n two c -> n (two c)")

        def batch(i):
            return bass.ds((i - 1) * (LB * P), LB * P)

        @block.sync
        def _(sp):
            def body(i):
                after(sp, x2_ready, i - 1)
                sp.dma_start(x1s[:], x1[batch(i), :].rearrange("(t p) c -> p t c", p=P)).then_inc(x1_loaded, 16)
                sp.wait_ge(xn_ready, i)
                sp.dma_start(rows_flat[batch(i), :].rearrange("(t p) c -> p t c", p=P),
                             both[:].rearrange("p t two c -> p t (two c)")).then_inc(stored, 16)
            loop(sp, body, last=batches)
            sp.wait_ge(stored, 16 * batches)

        @block.scalar
        def _(act):
            def body(i):
                act.wait_ge(xc_ready, i)
                after(act, xn_turned, i - 1)
                nc.scalar.activation(both[:, :, 0, :], xc[:], ACT.Square).then_inc(squared, 1)
                act.wait_ge(var_ready, i)
                nc.scalar.activation(sd[:], var[:], ACT.Sqrt).then_inc(sd_ready, 1)
            loop(act, body, last=batches)

        @block.vector
        def _(v):
            step = Chain(v, steps, 7)

            def wide(a):
                return a[:].rearrange("p (t o) -> p t o", o=1).broadcast_to([P, LB, C])

            def relu(i):
                after(v, agg_turned, i - 1)
                nc.vector.tensor_scalar(agg[:], keep.aggT[:, :, batch(i)], 0.0, None, ALU.max).then_inc(agg_ready, 1)

            def body(i):
                step.start(i - 1)
                if isinstance(i, int) and i == 1:
                    relu(1)
                v.wait_ge(agg_turned, i)
                v.wait_ge(x1_loaded, 16 * i)
                after(v, stored, 16 * (i - 1))
                nc.vector.tensor_tensor(both[:, :, 1, :], x1s[:], aggp[:].rearrange("p t k n -> p t (k n)"),
                                        ALU.add).then_inc(x2_ready, 1)
                v.wait_ge(x2_ready, i)
                step(nc.vector.tensor_reduce(total[:], both[:, :, 1, :], AX_X, ALU.add))
                step(nc.vector.tensor_scalar(total[:], total[:], 1.0 / C, None, ALU.mult))
                nc.vector.tensor_tensor(xc[:], both[:, :, 1, :], wide(total), ALU.subtract).then_inc(xc_ready, 1)
                if not (isinstance(i, int) and i == batches):
                    relu(i + 1)
                v.wait_ge(squared, i)
                step(nc.vector.tensor_reduce(var[:], both[:, :, 0, :], AX_X, ALU.add))
                nc.vector.tensor_scalar(var[:], var[:], 1.0 / C, LN_EPS, ALU.mult, ALU.add).then_inc(var_ready, 1)
                v.wait_ge(sd_ready, i)
                root_inverse(nc, step, inv, sd, var)
                nc.vector.scalar_tensor_tensor(out=both[:, :, 0, :], in0=xc[:], scalar=2.0, in1=wide(inv), op0=ALU.mult,
                                               op1=ALU.mult).then_inc(xn_ready, 1)
                step.end()
                v.wait_ge(xn_turned, i)
                for k in range(KC):
                    nc.vector.tensor_scalar(keep.xnT[:, k, batch(i)].rearrange("p (t n) -> p t n", n=P),
                                            xnp[:, :, k, :], 1.0, None, ALU.mult).then_inc(emptied, 1)
            loop(v, body, last=batches)

        @block.tensor
        def _(pe):
            def turn_agg(i):
                pe.wait_ge(agg_ready, i)
                after(pe, x2_ready, i - 1)
                for t in range(LB):
                    for k in range(KC):
                        last = nc.tensor.transpose(aggp[:, t, k, :], agg[:, k, t * P:(t + 1) * P], keep.ident[:])
                last.then_inc(agg_turned, 1)

            def body(i):
                if isinstance(i, int) and i == 1:
                    turn_agg(1)
                if not (isinstance(i, int) and i == batches):
                    turn_agg(i + 1)
                pe.wait_ge(xn_ready, i)
                after(pe, emptied, KC * (i - 1))
                for t in range(LB):
                    for k in range(KC):
                        last = nc.tensor.transpose(xnp[:, t, k, :], both[:, t, 0, k * P:(k + 1) * P], keep.ident[:])
                last.then_inc(xn_turned, 1)
            loop(pe, body, last=batches)


SLOTS = (N + EXP * (P - 1)) // P
REGION = (TILES + 1) * P
DEEP, LEAD = 4, 2
assert SLOTS % DEEP == 0


def choose(nc, keep, Wd, W1, b1, Wg, bg, bd, order):
    with Scope(nc) as s:
        wg = s.sb("c_wg", [P, HC, EXP])
        b1r = s.sb("c_b1r", [HC, P])
        bgb = s.sb("c_bg", [P, EXP])
        h = s.sb("c_h", [P, 2, LB * P])
        logit = s.sb("c_logit", [P, TILES, EXP])
        prob = s.sb("c_prob", [P, TILES, EXP])
        score = s.sb("c_score", [P, TILES, EXP])
        sel = s.sb("c_sel", [P, TILES, EXP])
        upto = s.sb("c_upto", [P, 2, TILES, EXP])
        a1, a2 = s.sb("c_a1", [P, TILES]), s.sb("c_a2", [P, TILES])
        first, start = s.sb("c_first", [P, EXP]), s.sb("c_start", [P, EXP])
        valid = s.sb("c_valid", [P, TILES])
        before = s.sb("c_before", [P, P])
        where = s.sb("c_where", [P, TILES], I32)
        slot = s.sb("c_slot", [P, LB], I32)
        entry = s.sb("c_entry", [P, TILES, 2])
        held = s.sb("c_held", [P, LB, 2])
        blank = s.sb("c_blank", [P, (EXP + 1) * REGION // P, 2])
        hundreds = s.sb("c_hundreds", [1, SLOTS])
        full = s.sb("c_full", [1, EXP, TILES])
        tiles, ends, gap = s.sb("c_tiles", [1, EXP]), s.sb("c_ends", [1, 2, EXP]), s.sb("c_gap", [1, EXP])
        past, pgap = s.sb("c_past", [1, SLOTS, EXP]), s.sb("c_pgap", [1, SLOTS, EXP])
        o1, o2 = s.sb("c_o1", [1, SLOTS]), s.sb("c_o2", [1, SLOTS])
        hp = s.ps("c_hp", [P, 2, 2, 512])
        lg = s.ps("c_lg", [P, 512])
        ranks = s.ps("c_ranks", [P, 512])
        counts = s.ps("c_counts", [P, 512])
        b1p = s.ps("c_b1p", [P, 512])
        half = LB * P // 2
        (loaded, b1_turned, consts, h_summed, h_ready, gated, logit_ready, exps, sel_ready, counted, placed, blanked,
         slot_ready, scattered, pool_go, steps, shifted) = (s.sem(n) for n in (
             "loaded", "b1_turned", "consts", "h_summed", "h_ready", "gated", "logit_ready", "exps", "sel_ready",
             "counted", "placed", "blanked", "slot_ready", "scattered", "pool_go", "dve_steps", "shifted"))
        block = s.block()
        batches = TILES // LB
        n_consts = 9

        @block.sync
        def _(sp):
            for dst, src in ((keep.w1[:], W1.rearrange("(k p) h -> p k h", p=P)),
                             (wg[:], Wg.rearrange("(c p) e -> p c e", p=P)),
                             (b1r[:], b1.rearrange("(c p) -> c p", p=P)), (bgb[:], bg.partition_broadcast(P))):
                sp.dma_start(dst, src).then_inc(loaded, 16)
            sp.wait_ge(consts, n_consts)
            sp.dma_start(order.rearrange("(p r) two -> p r two", p=P), blank[:]).then_inc(blanked, 16)
            for c in range(HC):
                sp.dma_start(keep.wd[:, c].rearrange("p (e o) -> p e o", o=C), Wd[:, c * P:(c + 1) * P, :].rearrange("e p o -> p e o")).then_inc(keep.wd_loaded, 16)
            sp.dma_start(keep.bd[:], bd.rearrange("e c -> (e c)").partition_broadcast(P)).then_inc(keep.wd_loaded, 16)
            sp.wait_ge(blanked, 16)

        @block.gpsimd
        def _(pool):
            nc.gpsimd.memset(blank[:], float(N)).then_inc(consts, 1)
            nc.gpsimd.memset(valid[:], 1.0).then_inc(consts, 1)
            nc.gpsimd.memset(before[:], 1.0).then_inc(consts, 1)
            nc.gpsimd.iota(entry[:, :, 0], [[P, TILES]], base=0, channel_multiplier=1,
                           allow_small_or_imprecise_dtypes=True).then_inc(consts, 1)
            nc.gpsimd.iota(hundreds[:], [[P, SLOTS]], base=0, channel_multiplier=0,
                           allow_small_or_imprecise_dtypes=True).then_inc(consts, 1)
            nc.gpsimd.iota(first[:], [[-1, EXP]], base=EXP, channel_multiplier=0,
                           allow_small_or_imprecise_dtypes=True).then_inc(consts, 1)
            nc.gpsimd.iota(start[:], [[REGION, EXP]], base=0, channel_multiplier=0,
                           allow_small_or_imprecise_dtypes=True).then_inc(consts, 1)
            pool.wait_ge(consts, n_consts - 2)
            nc.gpsimd.affine_select(out=valid[:, TILES - 1:TILES], in_=valid[:, TILES - 1:TILES], compare_op=ALU.is_ge,
                                    fill=0.0, base=LAST - 1, pattern=[[0, 1]], channel_multiplier=-1).then_inc(consts, 1)
            nc.gpsimd.affine_select(out=before[:], in_=before[:], compare_op=ALU.is_ge, fill=0.0, base=-1,
                                    pattern=[[1, P]], channel_multiplier=-1).then_inc(consts, 1)
            pool.wait_ge(placed, 1)
            pool.wait_ge(blanked, 16)

            def scatter(i):
                after(pool, scattered, 16 * LB * (i - 1))
                pool.sem_inc(pool_go, 1)
                nc.gpsimd.tensor_copy(slot[:], where[:, bass.ds((i - 1) * LB, LB)]).then_inc(slot_ready, 1)
                nc.gpsimd.tensor_copy(held[:], entry[:, bass.ds((i - 1) * LB, LB), :]).then_inc(slot_ready, 1)
                pool.wait_ge(slot_ready, 2 * i)
                pool.sem_inc(pool_go, 1)
                for t in range(LB):
                    m = LAST if isinstance(i, int) and i == batches and t == LB - 1 else P
                    nc.gpsimd.indirect_dma_start(order, bass.IndirectOffsetOnAxis(ap=slot[0:m, t:t + 1], axis=0),
                                                 held[0:m, t, :], None).then_inc(scattered, 16)
            loop(pool, scatter, last=batches)
            pool.wait_ge(scattered, 16 * TILES)

        @block.scalar
        def _(act):
            act.wait_ge(b1_turned, 1)
            nc.scalar.copy(keep.b1T[:], b1p[:, 0:HC]).then_inc(keep.b1_ready, 1)
            act.wait_ge(keep.b1_ready, 1)

            def body(i):
                for c in range(HC):
                    for q in range(2):
                        act.wait_ge(h_summed, 2 * HC * (i - 1) + (2 * c + q + 1))
                        if q == 0:
                            after(act, gated, HC * (i - 1) + (c - 1))
                        nc.scalar.activation(h[:, c % 2, q * half:(q + 1) * half], hp[:, c % 2, q, 0:half], ACT.Gelu,
                                             bias=keep.b1T[:, c:c + 1]).then_inc(h_ready, 1)
            loop(act, body, last=batches)
            act.wait_ge(shifted, 1)
            nc.scalar.activation(prob[:], logit[:], ACT.Exp).then_inc(exps, 1)

        @block.vector
        def _(v):
            v.wait_ge(loaded, 64)

            def body(i):
                v.wait_ge(gated, HC * i)
                shape = [P, LB, EXP]
                nc.vector.tensor_tensor(logit[:, bass.ds((i - 1) * LB, LB), :],
                                        lg[:, 0:LB * EXP].rearrange("p (t e) -> p t e", e=EXP),
                                        bgb[:].rearrange("p (o e) -> p o e", o=1).broadcast_to(shape),
                                        ALU.add).then_inc(logit_ready, 1)
            loop(v, body, last=batches)
            step = Chain(v, steps)
            shape = [P, TILES, EXP]

            def per_tile(a):
                return a[:].rearrange("p (t o) -> p t o", o=1).broadcast_to(shape)

            def per_expert(a):
                return a[:].rearrange("p (o e) -> p o e", o=1).broadcast_to(shape)
            v.wait_ge(logit_ready, batches)
            v.wait_ge(consts, n_consts)
            step(nc.vector.tensor_reduce(a1[:], logit[:], AX_X, ALU.max))
            nc.vector.tensor_tensor(logit[:], logit[:], per_tile(a1), ALU.subtract).then_inc(shifted, 1)
            v.wait_ge(exps, 1)
            step(nc.vector.tensor_reduce(a1[:], prob[:], AX_X, ALU.add))
            step(nc.vector.reciprocal(a1[:], a1[:]))
            step(nc.vector.tensor_tensor(prob[:], prob[:], per_tile(a1), ALU.mult))
            step(nc.vector.tensor_reduce(a1[:], prob[:], AX_X, ALU.max))
            step.mark(nc.vector.tensor_copy(entry[:, :, 1], a1[:]))
            step(nc.vector.tensor_tensor(score[:], prob[:], per_tile(a1), ALU.is_ge))
            step(nc.vector.tensor_tensor(score[:], score[:], per_expert(first), ALU.mult))
            step(nc.vector.tensor_reduce(a2[:], score[:], AX_X, ALU.max))
            step(nc.vector.tensor_tensor(sel[:], score[:], per_tile(a2), ALU.is_equal))
            nc.vector.tensor_tensor(sel[:], sel[:], per_tile(valid), ALU.mult).then_inc(sel_ready, 1)
            v.wait_ge(counted, 2)
            v.wait_ge(sel_ready, 1)
            step(nc.vector.tensor_copy(upto[:, 0], counts[:, 0:TILES * EXP].rearrange("p (t e) -> p t e", e=EXP)))
            k, d = 0, 1
            while d < TILES:
                step.mark(nc.vector.tensor_copy(upto[:, 1 - k, 0:d], upto[:, k, 0:d]))
                step(nc.vector.tensor_tensor(upto[:, 1 - k, d:], upto[:, k, d:], upto[:, k, 0:TILES - d], ALU.add))
                k, d = 1 - k, 2 * d
            step(nc.vector.tensor_tensor(score[:], upto[:, k], ranks[:, 0:TILES * EXP].rearrange("p (t e) -> p t e", e=EXP), ALU.add))
            step(nc.vector.tensor_tensor(score[:], score[:], counts[:, 0:TILES * EXP].rearrange("p (t e) -> p t e", e=EXP), ALU.subtract))
            step(nc.vector.tensor_tensor(score[:], score[:], per_expert(start), ALU.add))
            step(nc.vector.tensor_tensor(score[:], score[:], sel[:], ALU.mult))
            step(nc.vector.tensor_reduce(a2[:], score[:], AX_X, ALU.add))
            nc.vector.tensor_copy(where[:], a2[:]).then_inc(placed, 1)
            total = upto[0:1, k, TILES - 1, :]
            step(nc.vector.tensor_tensor(full[:], total.rearrange("o (e u) -> o e u", u=1).broadcast_to([1, EXP, TILES]),
                                         hundreds[:, 0:TILES].rearrange("o (u t) -> o u t", u=1).broadcast_to([1, EXP, TILES]),
                                         ALU.is_gt))
            step(nc.vector.tensor_reduce(tiles[:], full[:], AX_X, ALU.add))
            step.mark(nc.vector.tensor_scalar(gap[:], tiles[:], -float(P), float(REGION), ALU.mult, ALU.add))
            step(nc.vector.tensor_scalar(ends[:, 0], tiles[:], float(P), None, ALU.mult))
            k, d = 0, 1
            while d < EXP:
                step.mark(nc.vector.tensor_copy(ends[:, 1 - k, 0:d], ends[:, k, 0:d]))
                step(nc.vector.tensor_tensor(ends[:, 1 - k, d:], ends[:, k, d:], ends[:, k, 0:EXP - d], ALU.add))
                k, d = 1 - k, 2 * d
            shape1 = [1, SLOTS, EXP]
            step(nc.vector.tensor_tensor(past[:], hundreds[:].rearrange("o (t u) -> o t u", u=1).broadcast_to(shape1),
                                         ends[:, k].rearrange("o (u e) -> o u e", u=1).broadcast_to(shape1), ALU.is_ge))
            step.mark(nc.vector.tensor_tensor(pgap[:], past[:], gap[:].rearrange("o (u e) -> o u e", u=1).broadcast_to(shape1), ALU.mult))
            step(nc.vector.tensor_reduce(o1[:], past[:], AX_X, ALU.add))
            step.mark(nc.vector.tensor_scalar(keep.which[:], o1[:], float(EXP - 1), None, ALU.min))
            step(nc.vector.tensor_reduce(o2[:], pgap[:], AX_X, ALU.add))
            step(nc.vector.tensor_tensor(o2[:], o2[:], hundreds[:], ALU.add))
            nc.vector.tensor_scalar(keep.offs[:], o2[:], float(EXP * REGION), None, ALU.min)

        @block.tensor
        def _(pe):
            pe.wait_ge(loaded, 64)
            nc.tensor.transpose(b1p[:, 0:HC], b1r[:], keep.ident[0:HC, 0:HC]).then_inc(b1_turned, 1)

            def gate(i, c):
                pe.wait_ge(h_ready, 2 * HC * (i - 1) + 2 * (c + 1))
                if c == 0:
                    after(pe, logit_ready, i - 1)
                for t in range(LB):
                    last = nc.tensor.matmul(lg[:, t * EXP:(t + 1) * EXP], h[:, c % 2, t * P:(t + 1) * P], wg[:, c, :],
                                            start=(c == 0 and t == 0), stop=(c == HC - 1), skip_group_check=True)
                last.then_inc(gated, 1)

            def body(i):
                for c in range(HC):
                    for q in range(2):
                        after(pe, h_ready, 2 * HC * (i - 1) + (2 * (c - 2) + q + 1))
                        for k in range(KC):
                            last = nc.tensor.matmul(hp[:, c % 2, q, 0:half], keep.w1[:, k, c * P:(c + 1) * P],
                                                    keep.xnT[:, k, bass.ds((i - 1) * (LB * P) + q * half, half)],
                                                    start=(k == 0), stop=(k == KC - 1))
                        last.then_inc(h_summed, 1)
                    if c >= 1:
                        gate(i, c - 1)
                gate(i, HC - 1)
            loop(pe, body, last=batches)
            pe.wait_ge(sel_ready, 1)
            pe.wait_ge(consts, n_consts)
            flat = sel[:].rearrange("p t e -> p (t e)")
            nc.tensor.matmul(ranks[:, 0:TILES * EXP], before[:], flat, start=True, stop=True).then_inc(counted, 1)
            nc.tensor.matmul(counts[:, 0:TILES * EXP], keep.ones[:], flat, start=True, stop=True).then_inc(counted, 1)


def experts(nc, keep, rows, order, out):
    with Scope(nc) as s:
        om = s.sb("f_om", [P, DEEP, 2])
        node = s.sb("f_node", [P, DEEP, 1], I32)
        xs = s.sb("f_xs", [P, DEEP, 2 * C])
        xT = s.sb("f_xT", [P, KC, P])
        h = s.sb("f_h", [P, HC, P])
        z = s.sb("f_z", [P, C])
        res = s.sb("f_res", [P, DEEP, C])
        turned = s.ps("f_turned", [P, 512])
        hp = s.ps("f_hp", [P, 2, 4, P])
        y = s.ps("f_y", [P, 2, 512])
        listed, gathered, stored = (s.sems(n, DEEP) for n in ("listed", "gathered", "stored"))
        node_ready, pool_go, turned_sem, xT_ready, h_summed, h_ready, y_ready, z_ready, res_ready = (s.sem(n) for n in (
            "node_ready", "pool_go", "turned", "xT_ready", "h_summed", "h_ready", "y_ready", "z_ready", "res_ready"))
        block = s.block()
        per = 4
        rows_flat = rows.rearrange("n two c -> n (two c)")

        def slots(eng, body):
            for k in range(DEEP):
                body(k + 1, k, 1)
            with eng.Fori(1, SLOTS // DEEP - 1) as i:
                for k in range(DEEP):
                    body(DEEP * i + (k + 1), k, i + 1)
            for k in range(DEEP):
                body(SLOTS - DEEP + (k + 1), k, SLOTS // DEEP)

        def ahead(t, k, i, n):
            return t + n, (k + n) % DEEP, i + (k + n) // DEEP

        @block.sync
        def _(sp):
            def body(t, k, i):
                after(sp, res_ready, t - DEEP)
                off = sp.value_load(keep.offs[0:1, bass.ds(t - 1, 1)], min_val=0, max_val=EXP * REGION)
                sp.dma_start(om[:, k, :], order[bass.ds(off, P), :]).then_inc(listed[k], 16)
            slots(sp, body)

        @block.gpsimd
        def _(pool):
            def fetch(t, k, i):
                pool.wait_ge(listed[k], 16 * i)
                after(pool, stored[k], 16 * (i - 1))
                pool.sem_inc(pool_go, 1)
                nc.gpsimd.tensor_copy(node[:, k, :], om[:, k, 0:1]).then_inc(node_ready, 1)
                pool.wait_ge(node_ready, t)
                pool.sem_inc(pool_go, 1)
                nc.gpsimd.indirect_dma_start(xs[:, k, :], None, rows_flat,
                                             bass.IndirectOffsetOnAxis(ap=node[:, k, :], axis=0)).then_inc(gathered[k], 16)

            def body(t, k, i):
                if not (isinstance(t, int) and t > SLOTS - LEAD):
                    fetch(*ahead(t, k, i, LEAD))
                pool.wait_ge(res_ready, t)
                pool.sem_inc(pool_go, 1)
                nc.gpsimd.indirect_dma_start(out, bass.IndirectOffsetOnAxis(ap=node[:, k, :], axis=0), res[:, k, :], None,
                                             bounds_check=N - 1, oob_is_err=False).then_inc(stored[k], 16)
            for k in range(LEAD):
                fetch(k + 1, k, 1)
            slots(pool, body)
            for k in range(DEEP):
                pool.wait_ge(stored[k], 16 * (SLOTS // DEEP))

        @block.scalar
        def _(act):
            def body(t, k, i):
                for b in range(2):
                    act.wait_ge(h_summed, 2 * (t - 1) + (b + 1))
                    if b == 0:
                        after(act, y_ready, t - 1)
                    for c in range(per):
                        n = b * per + c
                        nc.scalar.activation(h[:, n, :], hp[:, b, c, :], ACT.Gelu,
                                             bias=keep.b1T[:, n:n + 1]).then_inc(h_ready, 1)
            act.wait_ge(keep.b1_ready, 1)
            slots(act, body)

        @block.vector
        def _(v):
            def copy(t, k, i):
                v.wait_ge(turned_sem, t)
                after(v, h_summed, 2 * (t - 1))
                nc.vector.tensor_copy(xT[:].rearrange("p k n -> p (k n)"), turned[:, 0:C]).then_inc(xT_ready, 1)

            def body(t, k, i):
                if not (isinstance(t, int) and t == SLOTS):
                    copy(*ahead(t, k, i, 1))
                e = v.value_load(keep.which[0:1, bass.ds(t - 1, 1)], min_val=0, max_val=EXP - 1)
                v.wait_ge(y_ready, t)
                after(v, res_ready, t - 1)
                nc.vector.tensor_tensor(z[:], y[:, k % 2, 0:C], keep.bd[:, bass.ds(e * C, C)], ALU.add).then_inc(z_ready, 1)
                v.wait_ge(z_ready, t)
                after(v, stored[k], 16 * (i - 1))
                v.wait_ge(gathered[k], 16 * i)
                nc.vector.scalar_tensor_tensor(out=res[:, k, :], in0=z[:], scalar=om[:, k, 1:2], in1=xs[:, k, C:2 * C],
                                               op0=ALU.mult, op1=ALU.add).then_inc(res_ready, 1)
            v.wait_ge(keep.wd_loaded, 16 * (HC + 1))
            copy(1, 0, 1)
            slots(v, body)

        @block.tensor
        def _(pe):
            def turn(t, k, i):
                pe.wait_ge(gathered[k], 16 * i)
                after(pe, xT_ready, t - 1)
                for c in range(KC):
                    last = nc.tensor.transpose(turned[:, c * P:(c + 1) * P], xs[:, k, c * P:(c + 1) * P], keep.ident[:])
                last.then_inc(turned_sem, 1)

            def body(t, k, i):
                e = pe.value_load(keep.which[0:1, bass.ds(t - 1, 1)], min_val=0, max_val=EXP - 1)
                pe.wait_ge(xT_ready, t)
                for b in range(2):
                    after(pe, h_ready, HC * (t - 1) - (per if b == 0 else 0))
                    for c in range(per):
                        n = b * per + c
                        for kc in range(KC):
                            last = nc.tensor.matmul(hp[:, b, c, :], keep.w1[:, kc, n * P:(n + 1) * P], xT[:, kc, :],
                                                    start=(kc == 0), stop=(kc == KC - 1))
                    last.then_inc(h_summed, 1)
                if not (isinstance(t, int) and t == SLOTS):
                    turn(*ahead(t, k, i, 1))
                after(pe, z_ready, t - 2)
                for c in range(HC):
                    pe.wait_ge(h_ready, HC * (t - 1) + (c + 1))
                    last = nc.tensor.matmul(y[:, k % 2, 0:C], h[:, c, :], keep.wd[:, c, bass.ds(e * C, C)],
                                            start=(c == 0), stop=(c == HC - 1))
                last.then_inc(y_ready, 1)
            pe.wait_ge(keep.wd_loaded, 16 * (HC + 1))
            turn(1, 0, 1)
            slots(pe, body)


class Keep:
    pass


def build(nc, x, src, dst, edge_type_20, edge_weight1, L0_gnn_weight, L0_mix_Wqkv, L0_mix_bqkv, L0_mix_Wproj,
          L0_mix_bproj, L0_mix_temperature, L0_ffn_W1, L0_ffn_b1, L0_ffn_Wg, L0_ffn_bg, L0_ffn_Wd, L0_ffn_bd, out):
    table = nc.dram_tensor("table", (NPAD * RELS, C), F32, kind="Internal").ap()
    x1 = nc.dram_tensor("x1", (NPAD, C), F32, kind="Internal").ap()
    rows = nc.dram_tensor("rows", (NPAD, 2, C), F32, kind="Internal").ap()
    order = nc.dram_tensor("order", ((EXP + 1) * REGION, 2), F32, kind="Internal").ap()
    keep = Keep()
    with Scope(nc) as s:
        keep.ident = s.sb("k_ident", [P, P])
        keep.offsets = s.sb("k_offsets", [P, WIN])
        keep.ones = s.sb("k_ones", [P, P])
        keep.idxT = s.sb("k_idxT", [P, COLS], I32)
        keep.winT = s.sb("k_winT", [P, COLS])
        keep.nrmT = s.sb("k_nrmT", [P, COLS])
        keep.base = s.sb("k_base", [1, GROUPS], I32)
        keep.far = s.sb("k_far", [1, 1], I32)
        keep.which = s.sb("k_which", [1, SLOTS], I32)
        keep.offs = s.sb("k_offs", [1, SLOTS], I32)
        keep.w_loaded, keep.wd_loaded, keep.b1_ready = s.sem("w_loaded"), s.sem("wd_loaded"), s.sem("b1_ready")
        keep.xnT = s.sb("k_xnT", [P, KC, NPAD])
        with Scope(nc) as t:
            keep.aggT = t.sb("k_aggT", [P, KC, AGG])
            keep.weight = keep.aggT[:].rearrange("p k n -> p (k n)")[:, 0:KC * RELS * C]\
                .rearrange("p (k r c) -> p k r c", k=KC, c=C)
            edges(nc, keep, src, dst, edge_type_20, edge_weight1.rearrange("e o -> (e o)"), L0_gnn_weight)
            relations(nc, keep, x, table)
            keep.wT = t.sb("k_wT", [P, KC, 3 * C])
            keep.wpT = t.sb("k_wpT", [P, KC, C])
            keep.bias_qkv = t.sb("k_bias_qkv", [P, 3 * C])
            keep.bias_p = t.sb("k_bias_p", [P, C])
            keep.temp = t.sb("k_temp", [P, HEADS])
            keep.factor = t.sb("k_factor", [P, 3])
            keep.mom = t.sb("k_mom", [P, PT, DV2])
            keep.momw = t.sb("k_momw", [P, HP, DV2])
            keep.mom1 = t.sb("k_mom1", [1, HEADS * DV])
            weights(nc, keep, L0_mix_Wqkv, L0_mix_bqkv, L0_mix_Wproj, L0_mix_bproj, L0_mix_temperature)
            moments(nc, keep, table)
            readout(nc, keep, table, x, x1)
            far_edges(nc, keep, table)
            second_norm(nc, keep, x1, rows)
        keep.w1 = s.sb("k_w1", [P, KC, HID])
        keep.b1T = s.sb("k_b1T", [P, HC])
        keep.wd = s.sb("k_wd", [P, HC, EXP * C])
        keep.bd = s.sb("k_bd", [P, EXP * C])
        choose(nc, keep, L0_ffn_Wd, L0_ffn_W1, L0_ffn_b1, L0_ffn_Wg, L0_ffn_bg, L0_ffn_bd, order)
        experts(nc, keep, rows, order, out)


_INS = ['x', 'src', 'dst', 'edge_type_20', 'edge_weight1', 'L0_gnn_weight', 'L0_mix_Wqkv', 'L0_mix_bqkv',
        'L0_mix_Wproj', 'L0_mix_bproj', 'L0_mix_temperature', 'L0_ffn_W1', 'L0_ffn_b1', 'L0_ffn_Wg', 'L0_ffn_bg',
        'L0_ffn_Wd', 'L0_ffn_bd']
_OUTS = [((N, C), 'float32')]


def kernel(**inputs):
    import numpy as _np
    import concourse.bacc as _bacc
    from concourse import mybir as _mybir
    from concourse.bass_utils import run_bass_kernel_spmd as _run

    nc = _bacc.Bacc("TRN2", target_bir_lowering=False, num_devices=1)
    arrays, args = {}, []
    for name in _INS:
        a = _np.ascontiguousarray(inputs[name])
        arrays[f"in_{name}_dram"] = a
        args.append(nc.dram_tensor(f"in_{name}_dram", a.shape, _mybir.dt.from_np(a.dtype), kind="ExternalInput").ap())
    for i, (shape, dtype) in enumerate(_OUTS):
        dt = _mybir.dt.from_np(_np.dtype(dtype))
        args.append(nc.dram_tensor(f"out_{i}_dram", shape, dt, kind="ExternalOutput").ap())
    build(nc, *args)
    r = _run(nc, [arrays], core_ids=[0])
    got = tuple(r.results[0][f"out_{i}_dram"] for i in range(len(_OUTS)))
    return got[0]
```

```python
from contextlib import ExitStack

import numpy as np

import concourse.bass as bass
from concourse import mybir

ALU = mybir.AluOpType
ACT = mybir.ActivationFunctionType
F32 = mybir.dt.float32
F32R = mybir.dt.float32r
I32 = mybir.dt.int32
AX_X = mybir.AxisListType.X

P = 128
N, C = 6250, 256
KC = C // P
TILES = (N + P - 1) // P
NPAD = TILES * P
LAST = N - (TILES - 1) * P
LN_EPS = 1e-5

E, RELS = 200000, 20
GE = 4
GROUP = GE * P
WIN = 64
GPT_KEYS, GPT_QUERIES = 3, 5
GROUPS = (GPT_KEYS + GPT_QUERIES) * TILES
GPT = 4
assert GROUPS % GPT == 0
CHUNKS = (GROUPS + P - 1) // P
COLS = GROUPS * GE
FULL_G, REST_E = E // GROUP, E % GROUP
WINDOWS = (N + WIN - 1) // WIN
AGG = N + WIN
assert GROUPS * GROUP >= E and FULL_G // P == CHUNKS - 1

HEADS, D = 8, 32
DV = D + 1
SHIFTS = D // 2
PAIRS = HEADS * SHIFTS * D
PT = PAIRS // P
TPH = PT // HEADS
FT = PT + 2 * HEADS * D // P
DW = D + SHIFTS
SC = float(D) ** 0.25
ROOT_EPS = 1e-12

HID, EXP = 1024, 8
HC = HID // P


def after(eng, sem, value):
    if isinstance(value, int) and value <= 0:
        return
    eng.wait_ge(sem, value)


class Chain:

    def __init__(self, eng, sem, per=0):
        self.eng, self.sem, self.per, self.n, self.base = eng, sem, per, 0, 0

    def start(self, done):
        self.base, self.n = done * self.per, 0

    def end(self):
        assert self.n == self.per, (self.n, self.per)

    def mark(self, ins):
        self.n += 1
        ins.then_inc(self.sem, 1)
        return self.n

    def wait(self, n=None):
        self.eng.wait_ge(self.sem, self.base + (self.n if n is None else n))

    def __call__(self, ins):
        self.mark(ins)
        self.wait()


def loop(eng, body, first=1, last=TILES):
    body(first)
    with eng.Fori(first + 1, last) as i:
        body(i)
    body(last)


def is_last(i):
    return isinstance(i, int) and i == TILES


def pairs(eng, body, count):
    body(1, 0, 1)
    body(2, 1, 1)
    with eng.Fori(1, count // 2) as i:
        for k in range(2):
            body(2 * i + (k + 1), k, i + 1)
    body(count, 0, count // 2 + 1)


class Scope:

    def __init__(self, nc):
        self.nc, self.ctx = nc, ExitStack()

    def __enter__(self):
        self.ctx.__enter__()
        return self

    def __exit__(self, *a):
        return self.ctx.__exit__(*a)

    def sb(self, name, shape, dt=F32):
        return self.ctx.enter_context(self.nc.sbuf_tensor(name, shape, dt))

    def ps(self, name, shape):
        return self.ctx.enter_context(self.nc.psum_tensor(name, shape, F32))

    def sem(self, name):
        return self.ctx.enter_context(self.nc.semaphore(name))

    def sems(self, name, n):
        return [self.sem(f"{name}{i}") for i in range(n)]

    def block(self):
        return self.ctx.enter_context(self.nc.Block())


def edges(nc, keep, src, dst, rel, norm, weight):
    with Scope(nc) as s:
        def room(n):
            size = CHUNKS * GROUP
            return keep.xnT[:].rearrange("p k n -> p (k n)")[:, n * size:(n + 1) * size]\
                .rearrange("p (c e) -> p c e", e=GROUP)
        raw = {k: room(n).bitcast(I32) for n, k in enumerate(("src", "rel", "dst"))}
        top = s.sb("e_top", [P, GROUP], I32)
        nrm, idx, dstf = room(3), room(4), room(5)
        topf = s.sb("e_topf", [P, GROUP])
        low = s.sb("e_low", [P, CHUNKS])
        high = s.sb("e_high", [P, CHUNKS])
        span = s.sb("e_span", [P, CHUNKS])
        wide = s.sb("e_wide", [P, 1])
        turned = s.ps("e_turned", [P, 2, GE, P])
        rows = s.ps("e_rows", [1, CHUNKS, P])
        count = s.ps("e_count", [1, 1])
        padded, loaded, ident_ready = s.sem("padded"), s.sem("loaded"), s.sem("ident_ready")
        ready, rows_ready, turned_sem, emptied = s.sem("ready"), s.sem("rows_ready"), s.sem("turned"), s.sem("emptied")
        steps = s.sem("dve_steps")
        block = s.block()
        named = {"src": src, "rel": rel, "dst": dst}

        def load(eng, out, a):
            eng.dma_start(out[:, 0:CHUNKS - 1, :],
                          a[0:(CHUNKS - 1) * P * GROUP].rearrange("(c g e) -> g c e", g=P, e=GROUP)).then_inc(loaded, 16)
            tail(eng, out[:, CHUNKS - 1, :], a)

        def tail(eng, out, a):
            g0, g1 = (CHUNKS - 1) * P, FULL_G
            eng.dma_start(out[0:g1 - g0, :], a[g0 * GROUP:g1 * GROUP].rearrange("(g e) -> g e", e=GROUP)).then_inc(loaded, 16)
            eng.dma_start(out[g1 - g0:g1 - g0 + 1, 0:REST_E], a[g1 * GROUP:E].rearrange("(g e) -> g e", g=1)).then_inc(loaded, 16)

        @block.sync
        def _(sp):
            sp.wait_ge(padded, 5)
            for k in ("dst", "src", "rel"):
                load(sp, raw[k], named[k])
            tail(sp, top, dst)
            load(sp, nrm, norm)
            for k in range(KC):
                sp.dma_start(keep.weight[:, k],
                             weight[:, k * P:(k + 1) * P, :].rearrange("r p o -> p r o")).then_inc(keep.w_loaded, 16)

        @block.gpsimd
        def _(pool):
            for k in ("src", "rel"):
                nc.gpsimd.memset(raw[k][:, CHUNKS - 1, :], 0).then_inc(padded, 1)
            nc.gpsimd.memset(raw["dst"][:, CHUNKS - 1, :], N - 1).then_inc(padded, 1)
            nc.gpsimd.memset(top[:], 0).then_inc(padded, 1)
            nc.gpsimd.memset(nrm[:, CHUNKS - 1, :], 0.0).then_inc(padded, 1)
            nc.gpsimd.memset(keep.ident[:], 0.0).then_inc(ident_ready, 1)
            pool.wait_ge(ident_ready, 1)
            nc.gpsimd.affine_select(out=keep.ident[:], in_=keep.ident[:], compare_op=ALU.not_equal, fill=1.0,
                                    base=0, pattern=[[-1, P]], channel_multiplier=1).then_inc(ident_ready, 1)
            nc.gpsimd.iota(keep.offsets[:], [[1, WIN]], base=0, channel_multiplier=0,
                           allow_small_or_imprecise_dtypes=True).then_inc(ident_ready, 1)
            nc.gpsimd.memset(keep.ones[:], 1.0).then_inc(ident_ready, 1)

        @block.vector
        def _(v):
            step = Chain(v, steps)
            v.wait_ge(loaded, 16 * 14)
            step.mark(nc.vector.tensor_copy(dstf[:], raw["dst"][:]))
            step.mark(nc.vector.tensor_copy(topf[:], top[:]))
            step.mark(nc.vector.tensor_scalar(idx[:], raw["src"][:], float(RELS), None, ALU.mult))
            step.wait()
            step.mark(nc.vector.tensor_tensor(idx[:], idx[:], raw["rel"][:], ALU.add))
            step.mark(nc.vector.tensor_reduce(low[:], dstf[:], AX_X, ALU.min))
            step.mark(nc.vector.tensor_reduce(high[:, 0:CHUNKS - 1], dstf[:, 0:CHUNKS - 1, :], AX_X, ALU.max))
            step.mark(nc.vector.tensor_reduce(high[:, CHUNKS - 1:CHUNKS], topf[:], AX_X, ALU.max))
            step.wait()
            step.mark(nc.vector.tensor_tensor(span[:], high[:], low[:], ALU.subtract))
            for c in range(CHUNKS):
                step.mark(nc.vector.tensor_scalar(dstf[:, c, :], dstf[:, c, :], low[:, c:c + 1], None, ALU.subtract))
            step.wait()
            step(nc.vector.tensor_scalar(span[:], span[:], float(WIN), None, ALU.is_ge))
            nc.vector.tensor_reduce(wide[:], span[:], AX_X, ALU.add).then_inc(ready, 1)
            v.wait_ge(rows_ready, 1)
            nc.vector.tensor_copy(keep.base[:], rows[:].rearrange("o c g -> o (c g)")[:, 0:GROUPS]).then_inc(emptied, 1)
            nc.vector.tensor_copy(keep.far[:], count[:]).then_inc(emptied, 1)
            n = 0
            for out in (keep.winT, keep.idxT, keep.nrmT):
                for c in range(CHUNKS):
                    g = min(P, GROUPS - c * P)
                    v.wait_ge(turned_sem, n + 1)
                    nc.vector.tensor_copy(out[:, c * P * GE:(c * P + g) * GE].rearrange("p (g j) -> p j g", j=GE),
                                          turned[:, n % 2, :, 0:g]).then_inc(emptied, 1)
                    n += 1

        @block.tensor
        def _(pe):
            pe.wait_ge(ready, 1)
            pe.wait_ge(ident_ready, 4)
            for c in range(CHUNKS):
                nc.tensor.matmul(rows[:, c, :], low[:, c:c + 1], keep.ident[:], start=True, stop=True)
            nc.tensor.matmul(count[:], wide[:], keep.ones[:, 0:1], start=True, stop=True).then_inc(rows_ready, 1)
            n = 0
            for a in (dstf, idx, nrm):
                for c in range(CHUNKS):
                    after(pe, emptied, n + 1 if n >= 2 else 0)
                    for j in range(GE):
                        last = nc.tensor.transpose(turned[:, n % 2, j, :], a[:, c, j * P:(j + 1) * P], keep.ident[:])
                    last.then_inc(turned_sem, 1)
                    n += 1


LB = 7
assert TILES % LB == 0 and TILES // LB % 2 == 1 and TILES % 2 == 1


CH = 10
RPC = RELS // CH
BANKS = 5


def relations(nc, keep, x, table):
    with Scope(nc) as s:
        xs = s.sb("r_x", [P, 2, C])
        sq = s.sb("r_sq", [P, C])
        total, var, sd, inv = (s.sb(f"r_{n}", [P, 1]) for n in ("total", "var", "sd", "inv"))
        xT = s.sb("r_xT", [P, 2, 2, KC, P], F32R)
        w_high, w_low = (s.sb(f"r_w_{n}", [P, KC, RELS, C], F32R) for n in ("high", "low"))
        rows = keep.aggT[:].rearrange("p k n -> p (k n)")[:, 0:2 * RELS * C].rearrange("p (b c) -> p b c", b=2)
        acc = s.ps("r_acc", [P, BANKS, 512])
        turned = s.ps("r_turned", [P, 512])
        loaded, stored, emptied = s.sems("x_loaded", 2), s.sems("stored", 2), s.sems("emptied", 2)
        (high_ready, w_ready, xc_ready, squared, var_ready, sd_ready, xn_ready, turned_sem, xT_high, xT_low,
         summed, steps) = (s.sem(n) for n in (
             "w_high_ready", "w_ready", "xc_ready", "squared", "var_ready", "sd_ready", "xn_ready", "turned",
             "xT_high", "xT_low", "summed", "dve_steps"))
        block = s.block()
        out = table.rearrange("(n r) c -> n (r c)", r=RELS)
        half = CH // 2
        step = Chain(nc.vector, steps, 7)

        def piece(a, c):
            return a[:, :, c * RPC:(c + 1) * RPC, :]

        def empty(eng, copy, n, k, i, c):
            eng.wait_ge(summed, CH * (n - 1) + (c + 1))
            if c < 2:
                after(eng, stored[k], (i - 1) * 16)
            copy(rows[:, k, c * 512:(c + 1) * 512], acc[:, c % BANKS, :]).then_inc(emptied[c % 2], 1)

        @block.gpsimd
        def _(pool):
            def body(n, k, i):
                after(pool, turned_sem, n - 2)
                if is_last(n):
                    pool.dma_start(xs[0:LAST, k, :], x[(n - 1) * P:N, :]).then_inc(loaded[k], 16)
                else:
                    pool.dma_start(xs[:, k, :], x[bass.ds((n - 1) * P, P), :]).then_inc(loaded[k], 16)
            pairs(pool, body, TILES)

        @block.sync
        def _(sp):
            def body(n, k, i):
                sp.wait_ge(emptied[0], half * n)
                sp.wait_ge(emptied[1], half * n)
                sp.dma_start(out[bass.ds((n - 1) * P, P), :], rows[:, k, :]).then_inc(stored[k], 16)
            pairs(sp, body, TILES)
            sp.wait_ge(stored[0], (TILES // 2 + 1) * 16)
            sp.wait_ge(stored[1], (TILES // 2) * 16)

        @block.scalar
        def _(act):
            def square(n, k):
                act.wait_ge(xc_ready, n)
                nc.scalar.activation(sq[:], xs[:, k, :], ACT.Square).then_inc(squared, 1)

            def root(n):
                act.wait_ge(var_ready, n)
                nc.scalar.activation(sd[:], var[:], ACT.Sqrt).then_inc(sd_ready, 1)

            def split(n, k):
                act.wait_ge(turned_sem, n)
                after(act, summed, CH * (n - 2))
                nc.scalar.copy(xT[:, k, 0].rearrange("p c n -> p (c n)"), turned[:, 0:C]).then_inc(xT_high, 1)

            act.wait_ge(keep.w_loaded, 16 * KC)
            square(1, 0)
            root(1)
            for c in range(CH):
                nc.scalar.copy(piece(w_high, c), piece(keep.weight, c)).then_inc(high_ready, 1)
            split(1, 0)

            def body(n, k, i):
                for c in range(0, CH, 2):
                    empty(act, nc.scalar.copy, n, k, i, c)
                    if is_last(n):
                        continue
                    if c == 2:
                        square(n + 1, 1 - k)
                    if c == 4:
                        root(n + 1)
                    if c == 6:
                        split(n + 1, 1 - k)
            pairs(act, body, TILES)

        @block.vector
        def _(v):
            def centre(n, k, i):
                v.wait_ge(loaded[k], 16 * i)
                step.start(n - 1)
                step(nc.vector.tensor_reduce(total[:], xs[:, k, :], AX_X, ALU.add))
                step(nc.vector.tensor_scalar(total[:], total[:], 1.0 / C, None, ALU.mult))
                nc.vector.tensor_scalar(xs[:, k, :], xs[:, k, :], total[:], None, ALU.subtract).then_inc(xc_ready, 1)

            def normalise(n, k):
                v.wait_ge(squared, n)
                step(nc.vector.tensor_reduce(var[:], sq[:], AX_X, ALU.add))
                nc.vector.tensor_scalar(var[:], var[:], 1.0 / C, LN_EPS, ALU.mult, ALU.add).then_inc(var_ready, 1)
                v.wait_ge(sd_ready, n)
                root_inverse(nc, step, inv, sd, var)
                step.end()
                nc.vector.tensor_scalar(xs[:, k, :], xs[:, k, :], inv[:], 2.0, ALU.mult, ALU.mult).then_inc(xn_ready, 1)

            def split(n, k):
                v.wait_ge(xT_high, n)
                nc.vector.tensor_scalar(keep.xnT[:, :, bass.ds((n - 1) * P, P)],
                                        turned[:, 0:C].rearrange("p (k n) -> p k n", k=KC), 1.0, None,
                                        ALU.mult)
                nc.vector.tensor_tensor(xT[:, k, 1], turned[:, 0:C].rearrange("p (k n) -> p k n", k=KC),
                                        xT[:, k, 0].bitcast(F32), ALU.subtract).then_inc(xT_low, 1)

            centre(1, 0, 1)
            normalise(1, 0)
            v.wait_ge(keep.w_loaded, 16 * KC)
            for c in range(CH):
                v.wait_ge(high_ready, c + 1)
                nc.vector.tensor_tensor(piece(w_low, c), piece(keep.weight, c), piece(w_high, c).bitcast(F32),
                                        ALU.subtract).then_inc(w_ready, 1)
            split(1, 0)

            def body(n, k, i):
                for c in range(1, CH, 2):
                    empty(v, nc.vector.tensor_copy, n, k, i, c)
                    if is_last(n):
                        continue
                    if c == 1:
                        centre(n + 1, 1 - k, i + k)
                    if c == 3:
                        normalise(n + 1, 1 - k)
                    if c == 7:
                        split(n + 1, 1 - k)
            pairs(v, body, TILES)

        @block.tensor
        def _(pe):
            def turn(n, k):
                pe.wait_ge(xn_ready, n)
                after(pe, xT_low, n - 1)
                for c in range(KC):
                    last = nc.tensor.transpose(turned[:, c * P:(c + 1) * P], xs[:, k, c * P:(c + 1) * P], keep.ident[:])
                last.then_inc(turned_sem, 1)

            def body(n, k, i):
                pe.wait_ge(xT_high, n)
                pe.wait_ge(xT_low, n)
                for c in range(CH):
                    if isinstance(n, int) and n == 1:
                        pe.wait_ge(w_ready, c + 1)
                    old = (c - BANKS) % CH
                    after(pe, emptied[old % 2], half * (n - 2 if c < BANKS else n - 1) + (old // 2 + 1))
                    products = [(a, w, kc) for a, w in ((0, w_high), (0, w_low), (1, w_high))
                                for kc in range(KC)]
                    for m, (a, w, kc) in enumerate(products):
                        last = nc.tensor.matmul(acc[:, c % BANKS, :], xT[:, k, a, kc, :],
                                                w[:, kc, c * RPC:(c + 1) * RPC, :].rearrange("p r o -> p (r o)"),
                                                start=(m == 0), stop=(m == len(products) - 1))
                    last.then_inc(summed, 1)
                    if c == 6 and not is_last(n):
                        turn(n + 1, 1 - k)
            turn(1, 0)
            pairs(pe, body, TILES)


class Gather:

    def __init__(self, nc, s, keep, table, first, per, tag, counted=0):
        self.nc, self.keep, self.table, self.first, self.per = nc, keep, table, first, per
        self.counted = counted
        k = f"g_{tag}"
        self.rows = s.sb(f"{k}_rows", [P, per, GE, C])
        self.where = s.sb(f"{k}_where", [P, per, GE], I32)
        self.hot = s.sb(f"{k}_hot", [P, per, GE, WIN])
        self.node_regs = [nc.vector.alloc_register(f"{k}_node{j}") for j in range(per)]
        self.sum = s.ps(f"{k}_sum", [P, 2, 512])
        self.where_ready, self.pool_go = s.sem("where_ready"), s.sem("pool_go")
        self.equal_ready = s.sem("equal_ready")
        self.gathered = s.sems("gathered", per)
        self.hot_ready = s.sem("hot_ready")
        self.summed = s.sem("summed")
        self.added = s.sem("added")

    def cols(self, at, j=0, n=None):
        return bass.ds((at - 1) * (self.per * GE) + (self.first + j) * GE, self.per * GE if n is None else n)

    def pool_fetch(self, pool, i, at=None):
        at = i if at is None else at
        for j in range(self.per):
            after(pool, self.summed, self.per * (i - 2) + (j + 1))
            pool.sem_inc(self.pool_go, 1)
            self.nc.gpsimd.tensor_copy(self.where[:, j, :], self.keep.idxT[:, self.cols(at, j, GE)])\
                .then_inc(self.where_ready, 1)
            pool.wait_ge(self.where_ready, self.per * (i - 1) + (j + 1))
            pool.sem_inc(self.pool_go, 1)
            for t in range(GE):
                self.nc.gpsimd.indirect_dma_start(
                    self.rows[:, j, t, :], None, self.table,
                    bass.IndirectOffsetOnAxis(ap=self.where[:, j, t:t + 1], axis=0)).then_inc(self.gathered[j], 16)

    def vector_hot(self, v, i, at=None, between=None):
        at = i if at is None else at
        shape = [P, self.per * GE, WIN]
        hot = self.hot[:].rearrange("p g t w -> p (g t) w")

        def cols(a):
            return a[:, self.cols(at)].rearrange("p (c o) -> p c o", o=1).broadcast_to(shape)
        after(v, self.summed, self.per * (i - 1))
        self.nc.vector.tensor_tensor(hot, self.keep.offsets[:].rearrange("p (o w) -> p o w", o=1).broadcast_to(shape),
                                     cols(self.keep.winT), ALU.is_equal).then_inc(self.equal_ready, 1)
        if between:
            between()
        v.wait_ge(self.equal_ready, i)
        self.nc.vector.tensor_tensor(hot, hot, cols(self.keep.nrmT), ALU.mult).then_inc(self.hot_ready, 1)
        v.load(self.node_regs, self.keep.base[0:1, bass.ds((at - 1) * self.per + self.first, self.per)])

    def tensor_sum(self, pe, i, j):
        pe.wait_ge(self.hot_ready, i)
        pe.wait_ge(self.gathered[j], (i - self.counted) * (16 * GE))
        after(pe, self.added, self.per * (i - 1) + (j - 1 if j or self.per % 2 == 0 else 0))
        for t in range(GE):
            for k in range(KC):
                last = self.nc.tensor.matmul(self.sum[:, j % 2, k * WIN:(k + 1) * WIN],
                                             self.rows[:, j, t, k * P:(k + 1) * P], self.hot[:, j, t, :],
                                             start=(t == 0 and k == 0), stop=(t == GE - 1), skip_group_check=True)
        last.then_inc(self.summed, 1)

    def vector_add(self, v, i, j):
        v.wait_ge(self.summed, self.per * (i - 1) + (j + 1))
        after(v, self.added, self.per * (i - 1) + j)
        node = v.snap(self.node_regs[j], min_val=0, max_val=N)
        self.nc.vector.tensor_tensor(self.keep.aggT[:, :, bass.ds(node, WIN)], self.keep.aggT[:, :, bass.ds(node, WIN)],
                                     self.sum[:, j % 2, 0:KC * WIN].rearrange("p (k w) -> p k w", w=WIN),
                                     ALU.add).then_inc(self.added, 1)


def heads(a, n):
    return a.rearrange("p (h d) -> p h d", d=n)


HP = HEADS // 2
DV2 = 2 * DV
RES = 2 * D


def pair_features(nc, out, z, hp, ready):
    a = z[:, 2 * hp:2 * hp + 2, :]
    part = a.ap[0]
    shifted = bass.AP(a.tensor, a.offset, [part, (DW, 2), (1, SHIFTS), (1, D)])
    plain = bass.AP(a.tensor, a.offset, [part, (DW, 2), (0, SHIFTS), (1, D)])
    n = 2 * SHIFTS * D
    nc.vector.tensor_tensor(out[:, hp * n:(hp + 1) * n].rearrange("p (h s d) -> p h s d", s=SHIFTS, d=D),
                            plain, shifted, ALU.mult).then_inc(ready, 1)


def rest_features(nc, out, z, ready):
    nc.vector.tensor_tensor(out[:, :, 0:D], z[:, :, 0:D], z[:, :, SHIFTS:DW], ALU.mult).then_inc(ready, 1)
    nc.vector.tensor_copy(out[:, :, D:RES], z[:, :, 0:D]).then_inc(ready, 1)


def root_inverse(nc, step, inv, sd, ss):
    step(nc.vector.reciprocal(inv[:], sd[:]))
    step(nc.vector.tensor_tensor(inv[:], inv[:], ss[:], ALU.mult))
    step(nc.vector.tensor_tensor(inv[:], inv[:], sd[:], ALU.add))
    step(nc.vector.reciprocal(inv[:], inv[:]))


def moments(nc, keep, g):
    with Scope(nc) as s:
        xT = s.sb("m_xT", [P, KC, P])
        kv = s.sb("m_kv", [P, 2 * C])
        sq = s.sb("m_sq", [P, C])
        ss, sd, inv = (s.sb(f"m_{n}", [P, HEADS]) for n in ("ss", "sd", "inv"))
        kd = s.sb("m_kd", [P, HEADS, DW])
        kk = s.sb("m_kk", [P, PAIRS])
        kr = s.sb("m_kr", [P, HEADS, RES + 1])
        v1 = s.sb("m_v1", [P, HEADS, DV])
        proj = s.ps("m_proj", [P, 512])
        acc = s.ps("m_acc", [P, HP + 1, 512])
        x_ready, projected, kv_ready, squared = s.sem("x_ready"), s.sem("projected"), s.sem("kv_ready"), s.sem("squared")
        ss_ready, sd_ready, feats_ready, v_ready, multiplied = (s.sem(n) for n in (
            "ss_ready", "sd_ready", "feats_ready", "v_ready", "multiplied"))
        pairsT = s.sb("m_pairsT", [P, HP, 512])
        restT = s.sb("m_restT", [P, HP, 2 * RES])
        oneT = s.sb("m_oneT", [P, HP])
        zeroed, steps, kd_ready, emptied, turned = (s.sem(n) for n in ("zeroed", "dve_steps", "kd_ready", "emptied", "turned"))
        block = s.block()

        @block.gpsimd
        def _(pool):
            nc.gpsimd.memset(v1[:], 1.0).then_inc(zeroed, 1)
            nc.gpsimd.memset(kr[:], 1.0).then_inc(zeroed, 1)
            for a in (pairsT, restT, oneT, keep.mom, keep.momw):
                nc.gpsimd.memset(a[:], 0.0).then_inc(zeroed, 1)
            loop(pool, lambda i: g.pool_fetch(pool, i), first=2)

        @block.scalar
        def _(act):
            def tile(t):
                act.wait_ge(kv_ready, t)
                nc.scalar.activation(sq[:], kv[:, 0:C], ACT.Square).then_inc(squared, 1)
                act.wait_ge(ss_ready, t)
                nc.scalar.activation(sd[:], ss[:], ACT.Sqrt).then_inc(sd_ready, 1)
                for hp in range(HP):
                    after(act, multiplied, HP * (t - 2) + (hp + 1) if not isinstance(t, int) or t > 1 else 0)
                    nc.scalar.copy(v1[:, 2 * hp:2 * hp + 2, 1:DV],
                                   heads(kv[:, C + 2 * hp * D:C + (2 * hp + 2) * D], D)).then_inc(v_ready, 1)
            act.wait_ge(zeroed, 7)
            loop(act, tile)

        @block.vector
        def _(v):
            step = Chain(v, steps, 5)

            def fix(t):
                after(v, projected, t - 1)
                nc.vector.tensor_scalar(xT[:], keep.xnT[:, :, bass.ds((t - 1) * P, P)], 1.0, None,
                                        ALU.mult).then_inc(x_ready, 1)

            def norm(t):
                step.start(t - 1)
                v.wait_ge(projected, t)
                after(v, v_ready, HP * (t - 1))
                nc.vector.tensor_tensor(kv[:], proj[:], keep.bias_qkv[:, C:3 * C], ALU.add).then_inc(kv_ready, 1)
                v.wait_ge(squared, t)
                step(nc.vector.tensor_reduce(ss[:], heads(sq[:], D), AX_X, ALU.add))
                nc.vector.tensor_scalar(ss[:], ss[:], ROOT_EPS * ROOT_EPS, None, ALU.max).then_inc(ss_ready, 1)
                v.wait_ge(sd_ready, t)
                root_inverse(nc, step, inv, sd, ss)
                scaled = inv[:].rearrange("p (h o) -> p h o", o=1)
                for a, n in ((0, D), (D, SHIFTS)):
                    last = nc.vector.scalar_tensor_tensor(out=kd[:, :, a:a + n], in0=heads(kv[:, 0:C], D)[:, :, 0:n],
                                                          scalar=2.0 * SC, in1=scaled.broadcast_to([P, HEADS, n]),
                                                          op0=ALU.mult, op1=ALU.mult)
                    last.then_inc(kd_ready, 1)
                step.end()

            def part(hp):
                pair_features(nc, kk, kd, hp, feats_ready)
                h = slice(2 * hp, 2 * hp + 2)
                rest_features(nc, kr[:, h, :], kd[:, h, :], feats_ready)

            v.wait_ge(zeroed, 7)
            fix(1)
            norm(1)
            v.wait_ge(kd_ready, 2)
            for hp in range(HP):
                part(hp)

            def body(i):
                if not is_last(i):
                    fix(i + 1)
                g.vector_hot(v, i)
                if not is_last(i):
                    norm(i + 1)
                    v.wait_ge(kd_ready, 2 * (i + 1))
                for hp in range(HP):
                    if not is_last(i):
                        v.wait_ge(multiplied, HP * (i - 1) + (hp + 1))
                        part(hp)
                    if hp < g.per:
                        g.vector_add(v, i, hp)
            loop(v, body)

            v.wait_ge(multiplied, HP * TILES)
            for h2 in range(2):
                rows = slice(64 * h2, 64 * h2 + DV)
                rest = acc[rows, HP, 0:HP * (RES + 1)].rearrange("p (a f) -> p a f", f=RES + 1)
                nc.vector.tensor_copy(pairsT[rows], acc[rows, 0:HP, :]).then_inc(emptied, 1)
                nc.vector.tensor_copy(restT[rows, :, h2 * RES:(h2 + 1) * RES], rest[:, :, 0:RES]).then_inc(emptied, 1)
                nc.vector.tensor_copy(oneT[rows, :], rest[:, :, RES]).then_inc(emptied, 1)
            v.wait_ge(turned, 1)
            for h2 in range(2):
                src = slice(64 * h2, 64 * h2 + DV)
                dst = slice(DV * h2, DV * h2 + DV)
                for hp in range(HP):
                    for t in range(TPH):
                        nc.vector.tensor_scalar(keep.mom[:, (2 * hp + h2) * TPH + t, dst],
                                                acc[:, hp, t * P:(t + 1) * P][:, src],
                                                keep.factor[:, min(t, 1):min(t, 1) + 1], None, ALU.mult)
                nc.vector.tensor_scalar(keep.momw[:, :, dst], acc[:, HP, :].rearrange("p (a c) -> p a c", c=P)[:, :, src],
                                        keep.factor[:, 2:3], None, ALU.mult)
            nc.vector.tensor_scalar(keep.mom1[:].rearrange("o (h e) -> o h e", e=DV),
                                    proj[0:1, :].rearrange("o (h c) -> o h c", c=64)[:, :, 0:DV], SC ** 4 / N, None, ALU.mult)

        @block.tensor
        def _(pe):
            def project(t):
                pe.wait_ge(x_ready, t)
                after(pe, kv_ready, t - 1)
                for k in range(KC):
                    last = nc.tensor.matmul(proj[:], xT[:, k, :], keep.wT[:, k, C:3 * C], start=(k == 0), stop=(k == KC - 1))
                last.then_inc(projected, 1)

            def multiply(i, hp):
                first = isinstance(i, int) and i == 1
                m = LAST if is_last(i) else P
                pe.wait_ge(feats_ready, 3 * HP * (i - 1) + 3 * (hp + 1))
                pe.wait_ge(v_ready, HP * (i - 1) + (hp + 1))
                for h in (2 * hp, 2 * hp + 1):
                    p0 = 64 * (h % 2)
                    n = SHIFTS * D
                    last = nc.tensor.matmul(acc[p0:p0 + DV, hp, :], v1[0:m, h, :], kk[0:m, h * n:(h + 1) * n],
                                            start=first, stop=is_last(i), skip_group_check=True)
                    last = nc.tensor.matmul(acc[p0:p0 + DV, HP, hp * (RES + 1):(hp + 1) * (RES + 1)],
                                            v1[0:m, h, :], kr[0:m, h, :], start=(first and hp == 0),
                                            stop=is_last(i), skip_group_check=True)
                last.then_inc(multiplied, 1)

            pe.wait_ge(zeroed, 7)
            project(1)

            def body(i):
                for hp in range(HP):
                    multiply(i, hp)
                    if hp == 0 and not is_last(i):
                        project(i + 1)
                    if hp < g.per:
                        g.tensor_sum(pe, i, hp)
            loop(pe, body)
            pe.wait_ge(emptied, 6)
            for hp in range(HP):
                for t in range(TPH):
                    nc.tensor.transpose(acc[:, hp, t * P:(t + 1) * P], pairsT[:, hp, t * P:(t + 1) * P], keep.ident[:])
                nc.tensor.transpose(acc[:, HP, hp * P:(hp + 1) * P], restT[:, hp, :], keep.ident[:])
                last = nc.tensor.transpose(proj[0:1, hp * P:(hp + 1) * P], oneT[:, hp:hp + 1], keep.ident[:])
            last.then_inc(turned, 1)


FB = 4
FCH = FT // FB
RING = 3
assert FT % FB == 0 and TPH == FB


def readout(nc, keep, table, x, x1):
    with Scope(nc) as s:
        g = Gather(nc, s, keep, table, GPT_KEYS * TILES, GPT_QUERIES, "queries")
        xT = s.sb("q_xT", [P, KC, P])
        xs = s.sb("q_x", [P, C])
        q = s.sb("q_q", [P, C])
        sq = s.sb("q_sq", [P, C])
        ss, sd, inv, ry = (s.sb(f"q_{n}", [P, HEADS]) for n in ("ss", "sd", "inv", "ry"))
        qd = s.sb("q_qd", [P, HEADS, DW])
        qq = s.sb("q_qq", [P, PAIRS])
        qr = s.sb("q_qr", [P, HEADS, RES])
        fT = s.sb("q_fT", [P, RING, FB, P])
        o = s.sb("q_o", [P, C])
        oT = s.sb("q_oT", [P, KC, P])
        res = s.sb("q_res", [P, C])
        proj = s.ps("q_proj", [P, 512])
        turned = s.ps("q_turned", [P, 2, FB, P])
        y = s.ps("q_y", [P, 512])
        oTp = s.ps("q_oTp", [P, 512])
        out = s.ps("q_out", [P, 512])
        (x_ready, projected, q_ready, squared, ss_ready, sd_ready, qd_ready, feats_ready, rest_ready, turned_sem, copied,
         multiplied, ry_ready, o_ready, o_turned, oT_ready, out_ready, biased, res_ready, x_loaded, stored, steps) = (
            s.sem(n) for n in (
                "x_ready", "projected", "q_ready", "squared", "ss_ready", "sd_ready", "qd_ready", "feats_ready",
                "rest_ready", "turned", "copied", "multiplied", "ry_ready", "o_ready", "o_turned", "oT_ready",
                "out_ready", "biased", "res_ready", "x_loaded", "stored", "dve_steps"))
        block = s.block()

        def is_first(i):
            return isinstance(i, int) and i == 1

        @block.sync
        def _(sp):
            def body(i):
                after(sp, res_ready, i - 1)
                if is_last(i):
                    sp.dma_start(xs[0:LAST, :], x[(TILES - 1) * P:N, :]).then_inc(x_loaded, 16)
                    sp.wait_ge(res_ready, i)
                    sp.dma_start(x1[(TILES - 1) * P:NPAD, :], res[:]).then_inc(stored, 16)
                else:
                    sp.dma_start(xs[:], x[bass.ds((i - 1) * P, P), :]).then_inc(x_loaded, 16)
                    sp.wait_ge(res_ready, i)
                    sp.dma_start(x1[bass.ds((i - 1) * P, P), :], res[:]).then_inc(stored, 16)
            loop(sp, body)
            sp.wait_ge(stored, TILES * 16)

        @block.gpsimd
        def _(pool):
            loop(pool, lambda i: g.pool_fetch(pool, i))

        @block.scalar
        def _(act):
            def square(t):
                act.wait_ge(q_ready, t)
                nc.scalar.activation(sq[:], q[:], ACT.Square).then_inc(squared, 1)

            def root(t):
                act.wait_ge(ss_ready, t)
                nc.scalar.activation(sd[:], ss[:], ACT.Sqrt).then_inc(sd_ready, 1)

            def copy_output(i):
                act.wait_ge(o_turned, i)
                nc.scalar.copy(oT[:].rearrange("p k n -> p (k n)"), oTp[:, 0:C]).then_inc(oT_ready, 1)

            def copy(i, b):
                act.wait_ge(turned_sem, FCH * (i - 1) + (b + 1))
                after(act, multiplied, FCH * (i - 1) + (b + 1 - RING))
                nc.scalar.copy(fT[:, b % RING], turned[:, b % 2]).then_inc(copied, 1)

            def body(i):
                for b in range(FCH):
                    copy(i, b)
                    if b == 2 and not is_last(i):
                        square(i + 1)
                        root(i + 1)
                    if b == 3 and not is_first(i):
                        copy_output(i - 1)
            square(1)
            root(1)
            loop(act, body)
            copy_output(TILES)

        @block.vector
        def _(v):
            step = Chain(v, steps, 6)

            def fix(t):
                after(v, projected, t - 1)
                nc.vector.tensor_scalar(xT[:], keep.xnT[:, :, bass.ds((t - 1) * P, P)], 1.0, None,
                                        ALU.mult).then_inc(x_ready, 1)

            def norm(t):
                step.start(t - 1)
                v.wait_ge(projected, t)
                nc.vector.tensor_tensor(q[:], proj[:, 0:C], keep.bias_qkv[:, 0:C], ALU.add).then_inc(q_ready, 1)
                v.wait_ge(squared, t)
                step(nc.vector.tensor_reduce(ss[:], heads(sq[:], D), AX_X, ALU.add))
                nc.vector.tensor_scalar(ss[:], ss[:], SC * SC, ROOT_EPS * ROOT_EPS, ALU.mult, ALU.max).then_inc(ss_ready, 1)
                v.wait_ge(sd_ready, t)
                root_inverse(nc, step, inv, sd, ss)
                step(nc.vector.tensor_tensor(inv[:], inv[:], keep.temp[:], ALU.mult))
                scaled = inv[:].rearrange("p (h o) -> p h o", o=1)
                for a, n in ((0, D), (D, SHIFTS)):
                    nc.vector.tensor_tensor(qd[:, :, a:a + n], heads(q[:], D)[:, :, 0:n],
                                            scaled.broadcast_to([P, HEADS, n]), ALU.mult).then_inc(qd_ready, 1)
                step.end()

            def output(i):
                v.wait_ge(multiplied, FCH * i)
                yh = y[:, 0:HEADS * DV].rearrange("p (h e) -> p h e", e=DV)
                nc.vector.reciprocal(ry[:].rearrange("p (h o) -> p h o", o=1), yh[:, :, 0:1]).then_inc(ry_ready, 1)
                v.wait_ge(ry_ready, i)
                after(v, o_turned, i - 1)
                nc.vector.tensor_tensor(heads(o[:], D), yh[:, :, 1:DV],
                                        ry[:].rearrange("p (h o) -> p h o", o=1).broadcast_to([P, HEADS, D]),
                                        ALU.mult).then_inc(o_ready, 1)

            def add_up(i):
                v.wait_ge(x_loaded, i * 16)
                nc.vector.tensor_tensor(xs[:], xs[:], keep.bias_p[:], ALU.add).then_inc(biased, 1)
                v.wait_ge(biased, i)
                v.wait_ge(out_ready, i)
                after(v, stored, (i - 1) * 16)
                nc.vector.tensor_tensor(res[:], out[:, 0:C], xs[:], ALU.add).then_inc(res_ready, 1)

            fix(1)
            norm(1)
            v.wait_ge(qd_ready, 2)
            for hp in range(HP):
                pair_features(nc, qq, qd, hp, feats_ready)
            rest_features(nc, qr, qd, rest_ready)

            def body(i):
                if not is_last(i):
                    fix(i + 1)
                g.vector_hot(v, i, between=None if is_first(i) else lambda: output(i - 1))
                if not is_last(i):
                    norm(i + 1)
                    v.wait_ge(qd_ready, 2 * (i + 1))
                for hp in range(HP):
                    if not is_last(i):
                        v.wait_ge(turned_sem, FCH * (i - 1) + (2 * hp + 2))
                        pair_features(nc, qq, qd, hp, feats_ready)
                        if hp == HP - 1:
                            v.wait_ge(turned_sem, FCH * i)
                            rest_features(nc, qr, qd, rest_ready)
                    g.vector_add(v, i, hp)
                    if hp == 2 and not is_first(i):
                        add_up(i - 1)
                g.vector_add(v, i, HP)
            loop(v, body)
            output(TILES)
            add_up(TILES)

        @block.tensor
        def _(pe):
            def project(t):
                pe.wait_ge(x_ready, t)
                after(pe, q_ready, t - 1)
                for k in range(KC):
                    last = nc.tensor.matmul(proj[:, 0:C], xT[:, k, :], keep.wT[:, k, 0:C], start=(k == 0), stop=(k == KC - 1))
                last.then_inc(projected, 1)

            def turn(i, b):
                if b % 2 == 0 and b < FCH - 1:
                    pe.wait_ge(feats_ready, HP * (i - 1) + (b // 2 + 1))
                if b == FCH - 1:
                    pe.wait_ge(rest_ready, 2 * i)
                after(pe, copied, FCH * (i - 1) + max(b - 1, 0))
                for n in range(FB):
                    if b < FCH - 1:
                        a = qq[:, (b * FB + n) * P:(b * FB + n + 1) * P]
                    else:
                        a = qr[:, 2 * n:2 * n + 2, :].rearrange("p h f -> p (h f)")
                    last = nc.tensor.transpose(turned[:, b % 2, n, :], a, keep.ident[:])
                last.then_inc(turned_sem, 1)

            def multiply(i, b):
                pe.wait_ge(copied, FCH * (i - 1) + (b + 1))
                if b == 0:
                    after(pe, o_ready, i - 1)
                    nc.tensor.matmul(y[:, 0:HEADS * DV], keep.ones[0:1, :], keep.mom1[:], start=True, stop=False,
                                     skip_group_check=True)
                for n in range(FB):
                    hp = b // 2 if b < FCH - 1 else n
                    m = keep.mom[:, b * FB + n, :] if b < FCH - 1 else keep.momw[:, n, :]
                    last = nc.tensor.matmul(y[:, hp * DV2:(hp + 1) * DV2], fT[:, b % RING, n, :], m, start=False,
                                            stop=(b == FCH - 1), skip_group_check=True)
                last.then_inc(multiplied, 1)

            def turn_output(i):
                pe.wait_ge(o_ready, i)
                after(pe, oT_ready, i - 1)
                for k in range(KC):
                    last = nc.tensor.transpose(oTp[:, k * P:(k + 1) * P], o[:, k * P:(k + 1) * P], keep.ident[:])
                last.then_inc(o_turned, 1)

            def project_output(i):
                pe.wait_ge(oT_ready, i)
                after(pe, res_ready, i - 1)
                for k in range(KC):
                    last = nc.tensor.matmul(out[:, 0:C], oT[:, k, :], keep.wpT[:, k, :], start=(k == 0), stop=(k == KC - 1))
                last.then_inc(out_ready, 1)

            def body(i):
                turn(i, 0)
                turn(i, 1)
                if not is_last(i):
                    project(i + 1)
                turn(i, 2)
                multiply(i, 0)
                turn(i, 3)
                g.tensor_sum(pe, i, 0)
                if not is_first(i):
                    turn_output(i - 1)
                multiply(i, 1)
                turn(i, 4)
                g.tensor_sum(pe, i, 1)
                multiply(i, 2)
                turn(i, 5)
                multiply(i, 3)
                g.tensor_sum(pe, i, 2)
                turn(i, 6)
                multiply(i, 4)
                if not is_first(i):
                    project_output(i - 1)
                turn(i, 7)
                g.tensor_sum(pe, i, 3)
                multiply(i, 5)
                turn(i, 8)
                multiply(i, 6)
                g.tensor_sum(pe, i, 4)
                multiply(i, 7)
                multiply(i, 8)
            project(1)
            loop(pe, body)
            turn_output(TILES)
            project_output(TILES)


def weights(nc, keep, g, wqkv, bqkv, wproj, bproj, temperature):
    with Scope(nc) as s:
        rows = 3 * C // P
        w = s.sb("w_qkv", [P, rows, C])
        wp = s.sb("w_proj", [P, KC, C])
        turned = s.ps("w_turned", [P, KC, 2, 512])
        loaded, turned_sem, factors = s.sem("loaded"), s.sem("turned"), s.sem("factors")
        block = s.block()

        @block.sync
        def _(sp):
            sp.dma_start(w[:], wqkv.rearrange("(r p) c -> p r c", p=P)).then_inc(loaded, 16)
            sp.dma_start(wp[:], wproj.rearrange("(r p) c -> p r c", p=P)).then_inc(loaded, 16)
            sp.dma_start(keep.bias_qkv[:], bqkv.partition_broadcast(P)).then_inc(loaded, 16)
            sp.dma_start(keep.bias_p[:], bproj.partition_broadcast(P)).then_inc(loaded, 16)
            sp.dma_start(keep.temp[:], temperature.rearrange("a h b c -> (a h b c)").partition_broadcast(P)).then_inc(loaded, 16)

        @block.gpsimd
        def _(pool):
            g.pool_fetch(pool, 1)

        @block.tensor
        def _(pe):
            pe.wait_ge(loaded, 5 * 16)
            for k in range(KC):
                for r in range(rows):
                    nc.tensor.transpose(turned[:, k, r * P // 512, r * P % 512:r * P % 512 + P],
                                        w[:, r, k * P:(k + 1) * P], keep.ident[:])
                for r in range(KC):
                    last = nc.tensor.transpose(turned[:, k, 1, 256 + r * P:256 + (r + 1) * P],
                                               wp[:, r, k * P:(k + 1) * P], keep.ident[:])
            last.then_inc(turned_sem, 1)

        @block.vector
        def _(v):
            nc.vector.memset(keep.aggT[:], 0.0)
            v.wait_ge(loaded, 5 * 16)
            nc.vector.tensor_scalar(keep.temp[:], keep.temp[:], 2.0 * SC * SC, None, ALU.mult)
            nc.vector.memset(keep.factor[:], 1.0 / N).then_inc(factors, 1)
            v.wait_ge(factors, 1)
            nc.vector.memset(keep.factor[0:D, 0:1], 0.5 / N)
            for h in range(2):
                nc.vector.memset(keep.factor[h * RES:h * RES + D, 2:3], 0.5 / N)
                nc.vector.memset(keep.factor[h * RES + D:(h + 1) * RES, 2:3], SC ** 2 / N)
            v.wait_ge(turned_sem, 1)
            for k in range(KC):
                t = turned[:, k].rearrange("p b n -> p (b n)")
                nc.vector.tensor_copy(keep.wT[:, k, :], t[:, 0:3 * C])
                nc.vector.tensor_copy(keep.wpT[:, k, :], t[:, 3 * C:4 * C])


def far_edges(nc, keep, table):
    with Scope(nc) as s:
        g = Gather(nc, s, keep, table, 0, GPT, "far", counted=1)
        shifted, shift_seen = s.sem("shifted"), s.sem("shift_seen")
        block = s.block()
        steps = GROUPS // GPT

        def rounds(eng, body, before=None):
            far = eng.value_load(keep.far[0:1, 0:1], min_val=0, max_val=GROUPS)
            with eng.If(far > 0):
                with eng.Fori(1, WINDOWS) as k:
                    if before:
                        before(k)
                    with eng.Fori(0, steps) as n:
                        body((k - 1) * steps + n + 2, n + 1)

        @block.gpsimd
        def _(pool):
            pool.sem_inc(g.where_ready, GPT)
            rounds(pool, lambda i, at: g.pool_fetch(pool, i, at))

        @block.vector
        def _(v):
            for sem, n in ((g.equal_ready, 1), (g.hot_ready, 1), (g.added, GPT)):
                v.sem_inc(sem, n)

            def shift(k):
                v.wait_ge(g.added, (k - 1) * (steps * GPT) + GPT)
                nc.vector.tensor_scalar(keep.winT[:], keep.winT[:], -float(WIN), None, ALU.add).then_inc(shifted, 1)
                nc.vector.tensor_scalar(keep.base[:], keep.base[:], float(WIN), float(N), ALU.add,
                                        ALU.min).then_inc(shifted, 1)
                v.wait_ge(shifted, 2 * k)
                v.sem_inc(shift_seen, 1)

            def body(i, at):
                g.vector_hot(v, i, at)
                for j in range(GPT):
                    g.vector_add(v, i, j)
            rounds(v, body, shift)

        @block.tensor
        def _(pe):
            pe.sem_inc(g.summed, GPT)

            def body(i, at):
                for j in range(GPT):
                    g.tensor_sum(pe, i, j)
            rounds(pe, body)


SLOTS = (N + EXP * (P - 1)) // P
REGION = (TILES + 1) * P
DEEP, LEAD = 4, 2
assert SLOTS % DEEP == 0


def gate(nc, keep, x1, rows, Wd, W1, b1, Wg, bg, bd, order):
    with Scope(nc) as s:
        wg = s.sb("n_wg", [P, HC, EXP])
        b1r = s.sb("n_b1r", [HC, P])
        bgb = s.sb("n_bg", [P, EXP])
        h = s.sb("n_h", [P, 2, LB * P])
        agg = s.sb("n_agg", [P, KC, LB * P])
        both = s.sb("n_both", [P, LB, 2, C])
        xc = s.sb("n_xc", [P, LB, C])
        xnT = s.sb("n_xnT", [P, 2, KC, LB * P])
        blank = s.sb("n_blank", [P, (EXP + 1) * REGION // P, 2])
        total, var, sd, inv = (s.sb(f"n_{n}", [P, LB]) for n in ("total", "var", "sd", "inv"))
        tp = s.ps("n_tp", [P, LB * KC * P + 256])
        hp = s.ps("n_hp", [P, 2, 512])
        lg = s.ps("n_lg", [P, 512])
        b1p = s.ps("n_b1p", [P, 512])
        half = LB * P // 2
        (loaded, b1_turned, blank_ready, blanked, x1_loaded, agg_ready, agg_turned, x2_ready, xc_ready, squared,
         var_ready, sd_ready, xn_ready, xn_turned, xnT_ready, stored, h_summed, h_ready, gated, logit_ready,
         steps) = (s.sem(n) for n in (
             "loaded", "b1_turned", "blank_ready", "blanked", "x1_loaded", "agg_ready", "agg_turned", "x2_ready",
             "xc_ready", "squared", "var_ready", "sd_ready", "xn_ready", "xn_turned", "xnT_ready", "stored",
             "h_summed", "h_ready", "gated", "logit_ready", "dve_steps"))
        block = s.block()
        batches = TILES // LB
        rows_flat = rows.rearrange("n two c -> n (two c)")
        turned = tp[:, 0:LB * KC * P].rearrange("p (t k n) -> p t k n", t=LB, k=KC)

        def batch(i):
            return bass.ds((i - 1) * (LB * P), LB * P)

        def final(i):
            return isinstance(i, int) and i == batches

        @block.sync
        def _(sp):
            for dst, src in ((keep.w1[:], W1.rearrange("(k p) h -> p k h", p=P)),
                             (wg[:], Wg.rearrange("(c p) e -> p c e", p=P)),
                             (b1r[:], b1.rearrange("(c p) -> c p", p=P)), (bgb[:], bg.partition_broadcast(P))):
                sp.dma_start(dst, src).then_inc(loaded, 16)

            def body(i):
                after(sp, stored, 16 * (i - 1))
                sp.dma_start(both[:, :, 1, :], x1[batch(i), :].rearrange("(t p) c -> p t c", p=P)).then_inc(x1_loaded, 16)
                sp.wait_ge(xn_ready, i)
                sp.dma_start(rows_flat[batch(i), :].rearrange("(t p) c -> p t c", p=P),
                             both[:].rearrange("p t two c -> p t (two c)")).then_inc(stored, 16)
            loop(sp, body, last=batches)
            sp.wait_ge(stored, 16 * batches)

        @block.gpsimd
        def _(pool):
            nc.gpsimd.memset(blank[:], float(N)).then_inc(blank_ready, 1)
            pool.wait_ge(blank_ready, 1)
            pool.dma_start(order.rearrange("(p r) two -> p r two", p=P), blank[:]).then_inc(blanked, 16)
            for c in range(HC):
                pool.dma_start(keep.wd[:, c].rearrange("p (e o) -> p e o", o=C),
                               Wd[:, c * P:(c + 1) * P, :].rearrange("e p o -> p e o")).then_inc(keep.wd_loaded, 16)
            pool.dma_start(keep.bd[:], bd.rearrange("e c -> (e c)").partition_broadcast(P)).then_inc(keep.wd_loaded, 16)
            pool.wait_ge(blanked, 16)

        @block.scalar
        def _(act):
            def square(i):
                act.wait_ge(xc_ready, i)
                after(act, xn_turned, i - 1)
                nc.scalar.activation(both[:, :, 0, :], xc[:], ACT.Square).then_inc(squared, 1)

            def root(i):
                act.wait_ge(var_ready, i)
                nc.scalar.activation(sd[:], var[:], ACT.Sqrt).then_inc(sd_ready, 1)

            def body(i, k, j):
                for c in range(HC):
                    for q in range(2):
                        act.wait_ge(h_summed, 2 * HC * (i - 1) + (2 * c + q + 1))
                        if q == 0:
                            after(act, gated, HC * (i - 1) + (c - 1))
                        nc.scalar.activation(h[:, c % 2, q * half:(q + 1) * half], hp[:, q, 0:half], ACT.Gelu,
                                             bias=keep.b1T[:, c:c + 1]).then_inc(h_ready, 1)
                    if c == 2 and not final(i):
                        square(i + 1)
                    if c == 3 and not final(i):
                        root(i + 1)
            square(1)
            root(1)
            act.wait_ge(b1_turned, 1)
            nc.scalar.copy(keep.b1T[:], b1p[:, 0:HC]).then_inc(keep.b1_ready, 1)
            act.wait_ge(keep.b1_ready, 1)
            pairs(act, body, batches)

        @block.vector
        def _(v):
            step = Chain(v, steps, 7)

            def wide(a):
                return a[:].rearrange("p (t o) -> p t o", o=1).broadcast_to([P, LB, C])

            def norm(i, k):
                step.start(i - 1)
                after(v, agg_turned, i - 1)
                nc.vector.tensor_scalar(agg[:], keep.aggT[:, :, batch(i)], 0.0, None, ALU.max).then_inc(agg_ready, 1)
                v.wait_ge(agg_turned, i)
                v.wait_ge(x1_loaded, 16 * i)
                nc.vector.tensor_tensor(both[:, :, 1, :], both[:, :, 1, :], turned.rearrange("p t k n -> p t (k n)"),
                                        ALU.add).then_inc(x2_ready, 1)
                v.wait_ge(x2_ready, i)
                step(nc.vector.tensor_reduce(total[:], both[:, :, 1, :], AX_X, ALU.add))
                step(nc.vector.tensor_scalar(total[:], total[:], 1.0 / C, None, ALU.mult))
                nc.vector.tensor_tensor(xc[:], both[:, :, 1, :], wide(total), ALU.subtract).then_inc(xc_ready, 1)
                v.wait_ge(squared, i)
                step(nc.vector.tensor_reduce(var[:], both[:, :, 0, :], AX_X, ALU.add))
                nc.vector.tensor_scalar(var[:], var[:], 1.0 / C, LN_EPS, ALU.mult, ALU.add).then_inc(var_ready, 1)
                v.wait_ge(sd_ready, i)
                root_inverse(nc, step, inv, sd, var)
                nc.vector.scalar_tensor_tensor(out=both[:, :, 0, :], in0=xc[:], scalar=2.0, in1=wide(inv), op0=ALU.mult,
                                               op1=ALU.mult).then_inc(xn_ready, 1)
                step.end()
                v.wait_ge(xn_turned, i)
                after(v, h_summed, 2 * HC * (i - 2))
                for c in range(KC):
                    nc.vector.tensor_scalar(xnT[:, k, c, :].rearrange("p (t n) -> p t n", n=P), turned[:, :, c, :],
                                            1.0, None, ALU.mult).then_inc(xnT_ready, 1)

            def body(i, k, j):
                if not final(i):
                    norm(i + 1, 1 - k)
                v.wait_ge(gated, HC * i)
                nc.vector.tensor_tensor(keep.logit[:, bass.ds((i - 1) * LB, LB), :],
                                        lg[:, 0:LB * EXP].rearrange("p (t e) -> p t e", e=EXP),
                                        bgb[:].rearrange("p (o e) -> p o e", o=1).broadcast_to([P, LB, EXP]),
                                        ALU.add).then_inc(logit_ready, 1)
            norm(1, 0)
            v.wait_ge(loaded, 64)
            pairs(v, body, batches)

        @block.tensor
        def _(pe):
            def turn_agg(i):
                pe.wait_ge(agg_ready, i)
                after(pe, xnT_ready, KC * (i - 1))
                for t in range(LB):
                    for k in range(KC):
                        last = nc.tensor.transpose(turned[:, t, k, :], agg[:, k, t * P:(t + 1) * P], keep.ident[:])
                last.then_inc(agg_turned, 1)

            def turn_xn(i):
                pe.wait_ge(xn_ready, i)
                for t in range(LB):
                    for k in range(KC):
                        last = nc.tensor.transpose(turned[:, t, k, :], both[:, t, 0, k * P:(k + 1) * P], keep.ident[:])
                last.then_inc(xn_turned, 1)

            def logits(i, c):
                pe.wait_ge(h_ready, 2 * HC * (i - 1) + 2 * (c + 1))
                if c == 0:
                    after(pe, logit_ready, i - 1)
                for t in range(LB):
                    last = nc.tensor.matmul(lg[:, t * EXP:(t + 1) * EXP], h[:, c % 2, t * P:(t + 1) * P], wg[:, c, :],
                                            start=(c == 0 and t == 0), stop=(c == HC - 1), skip_group_check=True)
                last.then_inc(gated, 1)

            def body(i, k, j):
                pe.wait_ge(xnT_ready, KC * i)
                for c in range(HC):
                    for q in range(2):
                        after(pe, h_ready, 2 * HC * (i - 1) + (2 * (c - 1) + q + 1))
                        for kc in range(KC):
                            last = nc.tensor.matmul(hp[:, q, 0:half], keep.w1[:, kc, c * P:(c + 1) * P],
                                                    xnT[:, k, kc, q * half:(q + 1) * half],
                                                    start=(kc == 0), stop=(kc == KC - 1))
                        last.then_inc(h_summed, 1)
                    if c >= 1:
                        logits(i, c - 1)
                    if c == 0 and not final(i):
                        turn_agg(i + 1)
                    if c == 5 and not final(i):
                        turn_xn(i + 1)
                logits(i, HC - 1)
            turn_agg(1)
            pe.wait_ge(loaded, 64)
            nc.tensor.transpose(b1p[:, 0:HC], b1r[:], keep.ident[0:HC, 0:HC]).then_inc(b1_turned, 1)
            turn_xn(1)
            pairs(pe, body, batches)


def choose(nc, keep, order):
    with Scope(nc) as s:
        prob = s.sb("c_prob", [P, TILES, EXP])
        score = s.sb("c_score", [P, TILES, EXP])
        sel = s.sb("c_sel", [P, TILES, EXP])
        upto = s.sb("c_upto", [P, 2, TILES, EXP])
        a1, a2 = s.sb("c_a1", [P, TILES]), s.sb("c_a2", [P, TILES])
        first, start = s.sb("c_first", [P, EXP]), s.sb("c_start", [P, EXP])
        valid = s.sb("c_valid", [P, TILES])
        before = s.sb("c_before", [P, P])
        where = s.sb("c_where", [P, TILES], I32)
        slot = s.sb("c_slot", [P, 2, LB], I32)
        entry = s.sb("c_entry", [P, TILES, 2])
        held = s.sb("c_held", [P, 2, LB, 2])
        hundreds = s.sb("c_hundreds", [1, SLOTS])
        full = s.sb("c_full", [1, EXP, TILES])
        tiles, ends, gap = s.sb("c_tiles", [1, EXP]), s.sb("c_ends", [1, 2, EXP]), s.sb("c_gap", [1, EXP])
        past, pgap = s.sb("c_past", [1, SLOTS, EXP]), s.sb("c_pgap", [1, SLOTS, EXP])
        o1, o2 = s.sb("c_o1", [1, SLOTS]), s.sb("c_o2", [1, SLOTS])
        ranks = s.ps("c_ranks", [P, 512])
        counts = s.ps("c_counts", [P, 512])
        logit = keep.logit
        consts, exps, sel_ready, counted, placed, slot_ready, pool_go, steps, shifted = (s.sem(n) for n in (
            "consts", "exps", "sel_ready", "counted", "placed", "slot_ready", "pool_go", "dve_steps", "shifted"))
        scattered = s.sems("scattered", 2)
        block = s.block()
        batches = TILES // LB
        n_consts = 8

        @block.gpsimd
        def _(pool):
            nc.gpsimd.memset(valid[:], 1.0).then_inc(consts, 1)
            nc.gpsimd.memset(before[:], 1.0).then_inc(consts, 1)
            nc.gpsimd.iota(entry[:, :, 0], [[P, TILES]], base=0, channel_multiplier=1,
                           allow_small_or_imprecise_dtypes=True).then_inc(consts, 1)
            nc.gpsimd.iota(hundreds[:], [[P, SLOTS]], base=0, channel_multiplier=0,
                           allow_small_or_imprecise_dtypes=True).then_inc(consts, 1)
            nc.gpsimd.iota(first[:], [[-1, EXP]], base=EXP, channel_multiplier=0,
                           allow_small_or_imprecise_dtypes=True).then_inc(consts, 1)
            nc.gpsimd.iota(start[:], [[REGION, EXP]], base=0, channel_multiplier=0,
                           allow_small_or_imprecise_dtypes=True).then_inc(consts, 1)
            pool.wait_ge(consts, n_consts - 2)
            nc.gpsimd.affine_select(out=valid[:, TILES - 1:TILES], in_=valid[:, TILES - 1:TILES], compare_op=ALU.is_ge,
                                    fill=0.0, base=LAST - 1, pattern=[[0, 1]], channel_multiplier=-1).then_inc(consts, 1)
            nc.gpsimd.affine_select(out=before[:], in_=before[:], compare_op=ALU.is_ge, fill=0.0, base=-1,
                                    pattern=[[1, P]], channel_multiplier=-1).then_inc(consts, 1)
            pool.wait_ge(placed, 1)

            def scatter(i, k, use):
                after(pool, scattered[k], 16 * LB * (use - 1))
                pool.sem_inc(pool_go, 1)
                nc.gpsimd.tensor_copy(slot[:, k], where[:, bass.ds((i - 1) * LB, LB)]).then_inc(slot_ready, 1)
                nc.gpsimd.tensor_copy(held[:, k], entry[:, bass.ds((i - 1) * LB, LB), :]).then_inc(slot_ready, 1)
                pool.wait_ge(slot_ready, 2 * i)
                pool.sem_inc(pool_go, 1)
                for t in range(LB):
                    m = LAST if isinstance(i, int) and i == batches and t == LB - 1 else P
                    nc.gpsimd.indirect_dma_start(order, bass.IndirectOffsetOnAxis(ap=slot[0:m, k, t:t + 1], axis=0),
                                                 held[0:m, k, t, :], None).then_inc(scattered[k], 16)
            pairs(pool, scatter, batches)
            for k in range(2):
                pool.wait_ge(scattered[k], 16 * LB * (batches // 2 + 1 - k))

        @block.scalar
        def _(act):
            act.wait_ge(shifted, 1)
            nc.scalar.activation(prob[:], logit[:], ACT.Exp).then_inc(exps, 1)

        @block.vector
        def _(v):
            step = Chain(v, steps)
            shape = [P, TILES, EXP]

            def per_tile(a):
                return a[:].rearrange("p (t o) -> p t o", o=1).broadcast_to(shape)

            def per_expert(a):
                return a[:].rearrange("p (o e) -> p o e", o=1).broadcast_to(shape)
            v.wait_ge(consts, n_consts)
            step(nc.vector.tensor_reduce(a1[:], logit[:], AX_X, ALU.max))
            nc.vector.tensor_tensor(logit[:], logit[:], per_tile(a1), ALU.subtract).then_inc(shifted, 1)
            v.wait_ge(exps, 1)
            step(nc.vector.tensor_reduce(a1[:], prob[:], AX_X, ALU.add))
            step(nc.vector.reciprocal(a1[:], a1[:]))
            step(nc.vector.tensor_tensor(prob[:], prob[:], per_tile(a1), ALU.mult))
            step(nc.vector.tensor_reduce(a1[:], prob[:], AX_X, ALU.max))
            step.mark(nc.vector.tensor_copy(entry[:, :, 1], a1[:]))
            step(nc.vector.tensor_tensor(score[:], prob[:], per_tile(a1), ALU.is_ge))
            step(nc.vector.tensor_tensor(score[:], score[:], per_expert(first), ALU.mult))
            step(nc.vector.tensor_reduce(a2[:], score[:], AX_X, ALU.max))
            step(nc.vector.tensor_tensor(sel[:], score[:], per_tile(a2), ALU.is_equal))
            nc.vector.tensor_tensor(sel[:], sel[:], per_tile(valid), ALU.mult).then_inc(sel_ready, 1)
            v.wait_ge(counted, 2)
            v.wait_ge(sel_ready, 1)
            step(nc.vector.tensor_copy(upto[:, 0], counts[:, 0:TILES * EXP].rearrange("p (t e) -> p t e", e=EXP)))
            k, d = 0, 1
            while d < TILES:
                step.mark(nc.vector.tensor_copy(upto[:, 1 - k, 0:d], upto[:, k, 0:d]))
                step(nc.vector.tensor_tensor(upto[:, 1 - k, d:], upto[:, k, d:], upto[:, k, 0:TILES - d], ALU.add))
                k, d = 1 - k, 2 * d
            step(nc.vector.tensor_tensor(score[:], upto[:, k], ranks[:, 0:TILES * EXP].rearrange("p (t e) -> p t e", e=EXP), ALU.add))
            step(nc.vector.tensor_tensor(score[:], score[:], counts[:, 0:TILES * EXP].rearrange("p (t e) -> p t e", e=EXP), ALU.subtract))
            step(nc.vector.tensor_tensor(score[:], score[:], per_expert(start), ALU.add))
            step(nc.vector.tensor_tensor(score[:], score[:], sel[:], ALU.mult))
            step(nc.vector.tensor_reduce(a2[:], score[:], AX_X, ALU.add))
            nc.vector.tensor_copy(where[:], a2[:]).then_inc(placed, 1)
            total = upto[0:1, k, TILES - 1, :]
            step(nc.vector.tensor_tensor(full[:], total.rearrange("o (e u) -> o e u", u=1).broadcast_to([1, EXP, TILES]),
                                         hundreds[:, 0:TILES].rearrange("o (u t) -> o u t", u=1).broadcast_to([1, EXP, TILES]),
                                         ALU.is_gt))
            step(nc.vector.tensor_reduce(tiles[:], full[:], AX_X, ALU.add))
            step.mark(nc.vector.tensor_scalar(gap[:], tiles[:], -float(P), float(REGION), ALU.mult, ALU.add))
            step(nc.vector.tensor_scalar(ends[:, 0], tiles[:], float(P), None, ALU.mult))
            k, d = 0, 1
            while d < EXP:
                step.mark(nc.vector.tensor_copy(ends[:, 1 - k, 0:d], ends[:, k, 0:d]))
                step(nc.vector.tensor_tensor(ends[:, 1 - k, d:], ends[:, k, d:], ends[:, k, 0:EXP - d], ALU.add))
                k, d = 1 - k, 2 * d
            shape1 = [1, SLOTS, EXP]
            step(nc.vector.tensor_tensor(past[:], hundreds[:].rearrange("o (t u) -> o t u", u=1).broadcast_to(shape1),
                                         ends[:, k].rearrange("o (u e) -> o u e", u=1).broadcast_to(shape1), ALU.is_ge))
            step.mark(nc.vector.tensor_tensor(pgap[:], past[:], gap[:].rearrange("o (u e) -> o u e", u=1).broadcast_to(shape1), ALU.mult))
            step(nc.vector.tensor_reduce(o1[:], past[:], AX_X, ALU.add))
            step.mark(nc.vector.tensor_scalar(keep.which[:], o1[:], float(EXP - 1), None, ALU.min))
            step(nc.vector.tensor_reduce(o2[:], pgap[:], AX_X, ALU.add))
            step(nc.vector.tensor_tensor(o2[:], o2[:], hundreds[:], ALU.add))
            nc.vector.tensor_scalar(keep.offs[:], o2[:], float(EXP * REGION), None, ALU.min)

        @block.tensor
        def _(pe):
            pe.wait_ge(sel_ready, 1)
            pe.wait_ge(consts, n_consts)
            flat = sel[:].rearrange("p t e -> p (t e)")
            nc.tensor.matmul(ranks[:, 0:TILES * EXP], before[:], flat, start=True, stop=True).then_inc(counted, 1)
            nc.tensor.matmul(counts[:, 0:TILES * EXP], keep.ones[:], flat, start=True, stop=True).then_inc(counted, 1)


def experts(nc, keep, rows, order, out):
    with Scope(nc) as s:
        om = s.sb("f_om", [P, DEEP, 2])
        node = s.sb("f_node", [P, DEEP, 1], I32)
        xs = s.sb("f_xs", [P, DEEP, 2 * C])
        xT = s.sb("f_xT", [P, KC, P])
        h = s.sb("f_h", [P, HC, P])
        z = s.sb("f_z", [P, C])
        res = s.sb("f_res", [P, DEEP, C])
        turned = s.ps("f_turned", [P, 512])
        hp = s.ps("f_hp", [P, 2, 4, P])
        y = s.ps("f_y", [P, 2, 512])
        listed, gathered, stored = (s.sems(n, DEEP) for n in ("listed", "gathered", "stored"))
        node_ready, pool_go, turned_sem, xT_ready, h_summed, h_ready, y_ready, z_ready, res_ready = (s.sem(n) for n in (
            "node_ready", "pool_go", "turned", "xT_ready", "h_summed", "h_ready", "y_ready", "z_ready", "res_ready"))
        block = s.block()
        per = 4
        rows_flat = rows.rearrange("n two c -> n (two c)")

        def slots(eng, body):
            for k in range(DEEP):
                body(k + 1, k, 1)
            with eng.Fori(1, SLOTS // DEEP - 1) as i:
                for k in range(DEEP):
                    body(DEEP * i + (k + 1), k, i + 1)
            for k in range(DEEP):
                body(SLOTS - DEEP + (k + 1), k, SLOTS // DEEP)

        def ahead(t, k, i, n):
            return t + n, (k + n) % DEEP, i + (k + n) // DEEP

        @block.sync
        def _(sp):
            def body(t, k, i):
                after(sp, res_ready, t - DEEP)
                off = sp.value_load(keep.offs[0:1, bass.ds(t - 1, 1)], min_val=0, max_val=EXP * REGION)
                sp.dma_start(om[:, k, :], order[bass.ds(off, P), :]).then_inc(listed[k], 16)
            slots(sp, body)

        @block.gpsimd
        def _(pool):
            def fetch(t, k, i):
                pool.wait_ge(listed[k], 16 * i)
                after(pool, stored[k], 16 * (i - 1))
                pool.sem_inc(pool_go, 1)
                nc.gpsimd.tensor_copy(node[:, k, :], om[:, k, 0:1]).then_inc(node_ready, 1)
                pool.wait_ge(node_ready, t)
                pool.sem_inc(pool_go, 1)
                nc.gpsimd.indirect_dma_start(xs[:, k, :], None, rows_flat,
                                             bass.IndirectOffsetOnAxis(ap=node[:, k, :], axis=0)).then_inc(gathered[k], 16)

            def body(t, k, i):
                if not (isinstance(t, int) and t > SLOTS - LEAD):
                    fetch(*ahead(t, k, i, LEAD))
                pool.wait_ge(res_ready, t)
                pool.sem_inc(pool_go, 1)
                nc.gpsimd.indirect_dma_start(out, bass.IndirectOffsetOnAxis(ap=node[:, k, :], axis=0), res[:, k, :], None,
                                             bounds_check=N - 1, oob_is_err=False).then_inc(stored[k], 16)
            for k in range(LEAD):
                fetch(k + 1, k, 1)
            slots(pool, body)
            for k in range(DEEP):
                pool.wait_ge(stored[k], 16 * (SLOTS // DEEP))

        @block.scalar
        def _(act):
            def body(t, k, i):
                for b in range(2):
                    act.wait_ge(h_summed, 2 * (t - 1) + (b + 1))
                    if b == 0:
                        after(act, y_ready, t - 1)
                    for c in range(per):
                        n = b * per + c
                        nc.scalar.activation(h[:, n, :], hp[:, b, c, :], ACT.Gelu,
                                             bias=keep.b1T[:, n:n + 1]).then_inc(h_ready, 1)
            act.wait_ge(keep.b1_ready, 1)
            slots(act, body)

        @block.vector
        def _(v):
            def copy(t, k, i):
                v.wait_ge(turned_sem, t)
                after(v, h_summed, 2 * (t - 1))
                nc.vector.tensor_copy(xT[:].rearrange("p k n -> p (k n)"), turned[:, 0:C]).then_inc(xT_ready, 1)

            def body(t, k, i):
                if not (isinstance(t, int) and t == SLOTS):
                    copy(*ahead(t, k, i, 1))
                e = v.value_load(keep.which[0:1, bass.ds(t - 1, 1)], min_val=0, max_val=EXP - 1)
                v.wait_ge(y_ready, t)
                after(v, res_ready, t - 1)
                nc.vector.tensor_tensor(z[:], y[:, k % 2, 0:C], keep.bd[:, bass.ds(e * C, C)], ALU.add).then_inc(z_ready, 1)
                v.wait_ge(z_ready, t)
                after(v, stored[k], 16 * (i - 1))
                v.wait_ge(gathered[k], 16 * i)
                nc.vector.scalar_tensor_tensor(out=res[:, k, :], in0=z[:], scalar=om[:, k, 1:2], in1=xs[:, k, C:2 * C],
                                               op0=ALU.mult, op1=ALU.add).then_inc(res_ready, 1)
            v.wait_ge(keep.wd_loaded, 16 * (HC + 1))
            copy(1, 0, 1)
            slots(v, body)

        @block.tensor
        def _(pe):
            def turn(t, k, i):
                pe.wait_ge(gathered[k], 16 * i)
                after(pe, xT_ready, t - 1)
                for c in range(KC):
                    last = nc.tensor.transpose(turned[:, c * P:(c + 1) * P], xs[:, k, c * P:(c + 1) * P], keep.ident[:])
                last.then_inc(turned_sem, 1)

            def body(t, k, i):
                e = pe.value_load(keep.which[0:1, bass.ds(t - 1, 1)], min_val=0, max_val=EXP - 1)
                pe.wait_ge(xT_ready, t)
                for b in range(2):
                    after(pe, h_ready, HC * (t - 1) - (per if b == 0 else 0))
                    for c in range(per):
                        n = b * per + c
                        for kc in range(KC):
                            last = nc.tensor.matmul(hp[:, b, c, :], keep.w1[:, kc, n * P:(n + 1) * P], xT[:, kc, :],
                                                    start=(kc == 0), stop=(kc == KC - 1))
                    last.then_inc(h_summed, 1)
                if not (isinstance(t, int) and t == SLOTS):
                    turn(*ahead(t, k, i, 1))
                after(pe, z_ready, t - 2)
                for c in range(HC):
                    pe.wait_ge(h_ready, HC * (t - 1) + (c + 1))
                    last = nc.tensor.matmul(y[:, k % 2, 0:C], h[:, c, :], keep.wd[:, c, bass.ds(e * C, C)],
                                            start=(c == 0), stop=(c == HC - 1))
                last.then_inc(y_ready, 1)
            pe.wait_ge(keep.wd_loaded, 16 * (HC + 1))
            turn(1, 0, 1)
            slots(pe, body)


class Keep:
    pass


def build(nc, x, src, dst, edge_type_20, edge_weight1, L0_gnn_weight, L0_mix_Wqkv, L0_mix_bqkv, L0_mix_Wproj,
          L0_mix_bproj, L0_mix_temperature, L0_ffn_W1, L0_ffn_b1, L0_ffn_Wg, L0_ffn_bg, L0_ffn_Wd, L0_ffn_bd, out):
    table = nc.dram_tensor("table", (NPAD * RELS, C), F32, kind="Internal").ap()
    x1 = nc.dram_tensor("x1", (NPAD, C), F32, kind="Internal").ap()
    rows = nc.dram_tensor("rows", (NPAD, 2, C), F32, kind="Internal").ap()
    order = nc.dram_tensor("order", ((EXP + 1) * REGION, 2), F32, kind="Internal").ap()
    keep = Keep()
    with Scope(nc) as s:
        keep.ident = s.sb("k_ident", [P, P])
        keep.offsets = s.sb("k_offsets", [P, WIN])
        keep.ones = s.sb("k_ones", [P, P])
        keep.idxT = s.sb("k_idxT", [P, COLS], I32)
        keep.winT = s.sb("k_winT", [P, COLS])
        keep.nrmT = s.sb("k_nrmT", [P, COLS])
        keep.base = s.sb("k_base", [1, GROUPS], I32)
        keep.far = s.sb("k_far", [1, 1], I32)
        keep.which = s.sb("k_which", [1, SLOTS], I32)
        keep.offs = s.sb("k_offs", [1, SLOTS], I32)
        keep.w_loaded, keep.wd_loaded, keep.b1_ready = s.sem("w_loaded"), s.sem("wd_loaded"), s.sem("b1_ready")
        keep.aggT = s.sb("k_aggT", [P, KC, AGG])
        with Scope(nc) as t:
            keep.xnT = t.sb("k_xnT", [P, KC, NPAD])
            keep.weight = keep.aggT[:].rearrange("p k n -> p (k n)")[:, 0:KC * RELS * C]\
                .rearrange("p (k r c) -> p k r c", k=KC, c=C)
            edges(nc, keep, src, dst, edge_type_20, edge_weight1.rearrange("e o -> (e o)"), L0_gnn_weight)
            relations(nc, keep, x, table)
            keep.wT = t.sb("k_wT", [P, KC, 3 * C])
            keep.wpT = t.sb("k_wpT", [P, KC, C])
            keep.bias_qkv = t.sb("k_bias_qkv", [P, 3 * C])
            keep.bias_p = t.sb("k_bias_p", [P, C])
            keep.temp = t.sb("k_temp", [P, HEADS])
            keep.factor = t.sb("k_factor", [P, 3])
            keep.mom = t.sb("k_mom", [P, PT, DV2])
            keep.momw = t.sb("k_momw", [P, HP, DV2])
            keep.mom1 = t.sb("k_mom1", [1, HEADS * DV])
            with Scope(nc) as u:
                g = Gather(nc, u, keep, table, 0, GPT_KEYS, "keys")
                weights(nc, keep, g, L0_mix_Wqkv, L0_mix_bqkv, L0_mix_Wproj, L0_mix_bproj, L0_mix_temperature)
                moments(nc, keep, g)
            readout(nc, keep, table, x, x1)
            far_edges(nc, keep, table)
        keep.w1 = s.sb("k_w1", [P, KC, HID])
        keep.b1T = s.sb("k_b1T", [P, HC])
        keep.wd = s.sb("k_wd", [P, HC, EXP * C])
        keep.bd = s.sb("k_bd", [P, EXP * C])
        keep.logit = s.sb("k_logit", [P, TILES, EXP])
        gate(nc, keep, x1, rows, L0_ffn_Wd, L0_ffn_W1, L0_ffn_b1, L0_ffn_Wg, L0_ffn_bg, L0_ffn_bd, order)
        choose(nc, keep, order)
        experts(nc, keep, rows, order, out)


_INS = ['x', 'src', 'dst', 'edge_type_20', 'edge_weight1', 'L0_gnn_weight', 'L0_mix_Wqkv', 'L0_mix_bqkv',
        'L0_mix_Wproj', 'L0_mix_bproj', 'L0_mix_temperature', 'L0_ffn_W1', 'L0_ffn_b1', 'L0_ffn_Wg', 'L0_ffn_bg',
        'L0_ffn_Wd', 'L0_ffn_bd']
_OUTS = [((N, C), 'float32')]


def kernel(**inputs):
    import numpy as _np
    import concourse.bacc as _bacc
    from concourse import mybir as _mybir
    from concourse.bass_utils import run_bass_kernel_spmd as _run

    nc = _bacc.Bacc("TRN2", target_bir_lowering=False, num_devices=1)
    arrays, args = {}, []
    for name in _INS:
        a = _np.ascontiguousarray(inputs[name])
        arrays[f"in_{name}_dram"] = a
        args.append(nc.dram_tensor(f"in_{name}_dram", a.shape, _mybir.dt.from_np(a.dtype), kind="ExternalInput").ap())
    for i, (shape, dtype) in enumerate(_OUTS):
        dt = _mybir.dt.from_np(_np.dtype(dtype))
        args.append(nc.dram_tensor(f"out_{i}_dram", shape, dt, kind="ExternalOutput").ap())
    build(nc, *args)
    r = _run(nc, [arrays], core_ids=[0])
    got = tuple(r.results[0][f"out_{i}_dram"] for i in range(len(_OUTS)))
    return got[0]
```
